# Optimizing a Trainium2 kernel written in Bass

```python
import numpy as np
import jax
import jax.numpy as jnp

def _softmax(x, axis=-1):
    return jax.nn.softmax(x, axis=axis)

def _gelu(x):
    return jax.nn.gelu(x, approximate=True)

def _silu(x):
    return jax.nn.silu(x)

def _sigmoid(x):
    return jax.nn.sigmoid(x)

def _layernorm(x, axis=-1, eps=1e-05):
    m = jnp.mean(x, axis=axis, keepdims=True)
    v = jnp.var(x, axis=axis, keepdims=True)
    return (x - m) / jnp.sqrt(v + eps)

def _scatter_add(tgt, idx, src, axis=0):
    return tgt.at[idx].add(src)

def _segment_sum(src, seg, n):
    return jax.ops.segment_sum(src, seg, n)
kernel_name = 'mk_adaln_d1_jaxref_r4_f4c4b8'

def setup_inputs(seed: int=0):
    np.random.seed(seed)
    _w = jnp.asarray

    def _L0_attn_setup():
        import jax, jax.numpy as jnp
        import numpy as np
        B, N, D_IN, D_OUT, H = (2, 512, 256, 256, 16)
        HEAD_DIM = D_OUT // H
        key = jax.random.key(seed)
        ks = jax.random.split(key, 8)
        s = 0.02
        return {'x': jax.random.normal(ks[0], (B, N, D_IN), dtype=jnp.float32), 'Wq': jax.random.normal(ks[1], (D_IN, D_OUT), dtype=jnp.float32) * s, 'Wk': jax.random.normal(ks[2], (D_IN, D_OUT), dtype=jnp.float32) * s, 'Wv': jax.random.normal(ks[3], (D_IN, D_OUT), dtype=jnp.float32) * s, 'Wo': jax.random.normal(ks[4], (D_OUT, D_OUT), dtype=jnp.float32) * s, 'bo': jnp.zeros((D_OUT,), dtype=jnp.float32), 'w': jax.random.uniform(ks[5], (H,), dtype=jnp.float32), 'v': jax.random.uniform(ks[6], (H,), dtype=jnp.float32)}
    _L0_attn_in = _L0_attn_setup()

    def _L0_ffn_setup():
        import jax, jax.numpy as jnp
        import numpy as np
        B, S, D = (4, 1024, 256)
        DD = 4 * D
        N_EXPERTS = 8
        CAPACITY = 1.0
        LN_EPS = 1e-05
        key = jax.random.key(seed)
        ks = jax.random.split(key, 8)
        s1 = 1.0 / np.sqrt(D)
        s2 = 1.0 / np.sqrt(DD)
        return {'x': jax.random.normal(ks[0], (B, S, D), jnp.float32), 'gate_w': jax.random.normal(ks[1], (N_EXPERTS, D), jnp.float32) * 0.02, 'ln_w': jnp.ones((D,), jnp.float32), 'ln_b': jnp.zeros((D,), jnp.float32), 'fc1s': jax.random.normal(ks[2], (N_EXPERTS, DD, D), jnp.float32) * s1, 'b1s': jax.random.normal(ks[3], (N_EXPERTS, DD), jnp.float32) * s1, 'fc2s': jax.random.normal(ks[4], (N_EXPERTS, D, DD), jnp.float32) * s2, 'b2s': jax.random.normal(ks[5], (N_EXPERTS, D), jnp.float32) * s2}
    _L0_ffn_in = _L0_ffn_setup()
    _L0_c = _w((lambda *s: np.random.randn(*s).astype(np.float32) * 0.05)(2, 256))
    _L0_wmod = _w((lambda *s: np.random.randn(*s).astype(np.float32) * 0.05)(256, 6 * 256) * 256 ** (-0.5))
    _d = {'L0_attn_x': _L0_attn_in['x'], 'L0_attn_Wq': _L0_attn_in['Wq'], 'L0_attn_Wk': _L0_attn_in['Wk'], 'L0_attn_Wv': _L0_attn_in['Wv'], 'L0_attn_Wo': _L0_attn_in['Wo'], 'L0_attn_bo': _L0_attn_in['bo'], 'L0_attn_w': _L0_attn_in['w'], 'L0_attn_v': _L0_attn_in['v'], 'L0_ffn_gate_w': _L0_ffn_in['gate_w'], 'L0_ffn_ln_w': _L0_ffn_in['ln_w'], 'L0_ffn_ln_b': _L0_ffn_in['ln_b'], 'L0_ffn_fc1s': _L0_ffn_in['fc1s'], 'L0_ffn_b1s': _L0_ffn_in['b1s'], 'L0_ffn_fc2s': _L0_ffn_in['fc2s'], 'L0_ffn_b2s': _L0_ffn_in['b2s'], 'L0_c': _L0_c, 'L0_wmod': _L0_wmod}
    _x0 = _d['L0_attn_x']
    _d['L0_attn_x'] = jax.random.normal(jax.random.fold_in(jax.random.key(seed), 1), (2, 2048, 256), dtype=_x0.dtype)
    del _x0
    return _d

def reference(L0_attn_x, L0_attn_Wq, L0_attn_Wk, L0_attn_Wv, L0_attn_Wo, L0_attn_bo, L0_attn_w, L0_attn_v, L0_ffn_gate_w, L0_ffn_ln_w, L0_ffn_ln_b, L0_ffn_fc1s, L0_ffn_b1s, L0_ffn_fc2s, L0_ffn_b2s, L0_c, L0_wmod):

    def _L0_attn_ref(x, Wq, Wk, Wv, Wo, bo, w, v):
        import jax, jax.numpy as jnp
        import numpy as np
        B, N, D_IN, D_OUT, H = (2, 512, 256, 256, 16)
        HEAD_DIM = D_OUT // H
        b, n, _ = x.shape
        h = w.shape[0]
        hd = Wq.shape[1] // h

        def proj(W):
            return (x @ W).reshape(b, n, h, hd).transpose(0, 2, 1, 3)
        q, k, val = (proj(Wq), proj(Wk), proj(Wv))
        pos = jnp.arange(n)
        R = jnp.abs(pos[:, None] - pos[None, :]).astype(x.dtype)
        wv = w[:, None, None]
        vv = v[:, None, None]
        R_hat = (1.0 + jnp.exp(vv)) / (1.0 + jnp.exp(vv - wv * R))
        scores = jax.nn.relu(jnp.einsum('bhqd,bhkd->bhqk', q, k)) * R_hat[None]
        causal = jnp.triu(jnp.ones((n, n), dtype=bool), k=1)
        scores = jnp.where(causal[None, None], -jnp.inf, scores)
        attn = jax.nn.softmax(scores / np.sqrt(hd).astype(x.dtype), axis=-1)
        ctx = jnp.einsum('bhqk,bhkd->bhqd', attn, val)
        ctx = ctx.transpose(0, 2, 1, 3).reshape(b, n, h * hd)
        return ctx @ Wo + bo

    def _L0_ffn_ref(x, gate_w, ln_w, ln_b, fc1s, b1s, fc2s, b2s):
        import jax, jax.numpy as jnp
        import numpy as np
        B, S, D = (4, 1024, 256)
        DD = 4 * D
        N_EXPERTS = 8
        CAPACITY = 1.0
        LN_EPS = 1e-05
        og_shape = x.shape
        d = og_shape[-1]
        xf = x.reshape(-1, d)
        bs = xf.shape[0]
        n = gate_w.shape[0]
        k = int(bs * CAPACITY) // n
        scores = jax.nn.softmax(xf @ gate_w.T, axis=-1)
        vals, idx = jax.lax.top_k(scores.T, k)
        kept_w = vals.T
        kept_idx = idx.T
        flat_idx = kept_idx.reshape(-1)
        y = xf[flat_idx].reshape(k, n, d)
        mu = y.mean(-1, keepdims=True)
        var = ((y - mu) ** 2).mean(-1, keepdims=True)
        y = (y - mu) * jax.lax.rsqrt(var + LN_EPS) * ln_w + ln_b
        h = jnp.einsum('knd,nfd->knf', y, fc1s) + b1s
        h = jax.nn.gelu(h, approximate=True)
        out = jnp.einsum('knf,ndf->knd', h, fc2s) + b2s
        out = out * kept_w[..., None]
        xf = xf.at[flat_idx].add(out.reshape(k * n, d))
        return xf.reshape(og_shape)
    x = L0_attn_x
    mod = (_silu(L0_c) @ L0_wmod).reshape(L0_c.shape[0], 6, 1, -1)
    sa, ca, ga, sb, cb, gb = (mod[:, 0], mod[:, 1], mod[:, 2], mod[:, 3], mod[:, 4], mod[:, 5])
    ga = (2 * (ga >= 0) - 1) * jnp.maximum(jnp.abs(ga), 0.25)
    gb = (2 * (gb >= 0) - 1) * jnp.maximum(jnp.abs(gb), 0.25)
    h = _layernorm(x, axis=-1) * (1 + ca) + sa
    x = x + ga * _L0_attn_ref(h, L0_attn_Wq, L0_attn_Wk, L0_attn_Wv, L0_attn_Wo, L0_attn_bo, L0_attn_w, L0_attn_v)
    h = _layernorm(x, axis=-1) * (1 + cb) + sb
    x = x + gb * _L0_ffn_ref(h, L0_ffn_gate_w, L0_ffn_ln_w, L0_ffn_ln_b, L0_ffn_fc1s, L0_ffn_b1s, L0_ffn_fc2s, L0_ffn_b2s)
    return x

_drawn_inputs = setup_inputs


def setup_inputs(seed=0):
    import zlib

    import numpy as np

    out = dict(_drawn_inputs(seed))
    spreads = {'L0_attn_bo': (0.0, 0.322), 'L0_ffn_ln_w': (1.0, 0.6), 'L0_ffn_ln_b': (0.0, 2.0)}
    factors = {'L0_attn_Wq': 8.0,
     'L0_attn_Wk': 8.0,
     'L0_attn_Wv': 8.0,
     'L0_attn_Wo': 8.0,
     'L0_attn_w': 8.0,
     'L0_attn_v': 8.0,
     'L0_ffn_b1s': 49.429,
     'L0_ffn_b2s': 64.0}
    for name, (base, spread) in spreads.items():
        noise = np.random.default_rng([zlib.crc32(name.encode()), seed]).standard_normal(out[name].shape)
        drawn = base * np.exp(spread * noise) if base else spread * noise
        out[name] = jnp.asarray(drawn.astype(out[name].dtype))
    for name, factor in factors.items():
        out[name] = (out[name] * factor).astype(out[name].dtype)
    return out
```

```python
from contextlib import ExitStack

import concourse.bass as bass
from concourse import mybir

F32 = mybir.dt.float32
BF16 = mybir.dt.bfloat16
I32 = mybir.dt.int32
U32 = mybir.dt.uint32
ALU = mybir.AluOpType
ACT = mybir.ActivationFunctionType
AX = mybir.AxisListType

P = 128
B, N, D = 2, 2048, 256
H = 16
HD = D // H
TOK = B * N
NT = TOK // P
BT = N // P
KC = D // P
E = 8
F = 4 * D
FC = F // P
CAP = TOK // E
EC = CAP // P
EPS = 1e-5
NW = D + E
LN_GROUP = 4
NG = NT // LN_GROUP
GW = LN_GROUP * P
RW = N + P
MASKED = -1e30

C_ID, C_DIAG, C_FULL, C_SAME, C_BELOW, C_IOTA, C_TILE, C_ROW = (128 * i for i in range(8))
C_ROW = C_TILE + NT * E
C_W = C_ROW + NT * E


def adaln_block(nc, x, c_t, wmod, wq, wk, wv, wo, bo, dist_w, dist_v, gate_t, ln_w, ln_b,
                fc1_t, b1, fc2_t, b2, consts, out):
    ctx = ExitStack()
    with ctx:
        def sb(name, shape, dt=F32):
            return ctx.enter_context(nc.sbuf_tensor(name, shape, dt))

        def ps(name, shape, dt=F32):
            return ctx.enter_context(nc.psum_tensor(name, shape, dt))

        def dram(name, shape, dt):
            return nc.dram_tensor(name, shape, dt, kind="Internal").ap()

        q_split = dram("q_split", (3, D, TOK), BF16)
        k_split = dram("k_split", (3, D, TOK), BF16)
        factor_rows = dram("factor_rows", (H, RW), F32)
        normed = dram("normed", (TOK, NW), F32)

        region_x = sb("region_x", [P, NT * D])
        region_a = sb("region_a", [P, 8192])
        region_v = sb("region_v", [P, NT * D])
        region_c = sb("region_c", [P, NT * D])
        region_s = sb("region_s", [P, 4096])
        region_t = sb("region_t", [P, 4096])
        region_o = sb("region_o", [P, 4096])
        region_p = sb("region_p", [P, 2048])
        xs = region_x[:, :].rearrange("p (t d) -> p t d", d=D)
        vals = region_v[:, :].rearrange("p (t d) -> p t d", d=D)
        context = region_c[:, :].rearrange("p (t d) -> p t d", d=D)

        ident = sb("ident", [P, P])
        bconst = sb("bconst", [P, C_W], BF16)
        ident_b = bconst[:, C_ID:C_ID + P]
        mask_diag = bconst[:, C_DIAG:C_DIAG + P]
        mask_full = bconst[:, C_FULL:C_FULL + P]
        same_expert = bconst[:, C_SAME:C_SAME + P]
        rows_before = bconst[:, C_BELOW:C_BELOW + P]
        iota_row = bconst[:, C_IOTA:C_IOTA + P]
        tile_of = bconst[:, C_TILE:C_TILE + NT * E]
        row_of = bconst[:, C_ROW:C_ROW + NT * E]
        wo_gated = sb("wo_gated", [P, B, KC, D])
        bo_gated = sb("bo_gated", [P, B, D])
        gates = sb("gates", [P, B, 3, D])
        modt = sb("modt", [P, 12, B])
        gate_sb = sb("gate_sb", [P, KC, E])
        lnw_sb = sb("lnw_sb", [P, KC])
        lnb_sb = sb("lnb_sb", [P, KC])
        b1_sb = sb("b1_sb", [P, E, FC])
        moments = sb("moments", [P, NT, 2])
        rstd = sb("rstd", [P, NT])

        with ExitStack() as st, nc.Block() as block:
            sem = lambda name: st.enter_context(nc.semaphore(name))
            ld_x = [sem(f"ld_x{i}") for i in range(4)]
            ld_mod, ld_rest, ld_w, ld_dist = sem("ld_mod"), sem("ld_rest"), sem("ld_w"), sem("ld_dist")
            silu_exp, silu_done, modt_mm, modt_done = sem("silu_exp"), sem("silu_done"), sem("modt_mm"), sem("modt_done")
            bc_mm, gates_done = sem("bc_mm"), sem("gates_done")
            dist_iota, dist_exp, dist_done = sem("dist_iota"), sem("dist_exp"), sem("dist_done")
            dve_step, var_done, sqrt_done, xn_done = sem("dve_step"), sem("var_done"), sem("sqrt_done"), sem("xn_done")
            xt_mm, ht0_done, ht1_done = sem("xt_mm"), sem("ht0_done"), sem("ht1_done")
            proj_mm, part1, rest1, part2, part3 = sem("proj_mm"), sem("part1"), sem("rest1"), sem("part2"), sem("part3")
            val_mm, val_done, consts_done = sem("val_mm"), sem("val_done"), sem("consts_done")
            st_split, st_dist = sem("st_split"), sem("st_dist")

            psum_xt = st.enter_context(nc.psum_tensor("psum_xt", [P, 2, KC, GW], F32))
            psum_proj = st.enter_context(nc.psum_tensor("psum_proj", [P, 2, GW], F32))
            psum_val = st.enter_context(nc.psum_tensor("psum_val", [P, 2, 2, D], F32))
            ht = region_a[:, :].rearrange("p (k t) -> p k t", k=KC)
            w_sb = region_s[:, 0:3 * KC * D].rearrange("p (w k m) -> p w k m", w=3, k=KC)
            wmod_sb = region_c[:, 0:KC * 6 * D].rearrange("p (k m) -> p k m", k=KC)
            xn = region_c[:, 3072:3072 + 8 * D].rearrange("p (t d) -> p t d", d=D)
            rest = region_c[:, 5120:5120 + 2 * GW].rearrange("p (i t) -> p i t", i=2)
            parts = region_c[:, 6144:6144 + 3 * GW].bitcast(BF16).rearrange("p (i s t) -> p i s t", i=2, s=3)
            const_f = region_o[:, 2304:2304 + C_W]
            dist = region_o[0:H, 0:RW]
            silu_bc = region_p[:, 0:KC * B * P].rearrange("p (k b m) -> p k b m", k=KC, b=B)
            wo_sb = region_p[:, 512:1024].rearrange("p (k m) -> p k m", k=KC)
            attn_gate = region_p[:, 1024:1536].rearrange("p (b d) -> p b d", b=B)
            cs = st.enter_context(nc.sbuf_tensor("cs", [P, 4, KC, B], F32))
            dw_sb = st.enter_context(nc.sbuf_tensor("dw_sb", [H, 4], F32))
            bo_sb = st.enter_context(nc.sbuf_tensor("bo_sb", [P, D], F32))
            stats = st.enter_context(nc.sbuf_tensor("stats", [P, NT, 6], F32))
            gtmp = region_t[:, 0:2 * B * D].rearrange("p (i b d) -> p i b d", i=2, b=B)
            XQ = NT // 4
            N_MOD, N_REST = 2, 7

            @block.sync
            def _(sp):
                for i in range(4):
                    sp.dma_start(xs[:, i * XQ:(i + 1) * XQ, :],
                                 x[i * XQ * P:(i + 1) * XQ * P, :].rearrange("(t p) d -> p t d", p=P)).then_inc(ld_x[i], 16)
                for i, w in enumerate((wq, wk, wv)):
                    sp.dma_start(w_sb[:, i, :, :], w.rearrange("(k p) m -> p k m", p=P)).then_inc(ld_w, 16)
                sp.wait_ge(dist_done, 1)
                sp.dma_start(factor_rows, dist).then_inc(st_dist, 16)
                for u in range(4 * NG):
                    g, which, m = u // 4, (u // 2) % 2, u % 2
                    sp.wait_ge(part3, u + 1)
                    dst = (q_split, k_split)[which]
                    sp.dma_start(dst[:, m * P:(m + 1) * P, g * GW:(g + 1) * GW].rearrange("s p t -> p s t"),
                                 parts[:, u % 2, :, :]).then_inc(st_split, 16)
                sp.wait_ge(st_split, 16 * 4 * NG)
                sp.wait_ge(st_dist, 16)

            @block.gpsimd
            def _(pool):
                nc.gpsimd.iota(dist, [[-1, RW]], base=N - 1, channel_multiplier=0,
                               allow_small_or_imprecise_dtypes=True).then_inc(dist_iota, 1)
                pool.dma_start(ident[:, :], consts[:, C_ID:C_ID + P]).then_inc(ld_rest, 16)
                pool.dma_start(const_f, consts).then_inc(ld_rest, 16)
                pool.dma_start(wo_sb, wo.rearrange("(k p) m -> p k m", p=P)).then_inc(ld_rest, 16)
                pool.dma_start(gate_sb[:, :, :], gate_t.rearrange("(k p) e -> p k e", p=P)).then_inc(ld_rest, 16)
                pool.dma_start(lnw_sb[:, :], ln_w).then_inc(ld_rest, 16)
                pool.dma_start(lnb_sb[:, :], ln_b).then_inc(ld_rest, 16)
                pool.dma_start(b1_sb[:, :, :], b1.rearrange("p (e f) -> p e f", e=E)).then_inc(ld_rest, 16)
                pool.wait_ge(ld_rest, 16 * N_REST)
                nc.gpsimd.tensor_copy(bconst[:, :], const_f).then_inc(consts_done, 1)
                for u in range(4 * NG):
                    pool.wait_ge(part2, u + 1)
                    nc.gpsimd.tensor_tensor(parts[:, u % 2, 2, :], rest[:, u % 2, :], parts[:, u % 2, 1, :],
                                            ALU.subtract).then_inc(part3, 1)

            def evacuate(act, split, second, g):
                for i in range(4):
                    u = 4 * g + i
                    split(u)
                    if u >= 1:
                        second(u - 1)
                if g == NG - 1:
                    second(4 * NG - 1)
                for i in range(2):
                    act.wait_ge(val_mm, 2 * g + i + 1)
                    nc.scalar.copy(vals[:, 4 * g + 2 * i:4 * g + 2 * i + 2, :], psum_val[:, i, :, :]).then_inc(val_done, 1)

            @block.scalar
            def _(act):
                act.dma_start(cs[:, 0, :, :], c_t.rearrange("(k p) b -> p k b", p=P)).then_inc(ld_mod, 16)
                act.dma_start(dw_sb[:, 0:1], dist_w).then_inc(ld_dist, 16)
                act.dma_start(dw_sb[:, 1:2], dist_v).then_inc(ld_dist, 16)
                act.dma_start(wmod_sb, wmod.rearrange("(k p) m -> p k m", p=P)).then_inc(ld_mod, 16)
                act.dma_start(bo_sb[:, :], bass.AP(tensor=bo.tensor, offset=bo.offset, ap=[[0, P], [1, D]])).then_inc(ld_dist, 16)
                act.wait_ge(ld_mod, 16 * N_MOD)
                nc.scalar.activation(cs[:, 1, :, :], cs[:, 0, :, :], ACT.Exp, scale=-1.0).then_inc(silu_exp, 1)
                act.wait_ge(ld_dist, 48)
                nc.scalar.activation(dw_sb[:, 2:3], dw_sb[:, 1:2], ACT.Exp).then_inc(dist_exp, 1)
                act.wait_ge(dist_iota, 2)
                nc.scalar.activation(dist, dist, ACT.Exp, bias=dw_sb[:, 1:2], scale=dw_sb[:, 3:4]).then_inc(dist_exp, 1)
                for i in range(4):
                    act.wait_ge(var_done, i + 1)
                    nc.scalar.activation(rstd[:, i * XQ:(i + 1) * XQ], rstd[:, i * XQ:(i + 1) * XQ],
                                         ACT.Sqrt).then_inc(sqrt_done, 1)

                def split(u):
                    act.wait_ge(proj_mm, u + 1)
                    if u >= 2:
                        act.wait_ge(st_split, 16 * (u - 1))
                    src = psum_proj[:, u % 2, :]
                    if (u // 2) % 2 == 0:
                        src = src.rearrange("p (a b) -> p a b", b=P)[:, :, ::-1]
                    dst = parts[:, u % 2, 0, :]
                    if (u // 2) % 2 == 0:
                        dst = dst.rearrange("p (a b) -> p a b", b=P)
                    nc.scalar.copy(dst, src).then_inc(part1, 1)

                def second(u):
                    act.wait_ge(rest1, u + 1)
                    nc.scalar.copy(parts[:, u % 2, 1, :], rest[:, u % 2, :]).then_inc(part2, 1)

                for g in range(NG):
                    act.wait_ge(xt_mm, 2 * g + 1)
                    act.wait_ge(modt_done, 1)
                    nc.scalar.activation(ht[:, 0, g * GW:(g + 1) * GW], psum_xt[:, g % 2, 0, :], ACT.Identity,
                                         bias=modt[:, 0, g // (NG // B):g // (NG // B) + 1],
                                         scale=modt[:, 2, g // (NG // B):g // (NG // B) + 1]).then_inc(ht0_done, 1)
                    if g >= 1:
                        evacuate(act, split, second, g - 1)
                evacuate(act, split, second, NG - 1)

            @block.vector
            def _(dve):
                steps = [0]

                def step(ins):
                    steps[0] += 1
                    ins.then_inc(dve_step, 1)
                    dve.wait_ge(dve_step, steps[0])

                dve.wait_ge(ld_dist, 48)
                step(nc.vector.tensor_scalar(dw_sb[:, 3:4], dw_sb[:, 0:1], -1.0, None, ALU.mult))
                dve.wait_ge(dist_iota, 1)
                nc.vector.tensor_scalar(dist, dist, 0.0, None, ALU.max).then_inc(dist_iota, 1)
                dve.wait_ge(silu_exp, 1)
                step(nc.vector.tensor_scalar_add(cs[:, 2, :, :], cs[:, 1, :, :], 1.0))
                step(nc.vector.reciprocal(cs[:, 3, :, :], cs[:, 2, :, :]))
                step(nc.vector.tensor_tensor(cs[:, 1, :, :], cs[:, 0, :, :], cs[:, 3, :, :], ALU.mult))
                nc.vector.tensor_copy(silu_bc, cs[:, 1, :, :].unsqueeze(3).to_broadcast([P, KC, B, P])).then_inc(silu_done, 1)
                dve.wait_ge(dist_exp, 1)
                step(nc.vector.tensor_scalar(dw_sb[:, 2:3], dw_sb[:, 2:3], 1.0, 1.0 / HD ** 0.5, ALU.add, ALU.mult))
                dve.wait_ge(dist_exp, 2)
                step(nc.vector.tensor_scalar_add(dist, dist, 1.0))

                def norm_group(i):
                    dve.wait_ge(ld_x[i], 16)
                    for t in range(i * XQ, (i + 1) * XQ):
                        last = nc.vector.bn_stats(stats[:, t, :], xs[:, t, :])
                    step(last)
                    for t in range(i * XQ, (i + 1) * XQ):
                        last = nc.vector.bn_aggr(moments[:, t, :], stats[:, t, :])
                    step(last)
                    nc.vector.tensor_scalar_add(rstd[:, i * XQ:(i + 1) * XQ], moments[:, i * XQ:(i + 1) * XQ, 1],
                                                EPS).then_inc(var_done, 1)

                def normed_tiles(g):
                    i = g * LN_GROUP // XQ
                    if g * LN_GROUP % XQ == 0:
                        dve.wait_ge(sqrt_done, i + 1)
                        step(nc.vector.reciprocal(rstd[:, i * XQ:(i + 1) * XQ], rstd[:, i * XQ:(i + 1) * XQ]))
                    if g >= 2:
                        dve.wait_ge(xt_mm, 2 * g - 2)
                    for t in range(g * LN_GROUP, (g + 1) * LN_GROUP):
                        last = nc.vector.tensor_scalar(xn[:, t % 8, :], xs[:, t, :], moments[:, t, 0:1], rstd[:, t:t + 1],
                                                       ALU.subtract, ALU.mult)
                    last.then_inc(xn_done, 1)

                def transposed(g):
                    dve.wait_ge(xt_mm, 2 * g + 2)
                    nc.vector.tensor_scalar(ht[:, 1, g * GW:(g + 1) * GW], psum_xt[:, g % 2, 1, :],
                                            modt[:, 3, g // (NG // B):g // (NG // B) + 1],
                                            modt[:, 1, g // (NG // B):g // (NG // B) + 1], ALU.mult, ALU.add).then_inc(ht1_done, 1)

                def remainder(u):
                    dve.wait_ge(part1, u + 1)
                    if u >= 2:
                        dve.wait_ge(part3, u - 1)
                    a, b_, c_ = rest[:, u % 2, :], psum_proj[:, u % 2, :], parts[:, u % 2, 0, :]
                    if (u // 2) % 2 == 0:
                        a, b_, c_ = (v.rearrange("p (a b) -> p a b", b=P) for v in (a, b_, c_))
                        b_ = b_[:, :, ::-1]
                    nc.vector.tensor_tensor(a, b_, c_, ALU.subtract).then_inc(rest1, 1)

                norm_group(0)
                dve.wait_ge(modt_mm, 1)
                step(nc.vector.tensor_copy(modt[:, :, :], psum_val[:, 0, 0, 0:24].rearrange("p (m b) -> p m b", b=B)))
                nc.vector.tensor_scalar_add(modt[:, 2:4, :], modt[:, 2:4, :], 1.0).then_inc(modt_done, 1)
                normed_tiles(0)
                normed_tiles(1)
                for i in range(1, 4):
                    norm_group(i)
                step(nc.vector.reciprocal(dist, dist))
                step(nc.vector.tensor_scalar(dist, dist, dw_sb[:, 2:3], None, ALU.mult))
                nc.vector.memset(dist[:, N:RW], 0.0).then_inc(dist_done, 1)
                for b in range(B):
                    dve.wait_ge(bc_mm, b + 1)
                    rows = psum_proj[:, :, :].rearrange("p i (s d) -> p (i s) d", d=D)
                    nc.vector.tensor_copy(gates[:, b, 0, :], rows[:, 1, :])
                    nc.vector.tensor_scalar_add(gates[:, b, 1, :], rows[:, 2, :], 1.0)
                    for s in (0, 3):
                        nc.vector.tensor_scalar(gtmp[:, 0, b, :], rows[:, s, :], 0.0, 2.0, ALU.is_ge, ALU.mult)
                        step(nc.vector.tensor_scalar(gtmp[:, 1, b, :], rows[:, s, :], -1.0, 0.25, ALU.mult, ALU.max))
                        nc.vector.tensor_tensor(gtmp[:, 1, b, :], gtmp[:, 1, b, :], rows[:, s, :], ALU.max)
                        step(nc.vector.tensor_scalar_add(gtmp[:, 0, b, :], gtmp[:, 0, b, :], -1.0))
                        step(nc.vector.tensor_tensor(attn_gate[:, b, :] if s == 0 else gates[:, b, 2, :], gtmp[:, 0, b, :], gtmp[:, 1, b, :], ALU.mult))
                    dve.wait_ge(ld_rest, 16 * N_REST)
                    for k in range(KC):
                        nc.vector.tensor_tensor(wo_gated[:, b, k, :], wo_sb[:, k, :], attn_gate[:, b, :], ALU.mult)
                    nc.vector.tensor_tensor(bo_gated[:, b, :], bo_sb[:, :], attn_gate[:, b, :], ALU.mult).then_inc(gates_done, 1)
                for g in range(NG):
                    transposed(g)
                    if g + 2 < NG:
                        normed_tiles(g + 2)
                    if g >= 1:
                        for u in range(4 * g - 4, 4 * g):
                            remainder(u)
                for u in range(4 * NG - 4, 4 * NG):
                    remainder(u)

            @block.tensor
            def _(pe):
                pe.wait_ge(ld_mod, 16 * N_MOD)
                pe.wait_ge(silu_done, 1)
                for m in range(12):
                    for k in range(KC):
                        last = nc.tensor.matmul(psum_val[:, 0, 0, 2 * m:2 * m + 2], wmod_sb[:, k, m * P:(m + 1) * P],
                                                cs[:, 1, k, :], start=(k == 0), stop=(k == KC - 1))
                last.then_inc(modt_mm, 1)
                for b in range(B):
                    if b:
                        pe.wait_ge(gates_done, b)
                    for i in range(2):
                        for k in range(KC):
                            last = nc.tensor.matmul(psum_proj[:, i, :], silu_bc[:, k, b, :],
                                                    wmod_sb[:, k, 2 * D + i * GW:2 * D + (i + 1) * GW],
                                                    start=(k == 0), stop=(k == KC - 1))
                    last.then_inc(bc_mm, 1)
                pe.wait_ge(ld_rest, 16 * N_REST)

                def transpose_group(g):
                    pe.wait_ge(xn_done, g + 1)
                    if g >= 2:
                        pe.wait_ge(ht0_done, g - 1)
                        pe.wait_ge(ht1_done, g - 1)
                    for k in range(KC):
                        for i in range(LN_GROUP):
                            last = nc.tensor.transpose(psum_xt[:, g % 2, k, i * P:(i + 1) * P],
                                                       xn[:, (g * LN_GROUP + i) % 8, k * P:(k + 1) * P], ident[:, :])
                        last.then_inc(xt_mm, 1)

                transpose_group(0)
                pe.wait_ge(ld_w, 48)
                pe.wait_ge(gates_done, 2)
                for g in range(NG):
                    if g + 1 < NG:
                        transpose_group(g + 1)
                    pe.wait_ge(ht0_done, g + 1)
                    pe.wait_ge(ht1_done, g + 1)
                    for i in range(4):
                        u = 4 * g + i
                        if u >= 2:
                            pe.wait_ge(rest1, u - 1)
                        for k in range(KC):
                            last = nc.tensor.matmul(psum_proj[:, u % 2, :], w_sb[:, i // 2, k, (i % 2) * P:(i % 2 + 1) * P],
                                                    ht[:, k, g * GW:(g + 1) * GW], start=(k == 0), stop=(k == KC - 1))
                        last.then_inc(proj_mm, 1)
                    for i in range(2):
                        if g >= 1:
                            pe.wait_ge(val_done, 2 * g + i - 1)
                        for j in range(2):
                            t = 4 * g + 2 * i + j
                            for k in range(KC):
                                last = nc.tensor.matmul(psum_val[:, i, j, :], ht[:, k, t * P:(t + 1) * P],
                                                        w_sb[:, 2, k, :], start=(k == 0), stop=(k == KC - 1))
                        last.then_inc(val_mm, 1)

        attention(nc, locals())
        mixture(nc, locals())


def attention(nc, o):
    region_a, region_s, region_t, region_o, region_p = (o[k] for k in ("region_a", "region_s", "region_t", "region_o", "region_p"))
    vals, context, ident, ident_b = o["vals"], o["context"], o["ident"], o["ident_b"]
    mask_diag, mask_full = o["mask_diag"], o["mask_full"]
    q_split, k_split, factor_rows = o["q_split"], o["k_split"], o["factor_rows"]

    VW = 32
    NP = BT // 2
    SW = 1024
    stacks = region_s[:, :].bitcast(BF16).rearrange("p (b w t) -> p b w t", b=B, w=2)
    factors = region_t[:, :].rearrange("p (b t) -> p b t", b=B)
    rows = [r[:, q * 4096:(q + 1) * 4096].rearrange("p (w t) -> p w t", w=2)
            for r in (region_a, o["region_x"]) for q in range(2)]
    LEAD = 2
    sums = region_o[:, :].rearrange("p (b t) -> p b t", b=B)
    weights = region_p[:, :].rearrange("p (i t) -> p i t", i=4)

    def cut(nb):
        return 0 if nb <= 2 else max(nb - SW // P, (nb * 7) // 16)

    tiles = [(b, i, w) for b in range(B) for i in reversed(range(NP)) for w in range(2)]
    pairs = [(b, i) for b in range(B) for i in reversed(range(NP))]
    slots = []
    for n, (b, i, w) in enumerate(tiles):
        nb = 2 * i + w + 1
        slots.append((n, False, cut(nb), nb))
        if cut(nb):
            slots.append((n, True, 0, cut(nb)))
    NS = len(slots)
    NX = sum(s[1] for s in slots)
    NTL = len(tiles)
    NPR = len(pairs)
    blocks = [(g, k) for g, (b, i) in enumerate(pairs) for k in range(i + 1)]
    NB = len(blocks)
    NC = 4 * B
    LOADS = 7 * 16
    assert NS % 2 == 0 and NB % 4 == 0 and NPR % len(rows) == 0
    slots_of = [[s for s in range(NS) if slots[s][0] == n] for n in range(NTL)]
    x_before = [sum(slots[r][1] for r in range(s + 1)) for s in range(NS)]
    blocks_to = [sum(1 for gg, _ in blocks if gg <= g) for g in range(NPR)]
    x_tiles_to = [sum(1 for s in slots if s[1] and s[0] <= n) for n in range(NTL)]

    with ExitStack() as st, nc.Block() as block:
        sem = lambda name: st.enter_context(nc.semaphore(name))
        loaded = [sem("loaded0"), sem("loaded1")]
        score_done, relu_done, scaled = sem("score_done"), sem("relu_done"), sem("scaled")
        shifted, shifted_x, negated = sem("shifted"), sem("shifted_x"), sem("negated")
        turned, exp_done, pv_done, pv_saved = sem("turned"), sem("exp_done"), sem("pv_done"), sem("pv_saved")
        back_done, summed, recip_done, cleared = sem("back_done"), sem("summed"), sem("recip_done"), sem("cleared")
        values_done = [sem("values_done0"), sem("values_done1")]
        passed, passed_pool = sem("passed"), sem("passed_pool")
        score_ps = st.enter_context(nc.psum_tensor("score_ps", [P, 2, SW], F32))
        turn_ps = st.enter_context(nc.psum_tensor("turn_ps", [P, 2, 2, 2, P], F32))
        pv_ps = st.enter_context(nc.psum_tensor("pv_ps", [P, 2, 2 * P], F32))
        back_ps = st.enter_context(nc.psum_tensor("back_ps", [P, 4, P], F32))
        vblock = st.enter_context(nc.sbuf_tensor("vblock", [P, B, BT, VW], F32))
        maxima = st.enter_context(nc.sbuf_tensor("maxima", [P, 3, NTL], F32))
        csum = st.enter_context(nc.sbuf_tensor("csum", [P, B, BT, HD + 1], F32))
        crec = st.enter_context(nc.sbuf_tensor("crec", [P, B, BT], F32))

        FREE_SCALED, FREE_RELU, FREE_PV, FREE_BLOCKS, FREE_PAIRS, FREE_BACK = NS, NX, 4 + NB, 2 + NB, 2 + NPR, 1 + NC

        def block_range(n):
            nb = 2 * tiles[n][1] + tiles[n][2] + 1
            return cut(nb), nb

        s_of_pair = [[s for s in range(NS) if slots[s][0] // 2 == g] for g in range(NPR)]
        lead_in = [("score", s, 0) for g in range(LEAD) for s in s_of_pair[g]]
        program = []
        n = 0
        for g in range(NPR):
            count = pairs[g][1] + 1
            ahead = [("score", s, (g + LEAD) // NPR) for s in s_of_pair[(g + LEAD) % NPR]]
            for k in range(count):
                program.append(("turn", n + k, 0))
                program += ahead[len(ahead) * k // count:len(ahead) * (k + 1) // count]
                if k >= 1:
                    program.append(("pv", n + k - 1, 0))
                if k == min(1, count - 1) and g >= 2 and g % 2 == 0:
                    program.append(("back", g // 2 - 1, 0))
                if k == 0 and g == 0:
                    program.append(("values", 1, 0))
                if k == 0 and g == NPR // 2:
                    program.append(("values", 0, 1))
            program.append(("pv", n + count - 1, 0))
            n += count
        program.append(("back", NC - 1, 0))

        lead_in_tiles = [("tile", n, 0) for n in range(2 * LEAD)]
        tile_program = []
        for m in range(2 * LEAD, NTL + 2 * LEAD):
            g = m // 2
            if m % 2 == 0 and g % 2 and g >= 2 * LEAD + 1 and (g - 2 * LEAD - 1) // 2 < NC - 2:
                tile_program.append(("back", (g - 2 * LEAD - 1) // 2, 0))
            if m == NTL // 2 + 2 * (2 * LEAD):
                tile_program.append(("divide", 0, 0))
            tile_program.append(("tile", m % NTL, m // NTL))
        tile_program += [("back", NC - 2, 0), ("back", NC - 1, 0), ("divide", 1, 0)]

        def row_free(g):
            return FREE_BLOCKS + (blocks_to[g - 4] if g >= 4 else blocks_to[g - 4] - NB)

        def over_heads(eng, emit, first, body):
            for what, j, _ in first:
                emit(what, j, 0)
            with eng.Fori(0, H - 1) as h:
                for what, j, later in body:
                    emit(what, j, h + later)
            for what, j, later in body:
                if not later:
                    emit(what, j, H - 1)

        @block.sync
        def _(sp):
            def load(h, b):
                t0 = b * N
                for first, s, copies in ((0, 0, 3), (3, 1, 3), (6, 2, 2)):
                    src = q_split[s, bass.ds(h * HD, HD), t0:t0 + N]
                    src = bass.AP(tensor=src.tensor, offset=src.offset, ap=[[0, copies], *src.ap])
                    sp.dma_start(stacks[first * HD:(first + copies) * HD, b, 0, :], src).then_inc(loaded[b], 16)
                for first, count in ((0, 3), (3, 3), (6, 2)):
                    src = k_split[0:count, bass.ds(h * HD, HD), t0:t0 + N]
                    sp.dma_start(stacks[first * HD:(first + count) * HD, b, 1, :], src).then_inc(loaded[b], 16)
                src = factor_rows[bass.ds(h, 1), 0:N]
                sp.dma_start(factors[:, b, :], bass.AP(tensor=src.tensor, offset=src.offset, ap=[[1, P], [1, N]])).then_inc(loaded[b], 16)

            for b in range(B):
                load(0, b)
            with sp.Fori(0, H - 1) as h:
                for b in range(B):
                    last = max(s for s in range(NS) if tiles[slots[s][0]][0] == b) + 1
                    sp.wait_ge(scaled, h * NS + (FREE_SCALED + last))
                    load(h + 1, b)

        @block.tensor
        def _(pe):
            pe.sem_inc(pv_done, FREE_PV)

            def emit(what, j, h):
                if what == "score":
                    n, on_act, lo, hi = slots[j]
                    b, i, w = tiles[n]
                    if j == 0 or tiles[slots[j - 1][0]][0] != b:
                        pe.wait_ge(loaded[b], h * LOADS + LOADS)
                    before = (j - 2) % NS
                    if slots[before][1]:
                        pe.wait_ge(relu_done, h * NX + (FREE_RELU + x_before[before] - (0 if j >= 2 else NX)))
                    else:
                        pe.wait_ge(scaled, h * NS + (FREE_SCALED + j - 1))
                    q0 = (2 * i + w) * P
                    for c in range(lo * P, hi * P, 512):
                        wd = min(512, hi * P - c)
                        last = nc.tensor.matmul(score_ps[:, j % 2, c - lo * P:c - lo * P + wd], stacks[:, b, 0, q0:q0 + P],
                                                stacks[:, b, 1, c:c + wd], start=True, stop=True)
                    last.then_inc(score_done, 1)
                elif what == "turn":
                    g, k = blocks[j]
                    b, i = pairs[g]
                    if k == 0:
                        pe.wait_ge(shifted, h * NTL + (2 * g + 2))
                        if x_tiles_to[2 * g + 1] > (x_tiles_to[2 * g - 1] if g else 0):
                            pe.wait_ge(shifted_x, h * NX + x_tiles_to[2 * g + 1])
                    pe.wait_ge(exp_done, h * NB + (FREE_BLOCKS + j - 1))
                    for a in range(2):
                        for w in range(2):
                            kb = 2 * k + a
                            dst = turn_ps[:, j % 2, a, w, :]
                            diagonal = kb == 2 * i + w
                            if kb > 2 * i + w:
                                last = nc.tensor.matmul(dst, ident_b, mask_full, start=True, stop=True)
                                continue
                            last = nc.tensor.matmul(dst, rows[g % 4][:, w, kb * P:(kb + 1) * P], ident[:, :],
                                                    is_transpose=True, start=True, stop=not diagonal)
                            if diagonal:
                                last = nc.tensor.matmul(dst, ident_b, mask_diag, start=False, stop=True)
                    last.then_inc(turned, 1)
                elif what == "pv":
                    g, k = blocks[j]
                    b, i = pairs[g]
                    if k == 0:
                        pe.wait_ge(pv_saved, h * NPR + (FREE_PAIRS + g - 1))
                        if i == NP - 1:
                            pe.wait_ge(values_done[b], h + 1)
                    pe.wait_ge(exp_done, h * NB + (FREE_BLOCKS + j + 1))
                    for a in range(2):
                        kb = 2 * k + a
                        c = 32 * (kb % 4)
                        last = nc.tensor.matmul(pv_ps[c:c + VW, g % 2, :], vblock[:, b, kb, :],
                                                weights[:, j % 4, a * 2 * P:(a + 1) * 2 * P],
                                                start=(kb < 4), stop=(kb + 4 > 2 * i + 1))
                    last.then_inc(pv_done, 1)
                elif what == "back":
                    b, c = j // 4, j % 4
                    pe.wait_ge(pv_saved, h * NPR + (FREE_PAIRS + 2 * j + 2))
                    pe.wait_ge(summed, h * NC + (FREE_BACK + j))
                    for q in range(4):
                        qt = 4 * (3 - c) + q
                        last = nc.tensor.transpose(back_ps[:, q, :], sums[:, b, qt * P:(qt + 1) * P], ident[:, :])
                    last.then_inc(back_done, 1)

            over_heads(pe, emit, lead_in, program)

        @block.scalar
        def _(act):
            act.sem_inc(exp_done, FREE_BLOCKS)
            act.sem_inc(pv_saved, FREE_PAIRS)
            act.sem_inc(relu_done, FREE_RELU)
            act.wait_ge(cleared, 3)

            def emit(what, j, h):
                if what == "values":
                    act.wait_ge(pv_done, h * NB + (FREE_PV - NB + NB // B * (j + 1)))
                    nc.scalar.copy(vblock[:, j, :, 0:HD], vals[:, j * BT:(j + 1) * BT, bass.ds(h * HD, HD)]).then_inc(values_done[j], 1)
                elif what == "score" and slots[j][1]:
                    n, _, lo, hi = slots[j]
                    g = n // 2
                    act.wait_ge(score_done, h * NS + (j + 1))
                    act.wait_ge(exp_done, h * NB + row_free(g))
                    nc.scalar.activation(rows[g % 4][:, n % 2, lo * P:hi * P], score_ps[:, j % 2, 0:(hi - lo) * P],
                                         ACT.Relu).then_inc(relu_done, 1)
                elif what == "turn":
                    act.wait_ge(turned, h * NB + (j + 1))
                    act.wait_ge(pv_done, h * NB + (FREE_PV + j - 3))
                    nc.scalar.activation(weights[:, j % 4, :], turn_ps[:, j % 2, :, :, :].rearrange("p a w t -> p (a w t)"),
                                         ACT.Exp).then_inc(exp_done, 1)
                elif what == "pv":
                    g, k = blocks[j]
                    b, i = pairs[g]
                    if k == i:
                        act.wait_ge(pv_done, h * NB + (FREE_PV + j + 1))
                        act.wait_ge(summed, h * NC + (FREE_BACK + 4 * b + 4 - NC))
                        used = P if i else P // 2
                        nc.scalar.copy(sums[0:used, b, 2 * i * P:(2 * i + 2) * P].rearrange("p (w t) -> p w t", w=2),
                                       pv_ps[0:used, g % 2, :].rearrange("p (w t) -> p w t", w=2)[:, :, ::-1]).then_inc(pv_saved, 1)

            over_heads(act, emit, [("values", 0, 0)] + lead_in, program)

        @block.vector
        def _(dve):
            dve.sem_inc(scaled, FREE_SCALED)
            dve.sem_inc(summed, FREE_BACK)
            nc.vector.memset(sums, 0.0).then_inc(cleared, 1)
            nc.vector.memset(vblock[:, :, :, :], 0.0).then_inc(cleared, 1)
            dve.wait_ge(cleared, 2)
            nc.vector.memset(vblock[:, :, :, HD:HD + 1], 1.0).then_inc(cleared, 1)

            def scale(s, h):
                n, on_act, lo, hi = slots[s]
                b, i, w = tiles[n]
                g = n // 2
                if s == 0 or tiles[slots[s - 1][0]][0] != b:
                    dve.wait_ge(loaded[b], h * LOADS + LOADS)
                row = rows[g % 4][:, w, lo * P:hi * P]
                u0 = N - P - (2 * i + w) * P + lo * P
                if on_act:
                    dve.wait_ge(scaled, h * NS + (FREE_SCALED + s))
                    dve.wait_ge(relu_done, h * NX + (FREE_RELU + x_before[s]))
                    src, start = row, maxima[:, 0, n:n + 1]
                else:
                    dve.wait_ge(exp_done, h * NB + row_free(g))
                    dve.wait_ge(score_done, h * NS + (s + 1))
                    src, start = score_ps[:, s % 2, 0:(hi - lo) * P], 0.0
                dve.sem_inc(passed, 1)
                nc.vector.tensor_tensor_reduce(out=row, in0=src, in1=factors[:, b, u0:u0 + (hi - lo) * P], scale=1.0,
                                               scalar=start, op0=ALU.mult, op1=ALU.max,
                                               accum_out=maxima[:, int(on_act), n:n + 1]).then_inc(scaled, 1)

            def shift(n, h):
                b, i, w = tiles[n]
                lo, hi = block_range(n)
                dve.wait_ge(scaled, h * NS + (FREE_SCALED + slots_of[n][-1] + 1))
                row = rows[(n // 2) % 4][:, w, lo * P:hi * P]
                top = maxima[:, 1 if lo else 0, n:n + 1]
                nc.vector.tensor_scalar(row, row, 0.0, top, ALU.max, ALU.subtract).then_inc(shifted, 1)

            def emit(what, j, h):
                if what == "tile":
                    scale(slots_of[j][0], h)
                    if j not in (0, 2 * LEAD):
                        shift(j - 1, h)
                    for s in slots_of[j][1:]:
                        scale(s, h)
                    if j in (2 * LEAD - 1, NTL - 1):
                        shift(j, h)
                elif what == "back":
                    b, c = j // 4, j % 4
                    dve.wait_ge(back_done, h * NC + (j + 1))
                    q0 = 4 * (3 - c)
                    nc.vector.tensor_reduce(csum[:, b, q0:q0 + 4, :],
                                            back_ps[:, :, :].rearrange("p q (j r) -> p q r j", r=VW)[:, :, 0:HD + 1, :],
                                            AX.X, ALU.add).then_inc(summed, 1)
                else:
                    b = j
                    dve.wait_ge(summed, h * NC + (FREE_BACK + 4 * b + 4))
                    nc.vector.reciprocal(crec[:, b, :], csum[:, b, :, HD]).then_inc(recip_done, 1)
                    dve.wait_ge(recip_done, h * B + (b + 1))
                    nc.vector.tensor_tensor(context[:, b * BT:(b + 1) * BT, bass.ds(h * HD, HD)], csum[:, b, :, 0:HD],
                                            crec[:, b, :].unsqueeze(2).to_broadcast([P, BT, HD]), ALU.mult)

            over_heads(dve, emit, lead_in_tiles, tile_program)

        @block.gpsimd
        def _(pool):
            def emit(what, n, h):
                if what != "tile" or not block_range(n)[0]:
                    return
                lo, hi = block_range(n)
                pool.wait_ge(scaled, h * NS + (FREE_SCALED + slots_of[n][-1] + 1))
                pool.sem_inc(passed_pool, 1)
                nc.gpsimd.tensor_scalar(maxima[:, 2, n:n + 1], maxima[:, 1, n:n + 1], -1.0, 0.0, ALU.mult, ALU.add).then_inc(negated, 1)
                pool.wait_ge(negated, h * NX + x_tiles_to[n])
                pool.sem_inc(passed_pool, 1)
                row = rows[(n // 2) % 4][:, n % 2, 0:lo * P]
                nc.gpsimd.tensor_scalar(row, row, maxima[:, 2, n:n + 1], 1.0, ALU.add, ALU.mult).then_inc(shifted_x, 1)

            over_heads(pool, emit, lead_in_tiles, tile_program)


def mixture(nc, o):
    g_ = lambda *names: [o[k] for k in names]
    x, out, normed, fc1_t, fc2_t, b2 = g_("x", "out", "normed", "fc1_t", "fc2_t", "b2")
    xs, context, ident, gates, gate_sb = g_("xs", "context", "ident", "gates", "gate_sb")
    wo_gated, bo_gated, lnw_sb, lnb_sb, b1_sb = g_("wo_gated", "bo_gated", "lnw_sb", "lnb_sb", "b1_sb")
    same_expert, rows_before, tile_of, row_of, iota_row = g_("same_expert", "rows_before", "tile_of", "row_of", "iota_row")
    region_a, region_v, region_s, region_t, region_o, region_p, region_x = g_(
        "region_a", "region_v", "region_s", "region_t", "region_o", "region_p", "region_x")

    GT = 4
    G = NT // GT
    GB = G // B
    T2 = NT // 2
    COLS = NT * E
    LOW = 32
    HIGH = CAP // LOW
    BITS = 30

    with ExitStack() as st, nc.Block() as block:
        sem = lambda name: st.enter_context(nc.semaphore(name))
        ld_x = [sem(f"ld_x2_{i}") for i in range(4)]
        xb_done, ctx_turned, ctxt_done, proj_done = sem("xb_done"), sem("ctx_turned"), sem("ctxt_done"), sem("proj_done")
        x2_done, rstd1_done, z_done, h2_done, rstd2_done = sem("x2_done"), sem("rstd1_done"), sem("z_done"), sem("h2_done"), sem("rstd2_done")
        h2_turned, h2t_done, gate_mm, gate_saved, gate_back, logits_done = (
            sem("h2_turned"), sem("h2t_done"), sem("gate_mm"), sem("gate_saved"), sem("gate_back"), sem("logits_done"))
        gbh_done, base_done, normed_done = sem("gbh_done"), sem("base_done"), sem("normed_done")
        st_out, st_normed, st_scores = sem("st_out"), sem("st_normed"), sem("st_scores")
        dve_step, cleared = sem("dve_step2"), sem("cleared2")
        centred, exped, scores_done, scores_turned = sem("centred"), sem("exped"), sem("scores_done"), sem("scores_turned")
        counted, totalled, places_done, places_turned = sem("counted"), sem("totalled"), sem("places_done"), sem("places_turned")
        onehot_done, tokens_mm, tokens_done, idx_moved = sem("onehot_done"), sem("tokens_mm"), sem("tokens_done"), sem("idx_moved")
        ld_weights, gathered = [sem("ld_weights0"), sem("ld_weights1")], [sem("gathered0"), sem("gathered1")]
        idx_copied, y_turned, yt_done = sem("idx_copied"), sem("y_turned"), sem("yt_done")
        fc1_mm, gelu_done, fc2_mm, o_done, scattered = sem("fc1_mm"), sem("gelu_done"), sem("fc2_mm"), sem("o_done"), sem("scattered")
        sum_done, kept_done, gw_step, bits_set = sem("sum_done"), sem("kept_done"), sem("gw_step"), sem("bits_set")
        var_done, sqrt_done = [sem("var1_done"), sem("var2_done")], [sem("sqrt1_done"), sem("sqrt2_done")]
        passed_pool = sem("passed_pool2")

        bank = [st.enter_context(nc.psum_tensor(f"bank{i}", [P, 512], F32)) for i in range(8)]
        ctx_ps, h2_ps, gate_ps, small_ps = bank[0:2], bank[2:4], bank[6], bank[7]
        proj_ps = [bank[4 + i][:, :].rearrange("p (t d) -> p t d", d=D) for i in range(2)]
        y_ps, fc1_ps, fc2_ps = bank[0:2], bank[2:4], bank[4:6]

        ctxt = region_s[:, 0:2048].rearrange("p (i k t) -> p i k t", i=2, k=KC)
        h2t = region_s[:, 2048:4096].rearrange("p (i k t) -> p i k t", i=2, k=KC)
        h2 = region_a[:, :].rearrange("p (t d) -> p t d", d=D)
        base = region_v[:, :].rearrange("p (t d) -> p t d", d=D)
        nrm = context
        stats = region_t[:, 0:NT * 6].rearrange("p (t s) -> p t s", s=6)
        mom = region_t[:, 192:192 + 2 * NT * 2].rearrange("p (l t s) -> p l t s", l=2, s=2)
        rst = region_t[:, 320:320 + 2 * NT].rearrange("p (l t) -> p l t", l=2)
        nmr = region_t[:, 384:384 + 2 * NT].rearrange("p (l t) -> p l t", l=2)
        gate_t_sb = region_t[:, 512:512 + 2 * P].rearrange("p (i t) -> p i t", i=2)
        scores = region_t[:, 1024:1024 + COLS].rearrange("p (h t e) -> p h t e", h=2, e=E)
        row_stat = region_t[:, 1280:1280 + 2 * NT].rearrange("p (i t) -> p i t", i=2)

        def tokens(i):
            return region_p[:, i * 256:(i + 1) * 256]
        scores_t, above, equal, chosen, run, zeros, trash = (tokens(i) for i in range(7))
        found = st.enter_context(nc.sbuf_tensor("found", [P, 4], I32))
        bits = st.enter_context(nc.sbuf_tensor("bits", [P, BITS], I32))
        count_b = st.enter_context(nc.sbuf_tensor("count_b", [P, 4], BF16))
        count_f = st.enter_context(nc.sbuf_tensor("count_f", [P, 4], F32))
        high = region_t[:, 1536:1536 + COLS // 2].bitcast(BF16)
        low = region_t[:, 1664:1664 + COLS // 2].bitcast(BF16)
        place_i = region_p[:, 0:3 * COLS].bitcast(I32).rearrange("p (i c) -> p i c", i=3)
        high_hot = region_t[:, 2048:4096].bitcast(BF16).rearrange("p (c r) -> p c r", r=HIGH)
        low_hot = region_o[:, :].bitcast(BF16).rearrange("p (c r) -> p c r", r=LOW)
        token_of = region_s[:, :].bitcast(BF16).rearrange("p (s c r) -> p s c r", r=HIGH, s=2)
        idx_low = st.enter_context(nc.sbuf_tensor("idx_low", [LOW, E, HIGH], U32))
        idx_f = region_t[0:LOW, 1792:1792 + E * HIGH].rearrange("p (e r) -> p e r", e=E)
        powers = st.enter_context(nc.sbuf_tensor("powers", [P, BITS], I32))
        idx_all = st.enter_context(nc.sbuf_tensor("idx_all", [P, E, EC], U32))
        idx_cur = st.enter_context(nc.sbuf_tensor("idx_cur", [P, 2, EC], U32))
        sides = st.enter_context(nc.sbuf_tensor("sides", [P, B, E, EC], F32))
        kept = st.enter_context(nc.sbuf_tensor("kept", [P, 2, B, EC], F32))
        w1_sb = [region_x[:, i * 4096:i * 4096 + 2048].rearrange("p (k f) -> p k f", k=KC) for i in range(2)]
        w2_sb = [region_x[:, i * 4096 + 2048:(i + 1) * 4096].rearrange("p (f d) -> p f d", d=D) for i in range(2)]
        hidden = region_a[:, 0:4096].rearrange("p (f t) -> p f t", f=FC)
        yt = region_a[:, 4096:6144].rearrange("p (i k t) -> p i k t", i=2, k=KC)
        o_sb = region_a[:, 6144:8192].rearrange("p (i c d) -> p i c d", i=2, c=EC)
        y_sb = region_v[:, 0:2 * EC * NW].rearrange("p (i c w) -> p i c w", i=2, c=EC)
        b2_sb = region_v[:, 4096:4096 + 2 * D].rearrange("p (i d) -> p i d", i=2)
        gw = region_v[:, 5120:5120 + EC * D].rearrange("p (c d) -> p c d", c=EC)

        def over_experts(eng, emit):
            with eng.Fori(0, E // 2 - 1) as n:
                emit(2 * n, n, 0, True, True)
                emit(2 * n + 1, n, 1, True, True)
            emit(E - 2, E // 2 - 1, 0, True, False)
            emit(E - 1, E // 2 - 1, 1, False, False)

        def at(e, base=0):
            return bass.ds(e + base, 1) if not isinstance(e, int) else slice(e + base, e + base + 1)

        @block.sync
        def _(sp):
            XQ = NT // 4
            for i in range(4):
                sp.dma_start(xs[:, i * XQ:(i + 1) * XQ, :],
                             x[i * XQ * P:(i + 1) * XQ * P, :].rearrange("(t p) d -> p t d", p=P)).then_inc(ld_x[i], 16)
            for g in range(G):
                t0, t1 = g * GT, (g + 1) * GT
                sp.wait_ge(base_done, g + 1)
                sp.dma_start(out[t0 * P:t1 * P, :].rearrange("(t p) d -> p t d", p=P), base[:, t0:t1, :]).then_inc(st_out, 16)
                sp.wait_ge(normed_done, g + 1)
                sp.dma_start(normed[t0 * P:t1 * P, 0:D].rearrange("(t p) d -> p t d", p=P), nrm[:, t0:t1, :]).then_inc(st_normed, 16)

            def load(e, i):
                src = fc1_t[at(e), :, :]
                sp.dma_start(w1_sb[i], src.rearrange("o (k p) f -> p (o k) f", p=P)).then_inc(ld_weights[i], 16)
                src = fc2_t[at(e), :, :]
                sp.dma_start(w2_sb[i], src.rearrange("o (f p) d -> p (o f) d", p=P)).then_inc(ld_weights[i], 16)
                src = b2[at(e), :]
                sp.dma_start(b2_sb[:, i, :], bass.AP(tensor=src.tensor, offset=src.offset, ap=[[0, P], [1, D]])).then_inc(ld_weights[i], 16)

            sp.wait_ge(st_out, 16 * G)
            for i in range(2):
                load(i, i)
            sp.wait_ge(scores_done, 1)
            for half in range(2):
                sp.dma_start(normed[:, D:NW].rearrange("(t h p) e -> h p t e", h=2, p=P)[half], scores[:, half, :, :]).then_inc(st_scores, 16)
            sp.wait_ge(tokens_done, 1)
            for j in range(P // LOW):
                sp.dma_start(idx_all[j * LOW:(j + 1) * LOW, :, :], idx_low[:, :, j * EC:(j + 1) * EC]).then_inc(idx_moved, 16)
            with sp.Fori(0, E // 2 - 1) as i:
                for j in range(2):
                    sp.wait_ge(sum_done, i * (2 * EC) + (2 + (j + 1) * EC))
                    load(2 * i + (2 + j), j)
            sp.wait_ge(scattered, 16 * EC * E)

        @block.tensor
        def _(pe):
            for s in range(G + 3):
                if s < G:
                    g = s
                    for k in range(KC):
                        if g:
                            pe.wait_ge(ctxt_done, KC * (g - 1) + k + 1)
                        for i in range(GT):
                            last = nc.tensor.transpose(ctx_ps[k][:, i * P:(i + 1) * P],
                                                       context[:, g * GT + i, k * P:(k + 1) * P], ident[:, :])
                        last.then_inc(ctx_turned, 1)
                if 0 <= s - 1 < G:
                    g = s - 1
                    pe.wait_ge(ctxt_done, KC * (g + 1))
                    if g:
                        pe.wait_ge(x2_done, g)
                    for i in range(GT):
                        for k in range(KC):
                            last = nc.tensor.matmul(proj_ps[i // 2][:, i % 2, :], ctxt[:, g % 2, k, i * P:(i + 1) * P],
                                                    wo_gated[:, g // GB, k, :], start=(k == 0), stop=(k == KC - 1))
                    last.then_inc(proj_done, 1)
                if 0 <= s - 3:
                    g = s - 3
                    pe.wait_ge(h2_done, g + 1)
                    for k in range(KC):
                        if g:
                            pe.wait_ge(h2t_done, KC * (g - 1) + k + 1)
                        for i in range(GT):
                            last = nc.tensor.transpose(h2_ps[k][:, i * P:(i + 1) * P], h2[:, g * GT + i, k * P:(k + 1) * P], ident[:, :])
                        last.then_inc(h2_turned, 1)
                    pe.wait_ge(h2t_done, KC * (g + 1))
                    if g:
                        pe.wait_ge(gate_saved, g)
                    else:
                        pe.wait_ge(cleared, 1)
                    for k in range(KC):
                        for i in range(GT):
                            last = nc.tensor.matmul(gate_ps[32 * i:32 * i + E, 0:P], gate_sb[:, k, :],
                                                    h2t[:, g % 2, k, i * P:(i + 1) * P], start=(k == 0), stop=(k == KC - 1))
                    last.then_inc(gate_mm, 1)
                    pe.wait_ge(gate_saved, g + 1)
                    if g:
                        pe.wait_ge(logits_done, g)
                    nc.tensor.transpose(small_ps[:, 0:P], gate_t_sb[:, g % 2, :], ident[:, :]).then_inc(gate_back, 1)
            pe.wait_ge(scores_done, 1)
            for half in range(2):
                last = nc.tensor.transpose(small_ps[:, half * P:(half + 1) * P],
                                           scores[:, half, :, :].rearrange("p t e -> p (t e)"), ident[:, :])
            last.then_inc(scores_turned, 1)
            for i in range(BITS + 1):
                pe.wait_ge(counted, i + 1)
                nc.tensor.matmul(gate_ps[:, i % 2:i % 2 + 1], same_expert, count_b[:, i % 2:i % 2 + 1], start=True, stop=True).then_inc(totalled, 1)
            for i in range(2):
                pe.wait_ge(counted, BITS + 2 + i)
                nc.tensor.matmul(gate_ps[:, 2 + i:3 + i], rows_before, count_b[:, 2 + i:3 + i], start=True, stop=True).then_inc(totalled, 1)
            pe.wait_ge(places_done, 1)
            for half in range(2):
                last = nc.tensor.transpose(small_ps[:, half * P:(half + 1) * P], chosen[:, half * P:(half + 1) * P], ident[:, :])
            last.then_inc(places_turned, 1)
            pe.wait_ge(onehot_done, 3)
            for e in range(E):
                for t in range(NT):
                    c = t * E + e
                    last = nc.tensor.matmul(bank[5][0:LOW, e * 2 * HIGH:(e + 1) * 2 * HIGH], low_hot[:, c, :],
                                            token_of[:, :, c, :], start=(t == 0), stop=(t == NT - 1))
                last.then_inc(tokens_mm, 1)

            def turn(n, i):
                pe.wait_ge(gathered[i], n * (16 * EC) + 16 * EC)
                for k in range(KC):
                    for c in range(EC):
                        last = nc.tensor.transpose(y_ps[k][:, c * P:(c + 1) * P], y_sb[:, i, c, k * P:(k + 1) * P], ident[:, :])
                    last.then_inc(y_turned, 1)

            def emit(e, n, i, ahead, gathers):
                pe.wait_ge(ld_weights[i], n * 48 + 48)
                pe.wait_ge(yt_done, e * KC + KC)
                for f in range(FC):
                    pe.wait_ge(gelu_done, e * FC + (f + 1))
                    for k in range(KC):
                        last = nc.tensor.matmul(fc1_ps[f % 2][:, :], w1_sb[i][:, k, f * P:(f + 1) * P], yt[:, i, k, :],
                                                start=(k == 0), stop=(k == KC - 1))
                    last.then_inc(fc1_mm, 1)
                if ahead:
                    turn(n + i, 1 - i)
                for c in range(EC):
                    pe.wait_ge(sum_done, e * EC + (c + 1))
                    for f in range(FC):
                        if c == 0 and f >= FC - 2:
                            pe.wait_ge(gelu_done, e * FC + (f + 3))
                        last = nc.tensor.matmul(fc2_ps[c % 2][:, 0:D], hidden[:, f, c * P:(c + 1) * P], w2_sb[i][:, f, :],
                                                start=(f == 0), stop=(f == FC - 1))
                    last.then_inc(fc2_mm, 1)

            turn(0, 0)
            over_experts(pe, emit)

        @block.scalar
        def _(act):
            act.sem_inc(gelu_done, 2)

            def deviation(lvl, g):
                act.wait_ge(var_done[lvl], g + 1)
                nc.scalar.activation(rst[:, lvl, g * GT:(g + 1) * GT], rst[:, lvl, g * GT:(g + 1) * GT], ACT.Sqrt).then_inc(sqrt_done[lvl], 1)

            for s in range(G + 3):
                if s < G:
                    g = s
                    for k in range(KC):
                        act.wait_ge(ctx_turned, KC * g + k + 1)
                        if g >= 2:
                            act.wait_ge(proj_done, g - 1)
                        nc.scalar.copy(ctxt[:, g % 2, k, :], ctx_ps[k][:, :]).then_inc(ctxt_done, 1)
                if 0 <= s - 1 < G:
                    deviation(0, s - 1)
                if s >= 3:
                    g = s - 3
                    for k in range(KC):
                        act.wait_ge(h2_turned, KC * g + k + 1)
                        if g >= 2:
                            act.wait_ge(gate_mm, g - 1)
                        nc.scalar.copy(h2t[:, g % 2, k, :], h2_ps[k][:, :]).then_inc(h2t_done, 1)
                if 0 <= s - 1 < G:
                    g = s - 1
                    act.wait_ge(rstd1_done, g + 1)
                    for t in range(g * GT, (g + 1) * GT):
                        last = nc.scalar.activation(h2[:, t, :], xs[:, t, :], ACT.Identity, bias=nmr[:, 0, t:t + 1], scale=rst[:, 0, t:t + 1])
                    last.then_inc(z_done, 1)
                if 0 <= s - 2 < G:
                    deviation(1, s - 2)
                if s >= 3:
                    g = s - 3
                    act.wait_ge(gate_mm, g + 1)
                    if g >= 2:
                        act.wait_ge(gate_back, g - 1)
                    nc.scalar.copy(gate_t_sb[:, g % 2, :], gate_ps[:, 0:P]).then_inc(gate_saved, 1)
                    act.wait_ge(rstd2_done, g + 1)
                    for t in range(g * GT, (g + 1) * GT):
                        last = nc.scalar.activation(nrm[:, t, :], h2[:, t, :], ACT.Identity, bias=nmr[:, 1, t:t + 1], scale=rst[:, 1, t:t + 1])
                    last.then_inc(normed_done, 1)
            act.wait_ge(centred, 1)
            nc.scalar.activation(scores[:, :, :, :], scores[:, :, :, :], ACT.Exp).then_inc(exped, 1)

            def emit(e, n, i, ahead, gathers):
                for f in range(FC):
                    act.wait_ge(fc1_mm, e * FC + (f + 1))
                    nc.scalar.activation(hidden[:, f, :], fc1_ps[f % 2][:, :], ACT.Gelu_apprx_tanh,
                                         bias=b1_sb[:, at(e), f].rearrange("p o -> p o")).then_inc(gelu_done, 1)

            over_experts(act, emit)

        @block.vector
        def _(dve):
            dve.sem_inc(sum_done, 2)
            steps = [0]

            def step(ins):
                steps[0] += 1
                ins.then_inc(dve_step, 1)
                dve.wait_ge(dve_step, steps[0])

            nc.vector.memset(gate_ps[:, :], 0.0).then_inc(cleared, 1)
            dve.wait_ge(bits_set, 2)
            nc.vector.tensor_tensor(bits[:, :], bits[:, :], powers[:, :], ALU.logical_shift_left)

            def norm(lvl, g, src):
                t0, t1 = g * GT, (g + 1) * GT
                for t in range(t0, t1):
                    last = nc.vector.bn_stats(stats[:, t, :], src[:, t, :])
                step(last)
                for t in range(t0, t1):
                    last = nc.vector.bn_aggr(mom[:, lvl, t, :], stats[:, t, :])
                step(last)
                nc.vector.tensor_scalar_add(rst[:, lvl, t0:t1], mom[:, lvl, t0:t1, 1], EPS).then_inc(var_done[lvl], 1)

            def rest_of_norm(lvl, g, done):
                t0, t1 = g * GT, (g + 1) * GT
                dve.wait_ge(sqrt_done[lvl], g + 1)
                step(nc.vector.reciprocal(rst[:, lvl, t0:t1], rst[:, lvl, t0:t1]))
                nc.vector.scalar_tensor_tensor(nmr[:, lvl, t0:t1], mom[:, lvl, t0:t1, 0], -1.0, rst[:, lvl, t0:t1], ALU.mult, ALU.mult).then_inc(done, 1)

            for s in range(G + 3):
                if 0 <= s - 1 < G:
                    g = s - 1
                    t0, t1 = g * GT, (g + 1) * GT
                    dve.wait_ge(proj_done, g + 1)
                    dve.wait_ge(xb_done, g + 1)
                    nc.vector.tensor_tensor(xs[:, t0:t0 + 2, :], xs[:, t0:t0 + 2, :], proj_ps[0], ALU.add)
                    nc.vector.tensor_tensor(xs[:, t0 + 2:t1, :], xs[:, t0 + 2:t1, :], proj_ps[1], ALU.add).then_inc(x2_done, 1)
                    dve.wait_ge(x2_done, g + 1)
                    norm(0, g, xs)
                if 0 <= s - 2 < G:
                    g = s - 2
                    b, t0, t1 = g // GB, g * GT, (g + 1) * GT
                    dve.wait_ge(z_done, g + 1)
                    step(nc.vector.tensor_tensor(h2[:, t0:t1, :], h2[:, t0:t1, :], gates[:, b, 1, :].unsqueeze(1).to_broadcast([P, GT, D]), ALU.mult))
                    nc.vector.tensor_tensor(h2[:, t0:t1, :], h2[:, t0:t1, :], gates[:, b, 0, :].unsqueeze(1).to_broadcast([P, GT, D]), ALU.add).then_inc(h2_done, 1)
                if 0 <= s - 1 < G:
                    rest_of_norm(0, s - 1, rstd1_done)
                if 0 <= s - 2 < G:
                    dve.wait_ge(h2_done, s - 1)
                    norm(1, s - 2, h2)
                if s >= 3:
                    g = s - 3
                    dve.wait_ge(gate_back, g + 1)
                    nc.vector.tensor_copy(scores[:, :, 2 * g:2 * g + 2, :].rearrange("p h t e -> p t h e"),
                                          small_ps[:, 0:P].rearrange("p (t h r) -> p t h r", t=2, h=2)[:, :, :, 0:E]).then_inc(logits_done, 1)
                if 0 <= s - 2 < G:
                    rest_of_norm(1, s - 2, rstd2_done)
            dve.wait_ge(logits_done, G)
            every = scores[:, :, :, :].rearrange("p h t e -> p (h t) e")
            step(nc.vector.tensor_reduce(row_stat[:, 0, :], every, AX.X, ALU.max))
            nc.vector.tensor_tensor(every, every, row_stat[:, 0, :].unsqueeze(2).to_broadcast([P, NT, E]), ALU.subtract).then_inc(centred, 1)
            nc.vector.memset(found[:, 0:1], 0)
            nc.vector.memset(zeros, 0.0)
            dve.wait_ge(exped, 1)
            step(nc.vector.tensor_reduce(row_stat[:, 0, :], every, AX.X, ALU.add))
            step(nc.vector.reciprocal(row_stat[:, 1, :], row_stat[:, 0, :]))
            nc.vector.tensor_tensor(every, every, row_stat[:, 1, :].unsqueeze(2).to_broadcast([P, NT, E]), ALU.mult).then_inc(scores_done, 1)
            step(nc.vector.tensor_copy(found[:, 1:2], bits[:, BITS - 1:BITS]))
            dve.wait_ge(scores_turned, 1)
            step(nc.vector.tensor_copy(scores_t, small_ps[:, 0:2 * P]))
            for i in range(BITS):
                bit = BITS - 1 - i
                nc.vector.tensor_scalar(trash, scores_t, found[:, 1:2].bitcast(F32), None, ALU.is_ge, ALU.add,
                                        accum_out=count_b[:, i % 2:i % 2 + 1]).then_inc(counted, 1)
                dve.wait_ge(totalled, i + 1)
                step(nc.vector.tensor_scalar(found[:, 2:3], gate_ps[:, i % 2:i % 2 + 1], float(CAP), float(1 << bit), ALU.is_ge, ALU.mult))
                step(nc.vector.tensor_tensor(found[:, 0:1], found[:, 0:1], found[:, 2:3], ALU.bitwise_or))
                if bit:
                    step(nc.vector.tensor_tensor(found[:, 1:2], found[:, 0:1], bits[:, bit - 1:bit], ALU.bitwise_or))
            threshold = found[:, 0:1].bitcast(F32)
            nc.vector.tensor_scalar(above, scores_t, threshold, None, ALU.is_gt, ALU.add, accum_out=count_b[:, BITS % 2:BITS % 2 + 1]).then_inc(counted, 1)
            nc.vector.tensor_scalar(equal, scores_t, threshold, None, ALU.is_equal, ALU.add, accum_out=count_b[:, 2:3]).then_inc(counted, 1)
            dve.wait_ge(counted, BITS + 2)
            step(nc.vector.tensor_tensor_scan(run, equal, zeros, 0.0, ALU.add, ALU.add))
            dve.wait_ge(totalled, BITS + 2)
            step(nc.vector.tensor_scalar(count_f[:, 0:1], gate_ps[:, BITS % 2:BITS % 2 + 1], -1.0, float(CAP), ALU.mult, ALU.add))
            step(nc.vector.tensor_tensor(count_f[:, 0:1], count_f[:, 0:1], gate_ps[:, 2:3], ALU.subtract))
            step(nc.vector.scalar_tensor_tensor(equal, run, count_f[:, 0:1], equal, ALU.is_le, ALU.mult))
            step(nc.vector.tensor_tensor(above, above, equal, ALU.add))
            nc.vector.tensor_scalar(trash, above, 1.0, None, ALU.mult, ALU.add, accum_out=count_b[:, 3:4]).then_inc(counted, 1)
            step(nc.vector.tensor_tensor_scan(run, above, zeros, 0.0, ALU.add, ALU.add))
            dve.wait_ge(totalled, BITS + 3)
            step(nc.vector.tensor_copy(count_f[:, 1:2], gate_ps[:, 3:4]))
            nc.vector.scalar_tensor_tensor(chosen, run, count_f[:, 1:2], above, ALU.add, ALU.mult).then_inc(places_done, 1)
            dve.wait_ge(places_turned, 1)
            step(nc.vector.tensor_scalar(place_i[:, 0, :], small_ps[:, 0:2 * P], float(LOW - 1), None, ALU.add))
            nc.vector.tensor_scalar(place_i[:, 1, :], place_i[:, 0, :], LOW.bit_length() - 1, None, ALU.arith_shift_right)
            step(nc.vector.tensor_scalar(place_i[:, 2, :], place_i[:, 0, :], LOW - 1, None, ALU.bitwise_and))
            nc.vector.tensor_copy(high, place_i[:, 1, :])
            step(nc.vector.tensor_scalar_add(low, place_i[:, 2, :], 1.0))
            step(nc.vector.tensor_tensor(high_hot, iota_row[:, 0:HIGH].unsqueeze(1).to_broadcast([P, COLS, HIGH]),
                                         high.unsqueeze(2).to_broadcast([P, COLS, HIGH]), ALU.is_equal))
            nc.vector.tensor_tensor(token_of[:, 0, :, :], high_hot, tile_of.unsqueeze(2).to_broadcast([P, COLS, HIGH]),
                                    ALU.mult).then_inc(onehot_done, 1)
            nc.vector.tensor_tensor(token_of[:, 1, :, :], high_hot, row_of.unsqueeze(2).to_broadcast([P, COLS, HIGH]),
                                    ALU.mult).then_inc(onehot_done, 1)
            nc.vector.tensor_tensor(low_hot, iota_row[:, 0:LOW].unsqueeze(1).to_broadcast([P, COLS, LOW]),
                                    low.unsqueeze(2).to_broadcast([P, COLS, LOW]), ALU.is_equal).then_inc(onehot_done, 1)
            dve.wait_ge(tokens_mm, E)
            found_ps = bank[5][0:LOW, 0:E * 2 * HIGH].rearrange("p (e s r) -> p e s r", e=E, s=2)
            step(nc.vector.tensor_scalar(idx_f, found_ps[:, :, 0, :], float(P), None, ALU.mult))
            nc.vector.tensor_tensor(idx_low[:, :, :], idx_f, found_ps[:, :, 1, :], ALU.add).then_inc(tokens_done, 1)
            dve.wait_ge(idx_moved, 16 * (P // LOW))
            nc.vector.tensor_scalar(sides[:, 0, :, :], idx_all[:, :, :], float(N), None, ALU.is_lt)
            step(nc.vector.tensor_scalar(sides[:, 1, :, :], idx_all[:, :, :], float(N), None, ALU.is_ge))

            def normed_in(e, i):
                for k in range(KC):
                    dve.wait_ge(y_turned, e * KC + (k + 1))
                    nc.vector.tensor_scalar(yt[:, i, k, :], y_ps[k][:, :], lnw_sb[:, k:k + 1], lnb_sb[:, k:k + 1],
                                            ALU.mult, ALU.add).then_inc(yt_done, 1)

            def emit(e, n, i, ahead, gathers):
                dve.wait_ge(gathered[i], n * (16 * EC) + 16 * EC)
                for b in range(B):
                    last = nc.vector.tensor_tensor(kept[:, i, b, :], y_sb[:, i, :, at(e, D)].rearrange("p c o -> p (c o)"),
                                                   sides[:, b, at(e), :].rearrange("p o c -> p (o c)"), ALU.mult)
                last.then_inc(kept_done, 1)
                dve.wait_ge(kept_done, e + 1)
                for c in range(EC):
                    last = nc.vector.tensor_scalar(gw[:, c, :], gates[:, 0, 2, :], kept[:, i, 0, c:c + 1], None, ALU.mult)
                last.then_inc(gw_step, 1)
                dve.wait_ge(gw_step, e * 2 + 1)
                for c in range(EC):
                    last = nc.vector.scalar_tensor_tensor(gw[:, c, :], gates[:, 1, 2, :], kept[:, i, 1, c:c + 1], gw[:, c, :], ALU.mult, ALU.add)
                last.then_inc(gw_step, 1)
                if ahead:
                    normed_in(e + 1, 1 - i)
                for c in range(EC):
                    dve.wait_ge(fc2_mm, e * EC + (c + 1))
                    if c == 0:
                        dve.wait_ge(ld_weights[i], n * 48 + 48)
                    nc.vector.tensor_tensor(o_sb[:, i, c, :], fc2_ps[c % 2][:, 0:D], b2_sb[:, i, :], ALU.add).then_inc(sum_done, 1)
                    dve.wait_ge(sum_done, e * EC + (c + 3))
                    if c == 0:
                        dve.wait_ge(gw_step, e * 2 + 2)
                    nc.vector.tensor_tensor(o_sb[:, i, c, :], o_sb[:, i, c, :], gw[:, c, :], ALU.mult).then_inc(o_done, 1)

            normed_in(0, 0)
            over_experts(dve, emit)

        @block.gpsimd
        def _(pool):
            nc.gpsimd.memset(bits[:, :], 1).then_inc(bits_set, 1)
            nc.gpsimd.iota(powers[:, :], [[1, BITS]], base=0, channel_multiplier=0).then_inc(bits_set, 1)
            for s in range(G + 3):
                if s < G:
                    g = s
                    t0, t1 = g * GT, (g + 1) * GT
                    if g % 2 == 0:
                        pool.wait_ge(ld_x[g // 2], 16)
                    nc.gpsimd.tensor_tensor(xs[:, t0:t1, :], xs[:, t0:t1, :], bo_gated[:, g // GB, :].unsqueeze(1).to_broadcast([P, GT, D]),
                                            ALU.add).then_inc(xb_done, 1)
                if s >= 3:
                    g = s - 3
                    t0, t1 = g * GT, (g + 1) * GT
                    pool.wait_ge(h2_done, g + 1)
                    nc.gpsimd.tensor_tensor(base[:, t0:t1, :], h2[:, t0:t1, :], gates[:, g // GB, 2, :].unsqueeze(1).to_broadcast([P, GT, D]),
                                            ALU.mult).then_inc(gbh_done, 1)
                    pool.wait_ge(gbh_done, g + 1)
                    nc.gpsimd.tensor_tensor(base[:, t0:t1, :], base[:, t0:t1, :], xs[:, t0:t1, :], ALU.add).then_inc(base_done, 1)

            def gather(e, i):
                nc.gpsimd.tensor_copy(idx_cur[:, i, :], idx_all[:, at(e), :].rearrange("p o c -> p (o c)")).then_inc(idx_copied, 1)
                pool.wait_ge(idx_copied, e + 1)
                pool.sem_inc(passed_pool, 1)
                for c in range(EC):
                    nc.gpsimd.indirect_dma_start(y_sb[:, i, c, :], None, normed,
                                                 bass.IndirectOffsetOnAxis(ap=idx_cur[:, i, c:c + 1], axis=0)).then_inc(gathered[i], 16)

            def emit(e, n, i, ahead, gathers):
                for c in range(EC):
                    pool.wait_ge(o_done, e * EC + (c + 1))
                    pool.sem_inc(passed_pool, 1)
                    nc.gpsimd.indirect_dma_start(out, bass.IndirectOffsetOnAxis(ap=idx_cur[:, i, c:c + 1], axis=0),
                                                 o_sb[:, i, c, :], None, compute_op=ALU.add).then_inc(scattered, 16)
                pool.wait_ge(scattered, e * (16 * EC) + 16 * EC)
                pool.sem_inc(passed_pool, 1)
                if gathers:
                    gather(e + 2, i)

            pool.wait_ge(idx_moved, 16 * (P // LOW))
            pool.wait_ge(st_normed, 16 * G)
            pool.wait_ge(st_scores, 32)
            pool.wait_ge(st_out, 16 * G)
            gather(0, 0)
            gather(1, 1)
            over_experts(pool, emit)


def kernel(L0_attn_x, L0_attn_Wq, L0_attn_Wk, L0_attn_Wv, L0_attn_Wo, L0_attn_bo, L0_attn_w, L0_attn_v,
           L0_ffn_gate_w, L0_ffn_ln_w, L0_ffn_ln_b, L0_ffn_fc1s, L0_ffn_b1s, L0_ffn_fc2s, L0_ffn_b2s, L0_c, L0_wmod):
    import concourse.bacc as bacc
    import numpy as np
    from concourse.bass_utils import run_bass_kernel_spmd

    def a(v):
        return np.asarray(v)

    p = np.arange(P)
    consts = np.zeros((P, C_W), np.float32)
    consts[:, C_ID:C_ID + P] = np.eye(P)
    consts[:, C_DIAG:C_DIAG + P] = np.where(p[:, None] > P - 1 - p[None, :], MASKED, 0.0)
    consts[:, C_FULL:C_FULL + P] = MASKED
    consts[:, C_SAME:C_SAME + P] = p[:, None] % E == p[None, :] % E
    consts[:, C_BELOW:C_BELOW + P] = (p[:, None] % E == p[None, :] % E) & (p[:, None] // E < p[None, :] // E)
    consts[:, C_IOTA:C_IOTA + P] = p[None, :] + 1
    col = np.arange(NT * E)
    consts[:, C_TILE:C_TILE + NT * E] = (2 * (col // E % (NT // 2)) + col // (NT * E // 2))[None, :]
    consts[:, C_ROW:C_ROW + NT * E] = p[:, None]
    arrays = {
        "x": a(L0_attn_x).reshape(TOK, D),
        "c_t": a(L0_c).T,
        "wmod": a(L0_wmod),
        "wq": a(L0_attn_Wq), "wk": a(L0_attn_Wk), "wv": a(L0_attn_Wv), "wo": a(L0_attn_Wo),
        "bo": a(L0_attn_bo).reshape(1, D),
        "dist_w": a(L0_attn_w).reshape(H, 1), "dist_v": a(L0_attn_v).reshape(H, 1),
        "gate_t": a(L0_ffn_gate_w).T,
        "ln_w": a(L0_ffn_ln_w).reshape(KC, P).T, "ln_b": a(L0_ffn_ln_b).reshape(KC, P).T,
        "fc1_t": a(L0_ffn_fc1s).transpose(0, 2, 1),
        "b1": a(L0_ffn_b1s).reshape(E, FC, P).transpose(2, 0, 1).reshape(P, E * FC),
        "fc2_t": a(L0_ffn_fc2s).transpose(0, 2, 1),
        "b2": a(L0_ffn_b2s),
        "consts": consts,
    }
    nc = bacc.Bacc("TRN2", target_bir_lowering=False, num_devices=1)
    arrays = {f"in_{k}": np.ascontiguousarray(v) for k, v in arrays.items()}
    args = [nc.dram_tensor(k, v.shape, mybir.dt.from_np(v.dtype), kind="ExternalInput").ap() for k, v in arrays.items()]
    result = nc.dram_tensor("result", (TOK, D), F32, kind="ExternalOutput").ap()
    adaln_block(nc, *args, result)
    r = run_bass_kernel_spmd(nc, [arrays], core_ids=[0])
    return r.results[0]["result"].reshape(B, N, D)
```

```python
from contextlib import ExitStack

import concourse.bass as bass
from concourse import mybir

F32 = mybir.dt.float32
BF16 = mybir.dt.bfloat16
I32 = mybir.dt.int32
U32 = mybir.dt.uint32
ALU = mybir.AluOpType
ACT = mybir.ActivationFunctionType
AX = mybir.AxisListType

P = 128
B, N, D = 2, 2048, 256
H = 16
HD = D // H
TOK = B * N
NT = TOK // P
BT = N // P
KC = D // P
E = 8
F = 4 * D
FC = F // P
CAP = TOK // E
EC = CAP // P
EPS = 1e-5
NW = D + E
LN_GROUP = 4
NG = NT // LN_GROUP
GW = LN_GROUP * P
RW = N + P
MASKED = -1e30

C_ID, C_DIAG, C_FULL, C_SAME, C_BELOW, C_IOTA, C_TILE, C_ROW = (128 * i for i in range(8))
C_ROW = C_TILE + NT * E
C_W = C_ROW + NT * E


def adaln_block(nc, x, c_t, wmod, wq, wk, wv, wo, bo, dist_w, dist_v, gate_t, ln_w, ln_b,
                fc1_t, b1, fc2_t, b2, consts, out):
    ctx = ExitStack()
    with ctx:
        def sb(name, shape, dt=F32):
            return ctx.enter_context(nc.sbuf_tensor(name, shape, dt))

        def ps(name, shape, dt=F32):
            return ctx.enter_context(nc.psum_tensor(name, shape, dt))

        def dram(name, shape, dt):
            return nc.dram_tensor(name, shape, dt, kind="Internal").ap()

        q_split = dram("q_split", (3, D, TOK), BF16)
        k_split = dram("k_split", (3, D, TOK), BF16)
        factor_rows = dram("factor_rows", (H, RW), F32)
        normed = dram("normed", (TOK, NW), F32)

        region_x = sb("region_x", [P, NT * D])
        region_a = sb("region_a", [P, 8192])
        region_v = sb("region_v", [P, NT * D])
        region_c = sb("region_c", [P, NT * D])
        region_s = sb("region_s", [P, 4096])
        region_t = sb("region_t", [P, 4096])
        region_o = sb("region_o", [P, 4096])
        region_p = sb("region_p", [P, 2048])
        xs = region_x[:, :].rearrange("p (t d) -> p t d", d=D)
        vals = region_v[:, :].rearrange("p (t d) -> p t d", d=D)
        context = region_c[:, :].rearrange("p (t d) -> p t d", d=D)

        ident = sb("ident", [P, P])
        bconst = sb("bconst", [P, C_W], BF16)
        ident_b = bconst[:, C_ID:C_ID + P]
        mask_diag = bconst[:, C_DIAG:C_DIAG + P]
        mask_full = bconst[:, C_FULL:C_FULL + P]
        same_expert = bconst[:, C_SAME:C_SAME + P]
        rows_before = bconst[:, C_BELOW:C_BELOW + P]
        iota_row = bconst[:, C_IOTA:C_IOTA + P]
        tile_of = bconst[:, C_TILE:C_TILE + NT * E]
        row_of = bconst[:, C_ROW:C_ROW + NT * E]
        wo_gated = sb("wo_gated", [P, B, KC, D])
        bo_gated = sb("bo_gated", [P, B, D])
        gates = sb("gates", [P, B, 3, D])
        modt = sb("modt", [P, 4, B])
        gate_sb = sb("gate_sb", [P, KC, E])
        lnw_sb = sb("lnw_sb", [P, KC])
        lnb_sb = sb("lnb_sb", [P, KC])
        b1_sb = sb("b1_sb", [P, E, FC])
        moments = sb("moments", [P, NT, 2])
        rstd = sb("rstd", [P, NT])

        with ExitStack() as st, nc.Block() as block:
            sem = lambda name: st.enter_context(nc.semaphore(name))
            ld_x = [sem(f"ld_x{i}") for i in range(4)]
            ld_c, ld_mod, ld_rows, ld_ident, ld_bo = sem("ld_c"), sem("ld_mod"), sem("ld_rows"), sem("ld_ident"), sem("ld_bo")
            ld_rest, ld_w, ld_dist = sem("ld_rest"), sem("ld_w"), sem("ld_dist")
            silu_exp, silu_done, modt_mm, modt_done = sem("silu_exp"), sem("silu_done"), sem("modt_mm"), sem("modt_done")
            bc_mm, gates_done = sem("bc_mm"), sem("gates_done")
            dist_iota, dist_exp, dist_done = sem("dist_iota"), sem("dist_exp"), sem("dist_done")
            dve_step, var_done, sqrt_done, xn_done = sem("dve_step"), sem("var_done"), sem("sqrt_done"), sem("xn_done")
            xt_mm, ht0_done, ht1_done = sem("xt_mm"), sem("ht0_done"), sem("ht1_done")
            proj_mm, part1, rest1, part2, part3 = sem("proj_mm"), sem("part1"), sem("rest1"), sem("part2"), sem("part3")
            val_mm, val_done, consts_done = sem("val_mm"), sem("val_done"), sem("consts_done")
            st_split, st_dist = [sem(f"st_split{i}") for i in range(4)], sem("st_dist")

            PB, SPLITS = 3, 4
            psum_xt = st.enter_context(nc.psum_tensor("psum_xt", [P, KC, GW], F32))
            psum_proj = st.enter_context(nc.psum_tensor("psum_proj", [P, PB, GW], F32))
            psum_rows = st.enter_context(nc.psum_tensor("psum_rows", [P, 2, D], F32))
            psum_val = st.enter_context(nc.psum_tensor("psum_val", [P, 2, 2, D], F32))
            ht = region_a[:, :].rearrange("p (k t) -> p k t", k=KC)
            w_sb = region_s[:, 0:3 * KC * D].rearrange("p (w k m) -> p w k m", w=3, k=KC)
            wmod_sb = region_c[:, 0:KC * 6 * D].rearrange("p (k m) -> p k m", k=KC)
            xn = region_c[:, 3072:3072 + 8 * D].rearrange("p (t d) -> p t d", d=D)
            rest = region_c[:, 5120:5120 + SPLITS * GW].rearrange("p (i t) -> p i t", i=SPLITS)
            parts = region_t[:, 1024:1024 + SPLITS * 3 * GW // 2].bitcast(BF16).rearrange("p (i s t) -> p i s t", i=SPLITS, s=3)
            const_f = region_o[:, 2304:2304 + C_W]
            DQ = RW // 4
            dist = region_o[:, 0:DQ]
            silu_bc = region_p[:, 0:KC * B * P].rearrange("p (k b m) -> p k b m", k=KC, b=B)
            wo_sb = region_p[:, 512:1024].rearrange("p (k m) -> p k m", k=KC)
            attn_gate = region_p[:, 1024:1536].rearrange("p (b d) -> p b d", b=B)
            cs = st.enter_context(nc.sbuf_tensor("cs", [P, 4, KC, B], F32))
            dw_sb = st.enter_context(nc.sbuf_tensor("dw_sb", [P, 4], F32))
            bo_sb = st.enter_context(nc.sbuf_tensor("bo_sb", [P, D], F32))
            stats = st.enter_context(nc.sbuf_tensor("stats", [P, NT, 6], F32))
            gtmp = region_t[:, 0:2 * B * D].rearrange("p (i b d) -> p i b d", i=2, b=B)
            XQ = NT // 4
            N_REST = 6

            @block.sync
            def _(sp):
                def load_x(i):
                    sp.dma_start(xs[:, i * XQ:(i + 1) * XQ, :],
                                 x[i * XQ * P:(i + 1) * XQ * P, :].rearrange("(t p) d -> p t d", p=P)).then_inc(ld_x[i], 16)

                load_x(0)
                for i, w in enumerate((wq, wk, wv)):
                    sp.dma_start(w_sb[:, i, :, :], w.rearrange("(k p) m -> p k m", p=P)).then_inc(ld_w, 16)
                for i in range(1, 4):
                    load_x(i)
                for u in range(4 * NG):
                    g, which, m = u // 4, (u // 2) % 2, u % 2
                    sp.wait_ge(part3, u + 1)
                    dst = (q_split, k_split)[which]
                    sp.dma_start(dst[:, m * P:(m + 1) * P, g * GW:(g + 1) * GW].rearrange("s p t -> p s t"),
                                 parts[:, u % SPLITS, :, :]).then_inc(st_split[u % SPLITS], 16)
                sp.wait_ge(dist_done, 1)
                for c in range(4):
                    sp.dma_start(factor_rows[:, c * DQ:(c + 1) * DQ], dist[32 * c:32 * c + H, :]).then_inc(st_dist, 16)
                for i in range(SPLITS):
                    sp.wait_ge(st_split[i], 16 * 4 * NG // SPLITS)
                sp.wait_ge(st_dist, 64)

            @block.gpsimd
            def _(pool):
                pool.dma_start(ident[:, :], consts[:, C_ID:C_ID + P]).then_inc(ld_ident, 16)
                for c in range(4):
                    if c:
                        pool.wait_ge(dist_iota, c)
                    nc.gpsimd.iota(dist[32 * c:32 * c + 32, :], [[-1, DQ]], base=N - 1 - c * DQ, channel_multiplier=0,
                                   allow_small_or_imprecise_dtypes=True).then_inc(dist_iota, 1)
                pool.dma_start(const_f, consts).then_inc(ld_rest, 16)
                pool.dma_start(wo_sb, wo.rearrange("(k p) m -> p k m", p=P)).then_inc(ld_rest, 16)
                pool.dma_start(gate_sb[:, :, :], gate_t.rearrange("(k p) e -> p k e", p=P)).then_inc(ld_rest, 16)
                pool.dma_start(lnw_sb[:, :], ln_w).then_inc(ld_rest, 16)
                pool.dma_start(lnb_sb[:, :], ln_b).then_inc(ld_rest, 16)
                pool.dma_start(b1_sb[:, :, :], b1.rearrange("p (e f) -> p e f", e=E)).then_inc(ld_rest, 16)
                pool.wait_ge(ld_rest, 16 * N_REST)
                pool.wait_ge(dist_iota, 4)
                nc.gpsimd.tensor_copy(bconst[:, :], const_f).then_inc(consts_done, 1)
                for u in range(4 * NG):
                    pool.wait_ge(part2, u + 1)
                    nc.gpsimd.tensor_tensor(parts[:, u % SPLITS, 2, :], rest[:, u % SPLITS, :], parts[:, u % SPLITS, 1, :],
                                            ALU.subtract).then_inc(part3, 1)

            def evacuate(act, split, second, g):
                for i in range(4):
                    u = 4 * g + i
                    split(u)
                    if u >= 1:
                        second(u - 1)
                if g == NG - 1:
                    second(4 * NG - 1)
                for i in range(2):
                    act.wait_ge(val_mm, 2 * g + i + 1)
                    nc.scalar.copy(vals[:, 4 * g + 2 * i:4 * g + 2 * i + 2, :], psum_val[:, i, :, :]).then_inc(val_done, 1)

            @block.scalar
            def _(act):
                act.dma_start(cs[:, 0, :, :], c_t.rearrange("(k p) b -> p k b", p=P)).then_inc(ld_c, 16)
                wmod_v = wmod.rearrange("(k p) m -> p k m", p=P)
                act.dma_start(wmod_sb[:, :, 0:2 * D], wmod_v[:, :, 0:2 * D]).then_inc(ld_mod, 16)
                for i, v in enumerate((dist_w, dist_v)):
                    act.dma_start(dw_sb[:, i:i + 1], bass.AP(tensor=v.tensor, offset=v.offset, ap=[[0, P // H], *v.ap])).then_inc(ld_dist, 16)
                act.dma_start(wmod_sb[:, :, 2 * D:], wmod_v[:, :, 2 * D:]).then_inc(ld_rows, 16)
                act.dma_start(bo_sb[:, :], bass.AP(tensor=bo.tensor, offset=bo.offset, ap=[[0, P], [1, D]])).then_inc(ld_bo, 16)
                act.wait_ge(ld_c, 16)
                nc.scalar.activation(cs[:, 1, :, :], cs[:, 0, :, :], ACT.Exp, scale=-1.0).then_inc(silu_exp, 1)
                act.wait_ge(ld_dist, 32)
                nc.scalar.activation(dw_sb[:, 2:3], dw_sb[:, 1:2], ACT.Exp).then_inc(dist_exp, 1)
                act.wait_ge(dist_iota, 5)
                nc.scalar.activation(dist, dist, ACT.Exp, bias=dw_sb[:, 1:2], scale=dw_sb[:, 3:4]).then_inc(dist_exp, 1)

                def deviation(i):
                    act.wait_ge(var_done, i + 1)
                    nc.scalar.activation(rstd[:, i * XQ:(i + 1) * XQ], rstd[:, i * XQ:(i + 1) * XQ],
                                         ACT.Sqrt).then_inc(sqrt_done, 1)

                deviation(0)
                deviation(1)

                def split(u):
                    act.wait_ge(proj_mm, u + 1)
                    if u >= SPLITS:
                        act.wait_ge(st_split[u % SPLITS], 16 * (u // SPLITS))
                    src = psum_proj[:, u % PB, :]
                    if (u // 2) % 2 == 0:
                        src = src.rearrange("p (a b) -> p a b", b=P)[:, :, ::-1]
                    dst = parts[:, u % SPLITS, 0, :]
                    if (u // 2) % 2 == 0:
                        dst = dst.rearrange("p (a b) -> p a b", b=P)
                    nc.scalar.copy(dst, src).then_inc(part1, 1)

                def second(u):
                    act.wait_ge(rest1, u + 1)
                    nc.scalar.copy(parts[:, u % SPLITS, 1, :], rest[:, u % SPLITS, :]).then_inc(part2, 1)

                for g in range(NG):
                    act.wait_ge(xt_mm, 2 * g + 1)
                    act.wait_ge(modt_done, 1)
                    nc.scalar.activation(ht[:, 0, g * GW:(g + 1) * GW], psum_xt[:, 0, :], ACT.Identity,
                                         bias=modt[:, 0, g // (NG // B):g // (NG // B) + 1],
                                         scale=modt[:, 2, g // (NG // B):g // (NG // B) + 1]).then_inc(ht0_done, 1)
                    if g >= 1:
                        evacuate(act, split, second, g - 1)
                    if g in (1, 3):
                        deviation((g + 3) // 2)
                evacuate(act, split, second, NG - 1)

            @block.vector
            def _(dve):
                steps = [0]

                def step(ins):
                    steps[0] += 1
                    ins.then_inc(dve_step, 1)
                    dve.wait_ge(dve_step, steps[0])

                dve.wait_ge(silu_exp, 1)
                step(nc.vector.tensor_scalar_add(cs[:, 2, :, :], cs[:, 1, :, :], 1.0))
                step(nc.vector.reciprocal(cs[:, 3, :, :], cs[:, 2, :, :]))
                step(nc.vector.tensor_tensor(cs[:, 1, :, :], cs[:, 0, :, :], cs[:, 3, :, :], ALU.mult))
                nc.vector.tensor_copy(silu_bc, cs[:, 1, :, :].unsqueeze(3).to_broadcast([P, KC, B, P])).then_inc(silu_done, 1)
                dve.wait_ge(ld_dist, 32)
                step(nc.vector.tensor_scalar(dw_sb[:, 3:4], dw_sb[:, 0:1], -1.0, None, ALU.mult))
                dve.wait_ge(dist_iota, 4)
                nc.vector.tensor_scalar(dist, dist, 0.0, None, ALU.max).then_inc(dist_iota, 1)

                def norm_group(i):
                    dve.wait_ge(ld_x[i], 16)
                    for t in range(i * XQ, (i + 1) * XQ):
                        last = nc.vector.bn_stats(stats[:, t, :], xs[:, t, :])
                    step(last)
                    for t in range(i * XQ, (i + 1) * XQ):
                        last = nc.vector.bn_aggr(moments[:, t, :], stats[:, t, :])
                    step(last)
                    nc.vector.tensor_scalar_add(rstd[:, i * XQ:(i + 1) * XQ], moments[:, i * XQ:(i + 1) * XQ, 1],
                                                EPS).then_inc(var_done, 1)

                def normed_tiles(g):
                    i = g * LN_GROUP // XQ
                    if g * LN_GROUP % XQ == 0:
                        dve.wait_ge(sqrt_done, i + 1)
                        step(nc.vector.reciprocal(rstd[:, i * XQ:(i + 1) * XQ], rstd[:, i * XQ:(i + 1) * XQ]))
                    if g >= 2:
                        dve.wait_ge(xt_mm, 2 * g - 2)
                    for t in range(g * LN_GROUP, (g + 1) * LN_GROUP):
                        last = nc.vector.tensor_scalar(xn[:, t % 8, :], xs[:, t, :], moments[:, t, 0:1], rstd[:, t:t + 1],
                                                       ALU.subtract, ALU.mult)
                    last.then_inc(xn_done, 1)

                def transposed(g):
                    dve.wait_ge(xt_mm, 2 * g + 2)
                    nc.vector.tensor_scalar(ht[:, 1, g * GW:(g + 1) * GW], psum_xt[:, 1, :],
                                            modt[:, 3, g // (NG // B):g // (NG // B) + 1],
                                            modt[:, 1, g // (NG // B):g // (NG // B) + 1], ALU.mult, ALU.add).then_inc(ht1_done, 1)

                def remainder(u):
                    dve.wait_ge(part1, u + 1)
                    if u >= SPLITS:
                        dve.wait_ge(part3, u - SPLITS + 1)
                    a, b_, c_ = rest[:, u % SPLITS, :], psum_proj[:, u % PB, :], parts[:, u % SPLITS, 0, :]
                    if (u // 2) % 2 == 0:
                        a, b_, c_ = (v.rearrange("p (a b) -> p a b", b=P) for v in (a, b_, c_))
                        b_ = b_[:, :, ::-1]
                    nc.vector.tensor_tensor(a, b_, c_, ALU.subtract).then_inc(rest1, 1)

                def factors():
                    dve.wait_ge(dist_exp, 2)
                    step(nc.vector.tensor_scalar(dw_sb[:, 2:3], dw_sb[:, 2:3], 1.0, 1.0 / HD ** 0.5, ALU.add, ALU.mult))
                    step(nc.vector.tensor_scalar_add(dist, dist, 1.0))
                    step(nc.vector.reciprocal(dist, dist))
                    step(nc.vector.tensor_scalar(dist, dist, dw_sb[:, 2:3], None, ALU.mult))
                    nc.vector.memset(dist[96:P, N - 3 * DQ:DQ], 0.0).then_inc(dist_done, 1)

                def gate_rows(n):
                    b, i = n // 2, n % 2
                    dve.wait_ge(bc_mm, n + 1)
                    raw = psum_rows[:, i, :]
                    nc.vector.tensor_scalar(gtmp[:, 0, b, :], raw, 0.0, 2.0, ALU.is_ge, ALU.mult)
                    step(nc.vector.tensor_scalar(gtmp[:, 1, b, :], raw, -1.0, 0.25, ALU.mult, ALU.max))
                    step(nc.vector.tensor_tensor(gtmp[:, 1, b, :], gtmp[:, 1, b, :], raw, ALU.max))
                    if i == 0:
                        nc.vector.tensor_copy(gates[:, b, 0, :], psum_rows[:, 1, :]).then_inc(gates_done, 1)
                    else:
                        nc.vector.tensor_scalar_add(gates[:, b, 1, :], psum_rows[:, 0, :], 1.0).then_inc(gates_done, 1)
                    dst = gates[:, b, 2, :] if i else attn_gate[:, b, :]
                    step(nc.vector.scalar_tensor_tensor(dst, gtmp[:, 0, b, :], -1.0, gtmp[:, 1, b, :], ALU.add, ALU.mult))
                    if i == 0:
                        dve.wait_ge(ld_rest, 16 * N_REST)
                        dve.wait_ge(ld_bo, 16)
                        for k in range(KC):
                            nc.vector.tensor_tensor(wo_gated[:, b, k, :], wo_sb[:, k, :], attn_gate[:, b, :], ALU.mult)
                        nc.vector.tensor_tensor(bo_gated[:, b, :], bo_sb[:, :], attn_gate[:, b, :], ALU.mult)

                norm_group(0)
                dve.wait_ge(modt_mm, 1)
                step(nc.vector.tensor_copy(modt[:, :, :], psum_val[:, 0, 0, 0:8].rearrange("p (m b) -> p m b", b=B)))
                nc.vector.tensor_scalar_add(modt[:, 2:4, :], modt[:, 2:4, :], 1.0).then_inc(modt_done, 1)
                normed_tiles(0)
                normed_tiles(1)
                norm_group(1)
                for g in range(NG):
                    transposed(g)
                    if g + 2 < NG:
                        normed_tiles(g + 2)
                    if g >= 1:
                        for u in range(4 * g - 4, 4 * g):
                            remainder(u)
                    if g in (1, 3):
                        norm_group((g + 3) // 2)
                    if g == 1:
                        factors()
                    if 2 <= g < 2 + 2 * B:
                        gate_rows(g - 2)
                for u in range(4 * NG - 4, 4 * NG):
                    remainder(u)

            @block.tensor
            def _(pe):
                pe.wait_ge(ld_mod, 16)
                pe.wait_ge(silu_done, 1)
                for m in range(4):
                    for k in range(KC):
                        last = nc.tensor.matmul(psum_val[:, 0, 0, 2 * m:2 * m + 2], wmod_sb[:, k, m * P:(m + 1) * P],
                                                cs[:, 1, k, :], start=(k == 0), stop=(k == KC - 1))
                last.then_inc(modt_mm, 1)
                pe.wait_ge(ld_ident, 16)

                def mod_rows(n):
                    b, i = n // 2, n % 2
                    if n:
                        pe.wait_ge(gates_done, n)
                    else:
                        pe.wait_ge(ld_rows, 16)
                    for k in range(KC):
                        last = nc.tensor.matmul(psum_rows[:, :, :].rearrange("p i d -> p (i d)"), silu_bc[:, k, b, :],
                                                wmod_sb[:, k, 2 * D + i * GW:2 * D + (i + 1) * GW], start=(k == 0), stop=(k == KC - 1))
                    last.then_inc(bc_mm, 1)

                def transpose_group(g):
                    pe.wait_ge(xn_done, g + 1)
                    if g >= 1:
                        pe.wait_ge(ht0_done, g)
                        pe.wait_ge(ht1_done, g)
                    for k in range(KC):
                        for i in range(LN_GROUP):
                            last = nc.tensor.transpose(psum_xt[:, k, i * P:(i + 1) * P],
                                                       xn[:, (g * LN_GROUP + i) % 8, k * P:(k + 1) * P], ident[:, :])
                        last.then_inc(xt_mm, 1)

                transpose_group(0)
                pe.wait_ge(ld_w, 48)
                for g in range(NG):
                    if g + 1 < NG:
                        transpose_group(g + 1)
                    pe.wait_ge(ht0_done, g + 1)
                    pe.wait_ge(ht1_done, g + 1)
                    for i in range(4):
                        u = 4 * g + i
                        if u >= PB:
                            pe.wait_ge(rest1, u - PB + 1)
                        for k in range(KC):
                            last = nc.tensor.matmul(psum_proj[:, u % PB, :], w_sb[:, i // 2, k, (i % 2) * P:(i % 2 + 1) * P],
                                                    ht[:, k, g * GW:(g + 1) * GW], start=(k == 0), stop=(k == KC - 1))
                        last.then_inc(proj_mm, 1)
                    for i in range(2):
                        if g >= 1:
                            pe.wait_ge(val_done, 2 * g + i - 1)
                        for j in range(2):
                            t = 4 * g + 2 * i + j
                            for k in range(KC):
                                last = nc.tensor.matmul(psum_val[:, i, j, :], ht[:, k, t * P:(t + 1) * P],
                                                        w_sb[:, 2, k, :], start=(k == 0), stop=(k == KC - 1))
                        last.then_inc(val_mm, 1)
                    if 1 <= g < 1 + 2 * B:
                        mod_rows(g - 1)

        attention(nc, locals())
        mixture(nc, locals())


def attention(nc, o):
    region_a, region_s, region_t, region_o, region_p = (o[k] for k in ("region_a", "region_s", "region_t", "region_o", "region_p"))
    vals, context, ident, ident_b = o["vals"], o["context"], o["ident"], o["ident_b"]
    mask_diag, mask_full = o["mask_diag"], o["mask_full"]
    q_split, k_split, factor_rows = o["q_split"], o["k_split"], o["factor_rows"]

    VW = 32
    NP = BT // 2
    SB, SW = 4, 512
    stacks = region_s[:, :].bitcast(BF16).rearrange("p (b w t) -> p b w t", b=B, w=2)
    factors = region_t[:, :].rearrange("p (b t) -> p b t", b=B)
    rows = [r[:, q * 4096:(q + 1) * 4096].rearrange("p (w t) -> p w t", w=2)
            for r in (region_a, o["region_x"]) for q in range(2)]
    LEAD = 3
    sums = region_o[:, :].rearrange("p (b t) -> p b t", b=B)
    weights = region_p[:, :].rearrange("p (i t) -> p i t", i=4)

    CUT = [0, 0, 0, 0, 0, 2, 2, 4, 4, 4, 4, 5, 6, 6, 7, 8, 8]

    def cut(nb):
        return CUT[nb]

    def pieces(lo, hi):
        count = -(-(hi - lo) // (SW // P))
        return [(lo + (hi - lo) * m // count, lo + (hi - lo) * (m + 1) // count) for m in range(count)]

    order = [m for i in range(NP // 2) for m in (NP - 1 - i, i)]
    pairs = [(b, i) for b in range(B) for i in order]
    tiles = [(b, i, w) for b, i in pairs for w in range(2)]
    slots = []
    for n, (b, i, w) in enumerate(tiles):
        nb = 2 * i + w + 1
        on_dve = [(n, False, lo, hi) for lo, hi in pieces(cut(nb), nb)]
        on_act = [(n, True, lo, hi) for lo, hi in pieces(0, cut(nb))]
        while on_dve or on_act:
            slots += on_dve[:1] + on_act[:1]
            on_dve, on_act = on_dve[1:], on_act[1:]
    NS = len(slots)
    NY = sum(not s[1] for s in slots)
    NX = sum(s[1] for s in slots)
    NTL = len(tiles)
    NPR = len(pairs)
    blocks = [(g, k) for g, (b, i) in enumerate(pairs) for k in range(i + 1)]
    NB = len(blocks)
    PV_LAG = 2
    NC = 4 * B
    LOADS = 7 * 16
    assert NS % SB == 0 and NB % 4 == 0 and NPR % len(rows) == 0
    on_dve = [[s for s in range(NS) if slots[s][0] == n and not slots[s][1]] for n in range(NTL)]
    on_act = [[s for s in range(NS) if slots[s][0] == n and slots[s][1]] for n in range(NTL)]
    x_to = [sum(slots[r][1] for r in range(s + 1)) for s in range(NS)]
    y_to = [s + 1 - x_to[s] for s in range(NS)]
    first_of = [min(s for s in range(NS) if tiles[slots[s][0]][0] == b) for b in range(B)]
    last_of = [max(s for s in range(NS) if tiles[slots[s][0]][0] == b) for b in range(B)]
    blocks_to = [sum(1 for gg, _ in blocks if gg <= g) for g in range(NPR)]
    x_tiles_to = [sum(1 for m in range(n + 1) if on_act[m]) for n in range(NTL)]
    NXT = x_tiles_to[-1]

    with ExitStack() as st, nc.Block() as block:
        sem = lambda name: st.enter_context(nc.semaphore(name))
        loaded = [sem("loaded0"), sem("loaded1")]
        score_done, relu_done = sem("score_done"), sem("relu_done")
        scaled_y, scaled_x = sem("scaled_y"), sem("scaled_x")
        shifted, shifted_x, negated = sem("shifted"), sem("shifted_x"), sem("negated")
        turned, exp_done, pv_done, pv_saved = sem("turned"), sem("exp_done"), sem("pv_done"), sem("pv_saved")
        back_done, summed, recip_done, cleared = sem("back_done"), sem("summed"), sem("recip_done"), sem("cleared")
        values_done = [sem("values_done0"), sem("values_done1")]
        passed, passed_pool, passed_sp = sem("passed"), sem("passed_pool"), sem("passed_sp")
        score_ps = st.enter_context(nc.psum_tensor("score_ps", [P, SB, SW], F32))
        turn_ps = st.enter_context(nc.psum_tensor("turn_ps", [P, 2, 2, 2, P], F32))
        pv_ps = st.enter_context(nc.psum_tensor("pv_ps", [P, 2, 2 * P], F32))
        back_ps = st.enter_context(nc.psum_tensor("back_ps", [P, 4, P], F32))
        vblock = st.enter_context(nc.sbuf_tensor("vblock", [P, B, BT, VW], F32))
        maxima = st.enter_context(nc.sbuf_tensor("maxima", [P, 5, NTL], F32))
        csum = st.enter_context(nc.sbuf_tensor("csum", [P, B, BT, HD + 1], F32))
        crec = st.enter_context(nc.sbuf_tensor("crec", [P, B, BT], F32))

        FREE_SCALED, FREE_RELU, FREE_PV, FREE_BLOCKS, FREE_PAIRS, FREE_BACK = NY, NX, 4 + NB, 2 + NB, 2 + NPR, 1 + NC

        def block_range(n):
            nb = 2 * tiles[n][1] + tiles[n][2] + 1
            return cut(nb), nb

        s_of_pair = [[s for s in range(NS) if slots[s][0] // 2 == g] for g in range(NPR)]
        lead_in = [("score", s, 0) for g in range(LEAD) for s in s_of_pair[g]]
        program = []
        n = 0
        for g in range(NPR):
            count = pairs[g][1] + 1
            ahead = [("score", s, (g + LEAD) // NPR) for s in s_of_pair[(g + LEAD) % NPR]]
            for k in range(count):
                program.append(("turn", n + k, 0))
                program += ahead[len(ahead) * k // count:len(ahead) * (k + 1) // count]
                if n + k >= PV_LAG:
                    program.append(("pv", n + k - PV_LAG, 0))
                if k == min(4, count - 1) and g >= 2 and g % 2 == 0:
                    program.append(("back", g // 2 - 1, 0))
                if k == PV_LAG and g == 0:
                    program.append(("values", 1, 0))
                if k == PV_LAG and g == NPR // 2:
                    program.append(("values", 0, 1))
            n += count
        program += [("pv", j, 0) for j in range(NB - PV_LAG, NB)]
        program.append(("back", NC - 1, 0))

        def tile_steps(m):
            steps = []
            mine = [("slot", s, m // NTL) for s in on_dve[m % NTL]]
            other = [("slot", s, (m - 1) // NTL) for s in on_act[(m - 1) % NTL]] if m >= 1 else []
            while mine or other:
                steps += mine[:1] + other[:1]
                mine, other = mine[1:], other[1:]
            return steps + ([("shift", (m - 2) % NTL, (m - 2) // NTL)] if m >= 2 else [])

        lead_in_tiles = [step for m in range(2 * LEAD) for step in tile_steps(m)]
        tile_program = []
        for m in range(2 * LEAD, NTL + 2 * LEAD):
            g = m // 2
            if m % 2 == 0 and g % 2 and g >= 2 * LEAD + 1 and (g - 2 * LEAD - 1) // 2 < NC - 2:
                tile_program.append(("back", (g - 2 * LEAD - 1) // 2, 0))
            if m == NTL // 2 + 2 * (2 * LEAD):
                tile_program.append(("divide", 0, 0))
            tile_program += tile_steps(m)
        tile_program += [("back", NC - 2, 0), ("back", NC - 1, 0), ("divide", 1, 0)]

        def row_free(g):
            return FREE_BLOCKS + (blocks_to[g - 4] if g >= 4 else blocks_to[g - 4] - NB)

        def top(n):
            place = len(on_dve[n]) + len(on_act[n]) - 1
            return maxima[:, place, n:n + 1]

        def wait_scaled(eng, n, h):
            if on_act[n]:
                eng.wait_ge(scaled_x, h * NX + x_to[on_act[n][-1]])
            else:
                eng.wait_ge(scaled_y, h * NY + (FREE_SCALED + y_to[on_dve[n][-1]]))

        def over_heads(eng, emit, first, body):
            for what, j, _ in first:
                emit(what, j, 0)
            with eng.Fori(0, H - 1) as h:
                for what, j, later in body:
                    emit(what, j, h + later)
            for what, j, later in body:
                if not later:
                    emit(what, j, H - 1)

        @block.sync
        def _(sp):
            def load(h, b):
                t0 = b * N
                for first, s, copies in ((0, 0, 3), (3, 1, 3), (6, 2, 2)):
                    src = q_split[s, bass.ds(h * HD, HD), t0:t0 + N]
                    src = bass.AP(tensor=src.tensor, offset=src.offset, ap=[[0, copies], *src.ap])
                    sp.dma_start(stacks[first * HD:(first + copies) * HD, b, 0, :], src).then_inc(loaded[b], 16)
                for first, count in ((0, 3), (3, 3), (6, 2)):
                    src = k_split[0:count, bass.ds(h * HD, HD), t0:t0 + N]
                    sp.dma_start(stacks[first * HD:(first + count) * HD, b, 1, :], src).then_inc(loaded[b], 16)
                src = factor_rows[bass.ds(h, 1), 0:N]
                sp.dma_start(factors[:, b, :], bass.AP(tensor=src.tensor, offset=src.offset, ap=[[1, P], [1, N]])).then_inc(loaded[b], 16)

            for b in range(B):
                load(0, b)
            with sp.Fori(0, H - 1) as h:
                for b in range(B):
                    sp.wait_ge(scaled_y, h * NY + (FREE_SCALED + y_to[last_of[b]]))
                    sp.sem_inc(passed_sp, 1)
                    sp.wait_ge(scaled_x, h * NX + x_to[last_of[b]])
                    sp.sem_inc(passed_sp, 1)
                    load(h + 1, b)

        @block.tensor
        def _(pe):
            pe.sem_inc(pv_done, FREE_PV)

            def emit(what, j, h):
                if what == "score":
                    n, on_act, lo, hi = slots[j]
                    b, i, w = tiles[n]
                    if j == first_of[b]:
                        pe.wait_ge(loaded[b], h * LOADS + LOADS)
                    before = (j - SB) % NS
                    if slots[before][1]:
                        pe.wait_ge(relu_done, h * NX + (FREE_RELU + x_to[before] - (0 if j >= SB else NX)))
                    else:
                        pe.wait_ge(scaled_y, h * NY + (FREE_SCALED + y_to[before] - (0 if j >= SB else NY)))
                    q0 = (2 * i + w) * P
                    nc.tensor.matmul(score_ps[:, j % SB, 0:(hi - lo) * P], stacks[:, b, 0, q0:q0 + P],
                                     stacks[:, b, 1, lo * P:hi * P], start=True, stop=True).then_inc(score_done, 1)
                elif what == "turn":
                    g, k = blocks[j]
                    b, i = pairs[g]
                    if k == 0:
                        pe.wait_ge(shifted, h * NTL + (2 * g + 2))
                        if x_tiles_to[2 * g + 1] > (x_tiles_to[2 * g - 1] if g else 0):
                            pe.wait_ge(shifted_x, h * NXT + x_tiles_to[2 * g + 1])
                    pe.wait_ge(exp_done, h * NB + (FREE_BLOCKS + j - 1))
                    for a in range(2):
                        for w in range(2):
                            kb = 2 * k + a
                            dst = turn_ps[:, j % 2, a, w, :]
                            diagonal = kb == 2 * i + w
                            if kb > 2 * i + w:
                                last = nc.tensor.matmul(dst, ident_b, mask_full, start=True, stop=True)
                                continue
                            last = nc.tensor.matmul(dst, rows[g % 4][:, w, kb * P:(kb + 1) * P], ident[:, :],
                                                    is_transpose=True, start=True, stop=not diagonal)
                            if diagonal:
                                last = nc.tensor.matmul(dst, ident_b, mask_diag, start=False, stop=True)
                    last.then_inc(turned, 1)
                elif what == "pv":
                    g, k = blocks[j]
                    b, i = pairs[g]
                    if k == 0:
                        pe.wait_ge(pv_saved, h * NPR + (FREE_PAIRS + g))
                        if i == NP - 1:
                            pe.wait_ge(values_done[b], h + 1)
                    pe.wait_ge(exp_done, h * NB + (FREE_BLOCKS + j + 1))
                    for a in range(2):
                        kb = 2 * k + a
                        c = 32 * (kb % 4)
                        last = nc.tensor.matmul(pv_ps[c:c + VW, g % 2, :], vblock[:, b, kb, :],
                                                weights[:, j % 4, a * 2 * P:(a + 1) * 2 * P],
                                                start=(kb < 4), stop=(kb + 4 > 2 * i + 1))
                    last.then_inc(pv_done, 1)
                elif what == "back":
                    b, c = j // 4, j % 4
                    pe.wait_ge(pv_saved, h * NPR + (FREE_PAIRS + 2 * j + 2))
                    pe.wait_ge(summed, h * NC + (FREE_BACK + j))
                    for q in range(4):
                        qt = 4 * c + q
                        last = nc.tensor.transpose(back_ps[:, q, :], sums[:, b, qt * P:(qt + 1) * P], ident[:, :])
                    last.then_inc(back_done, 1)

            over_heads(pe, emit, lead_in, program)

        @block.scalar
        def _(act):
            act.sem_inc(exp_done, FREE_BLOCKS)
            act.sem_inc(pv_saved, FREE_PAIRS)
            act.sem_inc(relu_done, FREE_RELU)
            act.wait_ge(cleared, 3)

            def emit(what, j, h):
                if what == "values":
                    act.wait_ge(pv_done, h * NB + (FREE_PV - NB + NB // B * (j + 1)))
                    nc.scalar.copy(vblock[:, j, :, 0:HD], vals[:, j * BT:(j + 1) * BT, bass.ds(h * HD, HD)]).then_inc(values_done[j], 1)
                elif what == "score" and slots[j][1]:
                    n, _, lo, hi = slots[j]
                    g = n // 2
                    act.wait_ge(score_done, h * NS + (j + 1))
                    act.wait_ge(exp_done, h * NB + row_free(g))
                    nc.scalar.activation(rows[g % 4][:, n % 2, lo * P:hi * P], score_ps[:, j % SB, 0:(hi - lo) * P],
                                         ACT.Relu).then_inc(relu_done, 1)
                elif what == "turn":
                    act.wait_ge(turned, h * NB + (j + 1))
                    act.wait_ge(pv_done, h * NB + (FREE_PV + j - 3))
                    nc.scalar.activation(weights[:, j % 4, :], turn_ps[:, j % 2, :, :, :].rearrange("p a w t -> p (a w t)"),
                                         ACT.Exp).then_inc(exp_done, 1)
                elif what == "pv":
                    g, k = blocks[j]
                    b, i = pairs[g]
                    if k == i:
                        act.wait_ge(pv_done, h * NB + (FREE_PV + j + 1))
                        act.wait_ge(summed, h * NC + (FREE_BACK + 4 * b + 4 - NC))
                        used = P if i else P // 2
                        nc.scalar.copy(sums[0:used, b, 2 * (g % NP) * P:(2 * (g % NP) + 2) * P].rearrange("p (w t) -> p w t", w=2),
                                       pv_ps[0:used, g % 2, :].rearrange("p (w t) -> p w t", w=2)[:, :, ::-1]).then_inc(pv_saved, 1)

            over_heads(act, emit, [("values", 0, 0)] + lead_in, program)

        @block.vector
        def _(dve):
            dve.sem_inc(scaled_y, FREE_SCALED)
            dve.sem_inc(summed, FREE_BACK)
            nc.vector.memset(sums, 0.0).then_inc(cleared, 1)
            nc.vector.memset(vblock[:, :, :, :], 0.0).then_inc(cleared, 1)
            dve.wait_ge(cleared, 2)
            nc.vector.memset(vblock[:, :, :, HD:HD + 1], 1.0).then_inc(cleared, 1)

            def scale(s, h):
                n, act_s, lo, hi = slots[s]
                b, i, w = tiles[n]
                g = n // 2
                if s == first_of[b]:
                    dve.wait_ge(loaded[b], h * LOADS + LOADS)
                row = rows[g % 4][:, w, lo * P:hi * P]
                u0 = N - P - (2 * i + w) * P + lo * P
                earlier = on_dve[n] + on_act[n]
                place = earlier.index(s)
                start = maxima[:, place - 1, n:n + 1] if place else 0.0
                if place > len(on_dve[n]):
                    dve.wait_ge(scaled_x, h * NX + x_to[s] - 1)
                elif place:
                    dve.wait_ge(scaled_y, h * NY + (FREE_SCALED + y_to[earlier[place - 1]]))
                if act_s:
                    dve.wait_ge(relu_done, h * NX + (FREE_RELU + x_to[s]))
                    src = row
                else:
                    dve.wait_ge(exp_done, h * NB + row_free(g))
                    dve.wait_ge(score_done, h * NS + (s + 1))
                    src = score_ps[:, s % SB, 0:(hi - lo) * P]
                dve.sem_inc(passed, 1)
                nc.vector.tensor_tensor_reduce(out=row, in0=src, in1=factors[:, b, u0:u0 + (hi - lo) * P], scale=1.0,
                                               scalar=start, op0=ALU.mult, op1=ALU.max,
                                               accum_out=maxima[:, place, n:n + 1]).then_inc(scaled_x if act_s else scaled_y, 1)

            def shift(n, h):
                b, i, w = tiles[n]
                lo, hi = block_range(n)
                wait_scaled(dve, n, h)
                row = rows[(n // 2) % 4][:, w, lo * P:hi * P]
                nc.vector.tensor_scalar(row, row, 0.0, top(n), ALU.max, ALU.subtract).then_inc(shifted, 1)

            def emit(what, j, h):
                if what == "slot":
                    scale(j, h)
                elif what == "shift":
                    shift(j, h)
                elif what == "back":
                    b, c = j // 4, j % 4
                    dve.wait_ge(back_done, h * NC + (j + 1))
                    nc.vector.tensor_reduce(csum[:, b, 4 * c:4 * c + 4, :],
                                            back_ps[:, :, :].rearrange("p q (j r) -> p q r j", r=VW)[:, :, 0:HD + 1, :],
                                            AX.X, ALU.add).then_inc(summed, 1)
                else:
                    b = j
                    dve.wait_ge(summed, h * NC + (FREE_BACK + 4 * b + 4))
                    nc.vector.reciprocal(crec[:, b, :], csum[:, b, :, HD]).then_inc(recip_done, 1)
                    dve.wait_ge(recip_done, h * B + (b + 1))
                    ordered = [v.rearrange("p (m r w) d -> p r m w d", r=2, w=2)
                               for v in (csum[:, b, :, 0:HD], crec[:, b, :].unsqueeze(2).to_broadcast([P, BT, HD]))]
                    for r in range(2):
                        t0 = b * BT + (1 - r) * BT // 2
                        dst = context[:, t0:t0 + BT // 2, bass.ds(h * HD, HD)].rearrange("p (m w) d -> p m w d", w=2)
                        parts = [v[:, r] if r else v[:, r, ::-1] for v in ordered]
                        nc.vector.tensor_tensor(dst, *parts, ALU.mult)

            over_heads(dve, emit, lead_in_tiles, tile_program)

        @block.gpsimd
        def _(pool):
            def emit(what, n, h):
                if what != "shift" or not block_range(n)[0]:
                    return
                lo, hi = block_range(n)
                wait_scaled(pool, n, h)
                pool.sem_inc(passed_pool, 1)
                nc.gpsimd.tensor_scalar(maxima[:, 4, n:n + 1], top(n), -1.0, 0.0, ALU.mult, ALU.add).then_inc(negated, 1)
                pool.wait_ge(negated, h * NXT + x_tiles_to[n])
                pool.sem_inc(passed_pool, 1)
                row = rows[(n // 2) % 4][:, n % 2, 0:lo * P]
                nc.gpsimd.tensor_scalar(row, row, maxima[:, 4, n:n + 1], 1.0, ALU.add, ALU.mult).then_inc(shifted_x, 1)

            over_heads(pool, emit, lead_in_tiles, tile_program)


def mixture(nc, o):
    g_ = lambda *names: [o[k] for k in names]
    x, out, normed, fc1_t, fc2_t, b2 = g_("x", "out", "normed", "fc1_t", "fc2_t", "b2")
    xs, context, ident, gates, gate_sb = g_("xs", "context", "ident", "gates", "gate_sb")
    wo_gated, bo_gated, lnw_sb, lnb_sb, b1_sb = g_("wo_gated", "bo_gated", "lnw_sb", "lnb_sb", "b1_sb")
    same_expert, rows_before, tile_of, row_of, iota_row = g_("same_expert", "rows_before", "tile_of", "row_of", "iota_row")
    region_a, region_v, region_s, region_t, region_o, region_p, region_x = g_(
        "region_a", "region_v", "region_s", "region_t", "region_o", "region_p", "region_x")

    GT = 4
    G = NT // GT
    GB = G // B
    T2 = NT // 2
    COLS = NT * E
    LOW = 32
    HIGH = CAP // LOW
    BITS = 30

    with ExitStack() as st, nc.Block() as block:
        sem = lambda name: st.enter_context(nc.semaphore(name))
        ld_x = [sem(f"ld_x2_{i}") for i in range(4)]
        xb_done, ctx_turned, ctxt_done, proj_done = sem("xb_done"), sem("ctx_turned"), sem("ctxt_done"), sem("proj_done")
        x2_done, rstd1_done, z_done, h2_done, rstd2_done = sem("x2_done"), sem("rstd1_done"), sem("z_done"), sem("h2_done"), sem("rstd2_done")
        h2_turned, h2t_done, gate_mm, gate_saved, gate_back, logits_done = (
            sem("h2_turned"), sem("h2t_done"), sem("gate_mm"), sem("gate_saved"), sem("gate_back"), sem("logits_done"))
        gbh_done, base_done, normed_done = sem("gbh_done"), sem("base_done"), sem("normed_done")
        st_out, st_normed, st_scores = sem("st_out"), sem("st_normed"), sem("st_scores")
        dve_step, cleared = sem("dve_step2"), sem("cleared2")
        centred, exped, scores_done, scores_turned = sem("centred"), sem("exped"), sem("scores_done"), sem("scores_turned")
        counted, totalled, places_done, places_turned = sem("counted"), sem("totalled"), sem("places_done"), sem("places_turned")
        onehot_done, tokens_mm, tokens_done, idx_moved = sem("onehot_done"), sem("tokens_mm"), sem("tokens_done"), sem("idx_moved")
        ld_weights, gathered = [sem("ld_weights0"), sem("ld_weights1")], [sem("gathered0"), sem("gathered1")]
        idx_copied, y_turned, yt_done = sem("idx_copied"), sem("y_turned"), sem("yt_done")
        fc1_mm, gelu_done, fc2_mm, o_done, scattered = sem("fc1_mm"), sem("gelu_done"), sem("fc2_mm"), sem("o_done"), sem("scattered")
        sum_done, kept_done, gw_step, bits_set = sem("sum_done"), sem("kept_done"), sem("gw_step"), sem("bits_set")
        var_done, sqrt_done = [sem("var1_done"), sem("var2_done")], [sem("sqrt1_done"), sem("sqrt2_done")]
        passed_pool = sem("passed_pool2")

        bank = [st.enter_context(nc.psum_tensor(f"bank{i}", [P, 512], F32)) for i in range(8)]
        ctx_ps, h2_ps, gate_ps, small_ps = bank[0:2], bank[2:4], bank[6], bank[7]
        proj_ps = [bank[4 + i][:, :].rearrange("p (t d) -> p t d", d=D) for i in range(2)]
        y_ps, fc1_ps, fc2_ps = bank[0:2], bank[2:4], bank[4:6]

        ctxt = region_s[:, 0:2048].rearrange("p (i k t) -> p i k t", i=2, k=KC)
        h2t = region_s[:, 2048:4096].rearrange("p (i k t) -> p i k t", i=2, k=KC)
        h2 = region_a[:, :].rearrange("p (t d) -> p t d", d=D)
        base = region_v[:, :].rearrange("p (t d) -> p t d", d=D)
        nrm = context
        stats = region_t[:, 0:NT * 6].rearrange("p (t s) -> p t s", s=6)
        mom = region_t[:, 192:192 + 2 * NT * 2].rearrange("p (l t s) -> p l t s", l=2, s=2)
        rst = region_t[:, 320:320 + 2 * NT].rearrange("p (l t) -> p l t", l=2)
        nmr = region_t[:, 384:384 + 2 * NT].rearrange("p (l t) -> p l t", l=2)
        gate_t_sb = region_t[:, 512:512 + 2 * P].rearrange("p (i t) -> p i t", i=2)
        scores = region_t[:, 1024:1024 + COLS].rearrange("p (h t e) -> p h t e", h=2, e=E)
        row_stat = region_t[:, 1280:1280 + 2 * NT].rearrange("p (i t) -> p i t", i=2)

        def tokens(i):
            return region_p[:, i * 256:(i + 1) * 256]
        scores_t, above, equal, chosen, run, zeros, trash = (tokens(i) for i in range(7))
        found = st.enter_context(nc.sbuf_tensor("found", [P, 4], I32))
        bits = st.enter_context(nc.sbuf_tensor("bits", [P, BITS], I32))
        count_b = st.enter_context(nc.sbuf_tensor("count_b", [P, 4], BF16))
        count_f = st.enter_context(nc.sbuf_tensor("count_f", [P, 4], F32))
        high = region_t[:, 1536:1536 + COLS // 2].bitcast(BF16)
        low = region_t[:, 1664:1664 + COLS // 2].bitcast(BF16)
        place_i = region_p[:, 0:3 * COLS].bitcast(I32).rearrange("p (i c) -> p i c", i=3)
        high_hot = region_t[:, 2048:4096].bitcast(BF16).rearrange("p (c r) -> p c r", r=HIGH)
        low_hot = region_o[:, :].bitcast(BF16).rearrange("p (c r) -> p c r", r=LOW)
        token_of = region_s[:, :].bitcast(BF16).rearrange("p (s c r) -> p s c r", r=HIGH, s=2)
        idx_low = st.enter_context(nc.sbuf_tensor("idx_low", [LOW, E, HIGH], U32))
        idx_f = region_t[0:LOW, 1792:1792 + E * HIGH].rearrange("p (e r) -> p e r", e=E)
        powers = st.enter_context(nc.sbuf_tensor("powers", [P, BITS], I32))
        idx_all = st.enter_context(nc.sbuf_tensor("idx_all", [P, E, EC], U32))
        idx_cur = st.enter_context(nc.sbuf_tensor("idx_cur", [P, 2, EC], U32))
        sides = st.enter_context(nc.sbuf_tensor("sides", [P, B, E, EC], F32))
        kept = st.enter_context(nc.sbuf_tensor("kept", [P, 2, B, EC], F32))
        w1_sb = [region_x[:, i * 4096:i * 4096 + 2048].rearrange("p (k f) -> p k f", k=KC) for i in range(2)]
        w2_sb = [region_x[:, i * 4096 + 2048:(i + 1) * 4096].rearrange("p (f d) -> p f d", d=D) for i in range(2)]
        hidden = region_a[:, 0:4096].rearrange("p (f t) -> p f t", f=FC)
        yt = region_a[:, 4096:6144].rearrange("p (i k t) -> p i k t", i=2, k=KC)
        o_sb = region_a[:, 6144:8192].rearrange("p (i c d) -> p i c d", i=2, c=EC)
        y_sb = region_v[:, 0:2 * EC * NW].rearrange("p (i c w) -> p i c w", i=2, c=EC)
        b2_sb = region_v[:, 4096:4096 + 2 * D].rearrange("p (i d) -> p i d", i=2)
        gw = region_v[:, 5120:5120 + EC * D].rearrange("p (c d) -> p c d", c=EC)

        def over_experts(eng, emit):
            with eng.Fori(0, E // 2 - 1) as n:
                emit(2 * n, n, 0, True, True)
                emit(2 * n + 1, n, 1, True, True)
            emit(E - 2, E // 2 - 1, 0, True, False)
            emit(E - 1, E // 2 - 1, 1, False, False)

        def at(e, base=0):
            return bass.ds(e + base, 1) if not isinstance(e, int) else slice(e + base, e + base + 1)

        @block.sync
        def _(sp):
            XQ = NT // 4
            for i in range(4):
                sp.dma_start(xs[:, i * XQ:(i + 1) * XQ, :],
                             x[i * XQ * P:(i + 1) * XQ * P, :].rearrange("(t p) d -> p t d", p=P)).then_inc(ld_x[i], 16)
            for g in range(G):
                t0, t1 = g * GT, (g + 1) * GT
                sp.wait_ge(base_done, g + 1)
                sp.dma_start(out[t0 * P:t1 * P, :].rearrange("(t p) d -> p t d", p=P), base[:, t0:t1, :]).then_inc(st_out, 16)
                sp.wait_ge(normed_done, g + 1)
                sp.dma_start(normed[t0 * P:t1 * P, 0:D].rearrange("(t p) d -> p t d", p=P), nrm[:, t0:t1, :]).then_inc(st_normed, 16)

            def load(e, i):
                src = fc1_t[at(e), :, :]
                sp.dma_start(w1_sb[i], src.rearrange("o (k p) f -> p (o k) f", p=P)).then_inc(ld_weights[i], 16)
                src = fc2_t[at(e), :, :]
                sp.dma_start(w2_sb[i], src.rearrange("o (f p) d -> p (o f) d", p=P)).then_inc(ld_weights[i], 16)
                src = b2[at(e), :]
                sp.dma_start(b2_sb[:, i, :], bass.AP(tensor=src.tensor, offset=src.offset, ap=[[0, P], [1, D]])).then_inc(ld_weights[i], 16)

            sp.wait_ge(st_out, 16 * G)
            for i in range(2):
                load(i, i)
            sp.wait_ge(scores_done, 1)
            for half in range(2):
                sp.dma_start(normed[:, D:NW].rearrange("(t h p) e -> h p t e", h=2, p=P)[half], scores[:, half, :, :]).then_inc(st_scores, 16)
            sp.wait_ge(tokens_done, 1)
            for j in range(P // LOW):
                sp.dma_start(idx_all[j * LOW:(j + 1) * LOW, :, :], idx_low[:, :, j * EC:(j + 1) * EC]).then_inc(idx_moved, 16)
            with sp.Fori(0, E // 2 - 1) as i:
                for j in range(2):
                    sp.wait_ge(sum_done, i * (2 * EC) + (2 + (j + 1) * EC))
                    load(2 * i + (2 + j), j)
            sp.wait_ge(scattered, 16 * EC * E)

        @block.tensor
        def _(pe):
            for s in range(G + 5):
                if s < G:
                    g = s
                    for k in range(KC):
                        if g:
                            pe.wait_ge(ctxt_done, KC * (g - 1) + k + 1)
                        for i in range(GT):
                            last = nc.tensor.transpose(ctx_ps[k][:, i * P:(i + 1) * P],
                                                       context[:, g * GT + i, k * P:(k + 1) * P], ident[:, :])
                        last.then_inc(ctx_turned, 1)
                if 0 <= s - 3 < G:
                    g = s - 3
                    pe.wait_ge(h2_done, g + 1)
                    for k in range(KC):
                        if g:
                            pe.wait_ge(h2t_done, KC * (g - 1) + k + 1)
                        for i in range(GT):
                            last = nc.tensor.transpose(h2_ps[k][:, i * P:(i + 1) * P], h2[:, g * GT + i, k * P:(k + 1) * P], ident[:, :])
                        last.then_inc(h2_turned, 1)
                if 0 <= s - 1 < G:
                    g = s - 1
                    pe.wait_ge(ctxt_done, KC * (g + 1))
                    if g:
                        pe.wait_ge(x2_done, g)
                    for i in range(GT):
                        for k in range(KC):
                            last = nc.tensor.matmul(proj_ps[i // 2][:, i % 2, :], ctxt[:, g % 2, k, i * P:(i + 1) * P],
                                                    wo_gated[:, g // GB, k, :], start=(k == 0), stop=(k == KC - 1))
                    last.then_inc(proj_done, 1)
                if 0 <= s - 4 < G:
                    g = s - 4
                    pe.wait_ge(h2t_done, KC * (g + 1))
                    if g:
                        pe.wait_ge(gate_saved, g)
                    else:
                        pe.wait_ge(cleared, 1)
                    for k in range(KC):
                        for i in range(GT):
                            last = nc.tensor.matmul(gate_ps[32 * i:32 * i + E, 0:P], gate_sb[:, k, :],
                                                    h2t[:, g % 2, k, i * P:(i + 1) * P], start=(k == 0), stop=(k == KC - 1))
                    last.then_inc(gate_mm, 1)
                if 0 <= s - 5:
                    g = s - 5
                    pe.wait_ge(gate_saved, g + 1)
                    if g:
                        pe.wait_ge(logits_done, g)
                    nc.tensor.transpose(small_ps[:, 0:P], gate_t_sb[:, g % 2, :], ident[:, :]).then_inc(gate_back, 1)
            pe.wait_ge(scores_done, 1)
            for half in range(2):
                last = nc.tensor.transpose(small_ps[:, half * P:(half + 1) * P],
                                           scores[:, half, :, :].rearrange("p t e -> p (t e)"), ident[:, :])
            last.then_inc(scores_turned, 1)
            for i in range(BITS + 1):
                pe.wait_ge(counted, i + 1)
                nc.tensor.matmul(gate_ps[:, i % 2:i % 2 + 1], same_expert, count_b[:, i % 2:i % 2 + 1], start=True, stop=True).then_inc(totalled, 1)
            for i in range(2):
                pe.wait_ge(counted, BITS + 2 + i)
                nc.tensor.matmul(gate_ps[:, 2 + i:3 + i], rows_before, count_b[:, 2 + i:3 + i], start=True, stop=True).then_inc(totalled, 1)
            pe.wait_ge(places_done, 1)
            for half in range(2):
                last = nc.tensor.transpose(small_ps[:, half * P:(half + 1) * P], chosen[:, half * P:(half + 1) * P], ident[:, :])
            last.then_inc(places_turned, 1)
            pe.wait_ge(onehot_done, 3)
            for e in range(E):
                for t in range(NT):
                    c = t * E + e
                    last = nc.tensor.matmul(bank[5][0:LOW, e * 2 * HIGH:(e + 1) * 2 * HIGH], low_hot[:, c, :],
                                            token_of[:, :, c, :], start=(t == 0), stop=(t == NT - 1))
                last.then_inc(tokens_mm, 1)

            def turn(n, i):
                pe.wait_ge(gathered[i], n * (16 * EC) + 16 * EC)
                for k in range(KC):
                    for c in range(EC):
                        last = nc.tensor.transpose(y_ps[k][:, c * P:(c + 1) * P], y_sb[:, i, c, k * P:(k + 1) * P], ident[:, :])
                    last.then_inc(y_turned, 1)

            def emit(e, n, i, ahead, gathers):
                pe.wait_ge(ld_weights[i], n * 48 + 48)
                pe.wait_ge(yt_done, e * KC + KC)
                for f in range(FC):
                    pe.wait_ge(gelu_done, e * FC + (f + 1))
                    for k in range(KC):
                        last = nc.tensor.matmul(fc1_ps[f % 2][:, :], w1_sb[i][:, k, f * P:(f + 1) * P], yt[:, i, k, :],
                                                start=(k == 0), stop=(k == KC - 1))
                    last.then_inc(fc1_mm, 1)
                if ahead:
                    turn(n + i, 1 - i)
                for c in range(EC):
                    pe.wait_ge(sum_done, e * EC + (c + 1))
                    for f in range(FC):
                        if c == 0 and f >= FC - 2:
                            pe.wait_ge(gelu_done, e * FC + (f + 3))
                        last = nc.tensor.matmul(fc2_ps[c % 2][:, 0:D], hidden[:, f, c * P:(c + 1) * P], w2_sb[i][:, f, :],
                                                start=(f == 0), stop=(f == FC - 1))
                    last.then_inc(fc2_mm, 1)

            turn(0, 0)
            over_experts(pe, emit)

        @block.scalar
        def _(act):
            act.sem_inc(gelu_done, 2)

            def deviation(lvl, g):
                act.wait_ge(var_done[lvl], g + 1)
                nc.scalar.activation(rst[:, lvl, g * GT:(g + 1) * GT], rst[:, lvl, g * GT:(g + 1) * GT], ACT.Sqrt).then_inc(sqrt_done[lvl], 1)

            for s in range(G + 5):
                if s < G:
                    g = s
                    for k in range(KC):
                        act.wait_ge(ctx_turned, KC * g + k + 1)
                        if g >= 2:
                            act.wait_ge(proj_done, g - 1)
                        nc.scalar.copy(ctxt[:, g % 2, k, :], ctx_ps[k][:, :]).then_inc(ctxt_done, 1)
                if 0 <= s - 2 < G:
                    deviation(0, s - 2)
                if 0 <= s - 3 < G:
                    deviation(1, s - 3)
                    g = s - 3
                    for k in range(KC):
                        act.wait_ge(h2_turned, KC * g + k + 1)
                        if g >= 2:
                            act.wait_ge(gate_mm, g - 1)
                        nc.scalar.copy(h2t[:, g % 2, k, :], h2_ps[k][:, :]).then_inc(h2t_done, 1)
                if 0 <= s - 2 < G:
                    g = s - 2
                    act.wait_ge(rstd1_done, g + 1)
                    for t in range(g * GT, (g + 1) * GT):
                        last = nc.scalar.activation(h2[:, t, :], xs[:, t, :], ACT.Identity, bias=nmr[:, 0, t:t + 1], scale=rst[:, 0, t:t + 1])
                    last.then_inc(z_done, 1)
                if 0 <= s - 4 < G:
                    g = s - 4
                    act.wait_ge(gate_mm, g + 1)
                    if g >= 2:
                        act.wait_ge(gate_back, g - 1)
                    nc.scalar.copy(gate_t_sb[:, g % 2, :], gate_ps[:, 0:P]).then_inc(gate_saved, 1)
                if 0 <= s - 3 < G:
                    g = s - 3
                    act.wait_ge(rstd2_done, g + 1)
                    for t in range(g * GT, (g + 1) * GT):
                        last = nc.scalar.activation(nrm[:, t, :], h2[:, t, :], ACT.Identity, bias=nmr[:, 1, t:t + 1], scale=rst[:, 1, t:t + 1])
                    last.then_inc(normed_done, 1)
            act.wait_ge(centred, 1)
            nc.scalar.activation(scores[:, :, :, :], scores[:, :, :, :], ACT.Exp).then_inc(exped, 1)

            def emit(e, n, i, ahead, gathers):
                for f in range(FC):
                    act.wait_ge(fc1_mm, e * FC + (f + 1))
                    nc.scalar.activation(hidden[:, f, :], fc1_ps[f % 2][:, :], ACT.Gelu_apprx_tanh,
                                         bias=b1_sb[:, at(e), f].rearrange("p o -> p o")).then_inc(gelu_done, 1)

            over_experts(act, emit)

        @block.vector
        def _(dve):
            dve.sem_inc(sum_done, 2)
            steps = [0]

            def step(ins):
                steps[0] += 1
                ins.then_inc(dve_step, 1)
                dve.wait_ge(dve_step, steps[0])

            nc.vector.memset(gate_ps[:, :], 0.0).then_inc(cleared, 1)
            dve.wait_ge(bits_set, 2)
            nc.vector.tensor_tensor(bits[:, :], bits[:, :], powers[:, :], ALU.logical_shift_left)

            def norm(lvl, g, src):
                t0, t1 = g * GT, (g + 1) * GT
                for t in range(t0, t1):
                    last = nc.vector.bn_stats(stats[:, t, :], src[:, t, :])
                step(last)
                for t in range(t0, t1):
                    last = nc.vector.bn_aggr(mom[:, lvl, t, :], stats[:, t, :])
                step(last)
                nc.vector.tensor_scalar_add(rst[:, lvl, t0:t1], mom[:, lvl, t0:t1, 1], EPS).then_inc(var_done[lvl], 1)

            def rest_of_norm(lvl, g, done):
                t0, t1 = g * GT, (g + 1) * GT
                dve.wait_ge(sqrt_done[lvl], g + 1)
                step(nc.vector.reciprocal(rst[:, lvl, t0:t1], rst[:, lvl, t0:t1]))
                nc.vector.scalar_tensor_tensor(nmr[:, lvl, t0:t1], mom[:, lvl, t0:t1, 0], -1.0, rst[:, lvl, t0:t1], ALU.mult, ALU.mult).then_inc(done, 1)

            for s in range(G + 5):
                if 0 <= s - 2 < G:
                    rest_of_norm(0, s - 2, rstd1_done)
                if 0 <= s - 3 < G:
                    rest_of_norm(1, s - 3, rstd2_done)
                if 0 <= s - 1 < G:
                    g = s - 1
                    t0, t1 = g * GT, (g + 1) * GT
                    dve.wait_ge(proj_done, g + 1)
                    dve.wait_ge(xb_done, g + 1)
                    nc.vector.tensor_tensor(xs[:, t0:t0 + 2, :], xs[:, t0:t0 + 2, :], proj_ps[0], ALU.add)
                    nc.vector.tensor_tensor(xs[:, t0 + 2:t1, :], xs[:, t0 + 2:t1, :], proj_ps[1], ALU.add).then_inc(x2_done, 1)
                    dve.wait_ge(x2_done, g + 1)
                    norm(0, g, xs)
                if 0 <= s - 2 < G:
                    g = s - 2
                    b, t0, t1 = g // GB, g * GT, (g + 1) * GT
                    dve.wait_ge(z_done, g + 1)
                    step(nc.vector.tensor_tensor(h2[:, t0:t1, :], h2[:, t0:t1, :], gates[:, b, 1, :].unsqueeze(1).to_broadcast([P, GT, D]), ALU.mult))
                    nc.vector.tensor_tensor(h2[:, t0:t1, :], h2[:, t0:t1, :], gates[:, b, 0, :].unsqueeze(1).to_broadcast([P, GT, D]), ALU.add).then_inc(h2_done, 1)
                    dve.wait_ge(h2_done, g + 1)
                    norm(1, g, h2)
                if 0 <= s - 5:
                    g = s - 5
                    dve.wait_ge(gate_back, g + 1)
                    nc.vector.tensor_copy(scores[:, :, 2 * g:2 * g + 2, :].rearrange("p h t e -> p t h e"),
                                          small_ps[:, 0:P].rearrange("p (t h r) -> p t h r", t=2, h=2)[:, :, :, 0:E]).then_inc(logits_done, 1)
            dve.wait_ge(logits_done, G)
            every = scores[:, :, :, :].rearrange("p h t e -> p (h t) e")
            step(nc.vector.tensor_reduce(row_stat[:, 0, :], every, AX.X, ALU.max))
            nc.vector.tensor_tensor(every, every, row_stat[:, 0, :].unsqueeze(2).to_broadcast([P, NT, E]), ALU.subtract).then_inc(centred, 1)
            nc.vector.memset(found[:, 0:1], 0)
            nc.vector.memset(zeros, 0.0)
            dve.wait_ge(exped, 1)
            step(nc.vector.tensor_reduce(row_stat[:, 0, :], every, AX.X, ALU.add))
            step(nc.vector.reciprocal(row_stat[:, 1, :], row_stat[:, 0, :]))
            nc.vector.tensor_tensor(every, every, row_stat[:, 1, :].unsqueeze(2).to_broadcast([P, NT, E]), ALU.mult).then_inc(scores_done, 1)
            step(nc.vector.tensor_copy(found[:, 1:2], bits[:, BITS - 1:BITS]))
            dve.wait_ge(scores_turned, 1)
            step(nc.vector.tensor_copy(scores_t, small_ps[:, 0:2 * P]))
            for i in range(BITS):
                bit = BITS - 1 - i
                nc.vector.tensor_scalar(trash, scores_t, found[:, 1:2].bitcast(F32), None, ALU.is_ge, ALU.add,
                                        accum_out=count_b[:, i % 2:i % 2 + 1]).then_inc(counted, 1)
                if i:
                    step(nc.vector.tensor_tensor(found[:, 0:1], found[:, 0:1], found[:, 2:3], ALU.bitwise_or))
                if bit:
                    nc.vector.tensor_tensor(found[:, 3:4], found[:, 0:1], bits[:, bit - 1:bit], ALU.bitwise_or)
                dve.wait_ge(totalled, i + 1)
                step(nc.vector.tensor_scalar(found[:, 2:3], gate_ps[:, i % 2:i % 2 + 1], float(CAP), float(1 << bit), ALU.is_ge, ALU.mult))
                if bit:
                    step(nc.vector.tensor_tensor(found[:, 1:2], found[:, 3:4], found[:, 2:3], ALU.bitwise_or))
            step(nc.vector.tensor_tensor(found[:, 0:1], found[:, 0:1], found[:, 2:3], ALU.bitwise_or))
            threshold = found[:, 0:1].bitcast(F32)
            nc.vector.tensor_scalar(above, scores_t, threshold, None, ALU.is_gt, ALU.add, accum_out=count_b[:, BITS % 2:BITS % 2 + 1]).then_inc(counted, 1)
            nc.vector.tensor_scalar(equal, scores_t, threshold, None, ALU.is_equal, ALU.add, accum_out=count_b[:, 2:3]).then_inc(counted, 1)
            dve.wait_ge(counted, BITS + 2)
            step(nc.vector.tensor_tensor_scan(run, equal, zeros, 0.0, ALU.add, ALU.add))
            dve.wait_ge(totalled, BITS + 2)
            step(nc.vector.tensor_scalar(count_f[:, 0:1], gate_ps[:, BITS % 2:BITS % 2 + 1], -1.0, float(CAP), ALU.mult, ALU.add))
            step(nc.vector.tensor_tensor(count_f[:, 0:1], count_f[:, 0:1], gate_ps[:, 2:3], ALU.subtract))
            step(nc.vector.scalar_tensor_tensor(equal, run, count_f[:, 0:1], equal, ALU.is_le, ALU.mult))
            step(nc.vector.tensor_tensor(above, above, equal, ALU.add))
            nc.vector.tensor_scalar(trash, above, 1.0, None, ALU.mult, ALU.add, accum_out=count_b[:, 3:4]).then_inc(counted, 1)
            step(nc.vector.tensor_tensor_scan(run, above, zeros, 0.0, ALU.add, ALU.add))
            dve.wait_ge(totalled, BITS + 3)
            step(nc.vector.tensor_copy(count_f[:, 1:2], gate_ps[:, 3:4]))
            nc.vector.scalar_tensor_tensor(chosen, run, count_f[:, 1:2], above, ALU.add, ALU.mult).then_inc(places_done, 1)
            dve.wait_ge(places_turned, 1)
            step(nc.vector.tensor_scalar(place_i[:, 0, :], small_ps[:, 0:2 * P], float(LOW - 1), None, ALU.add))
            nc.vector.tensor_scalar(place_i[:, 1, :], place_i[:, 0, :], LOW.bit_length() - 1, None, ALU.arith_shift_right)
            step(nc.vector.tensor_scalar(place_i[:, 2, :], place_i[:, 0, :], LOW - 1, None, ALU.bitwise_and))
            nc.vector.tensor_copy(high, place_i[:, 1, :])
            step(nc.vector.tensor_scalar_add(low, place_i[:, 2, :], 1.0))
            step(nc.vector.tensor_tensor(high_hot, iota_row[:, 0:HIGH].unsqueeze(1).to_broadcast([P, COLS, HIGH]),
                                         high.unsqueeze(2).to_broadcast([P, COLS, HIGH]), ALU.is_equal))
            nc.vector.tensor_tensor(token_of[:, 0, :, :], high_hot, tile_of.unsqueeze(2).to_broadcast([P, COLS, HIGH]),
                                    ALU.mult).then_inc(onehot_done, 1)
            nc.vector.tensor_tensor(token_of[:, 1, :, :], high_hot, row_of.unsqueeze(2).to_broadcast([P, COLS, HIGH]),
                                    ALU.mult).then_inc(onehot_done, 1)
            nc.vector.tensor_tensor(low_hot, iota_row[:, 0:LOW].unsqueeze(1).to_broadcast([P, COLS, LOW]),
                                    low.unsqueeze(2).to_broadcast([P, COLS, LOW]), ALU.is_equal).then_inc(onehot_done, 1)
            dve.wait_ge(tokens_mm, E)
            found_ps = bank[5][0:LOW, 0:E * 2 * HIGH].rearrange("p (e s r) -> p e s r", e=E, s=2)
            step(nc.vector.tensor_scalar(idx_f, found_ps[:, :, 0, :], float(P), None, ALU.mult))
            nc.vector.tensor_tensor(idx_low[:, :, :], idx_f, found_ps[:, :, 1, :], ALU.add).then_inc(tokens_done, 1)
            dve.wait_ge(idx_moved, 16 * (P // LOW))
            nc.vector.tensor_scalar(sides[:, 0, :, :], idx_all[:, :, :], float(N), None, ALU.is_lt)
            step(nc.vector.tensor_scalar(sides[:, 1, :, :], idx_all[:, :, :], float(N), None, ALU.is_ge))

            def normed_in(e, i):
                for k in range(KC):
                    dve.wait_ge(y_turned, e * KC + (k + 1))
                    nc.vector.tensor_scalar(yt[:, i, k, :], y_ps[k][:, :], lnw_sb[:, k:k + 1], lnb_sb[:, k:k + 1],
                                            ALU.mult, ALU.add).then_inc(yt_done, 1)

            def emit(e, n, i, ahead, gathers):
                dve.wait_ge(gathered[i], n * (16 * EC) + 16 * EC)
                for b in range(B):
                    last = nc.vector.tensor_tensor(kept[:, i, b, :], y_sb[:, i, :, at(e, D)].rearrange("p c o -> p (c o)"),
                                                   sides[:, b, at(e), :].rearrange("p o c -> p (o c)"), ALU.mult)
                last.then_inc(kept_done, 1)
                dve.wait_ge(kept_done, e + 1)
                for c in range(EC):
                    last = nc.vector.tensor_scalar(gw[:, c, :], gates[:, 0, 2, :], kept[:, i, 0, c:c + 1], None, ALU.mult)
                last.then_inc(gw_step, 1)
                dve.wait_ge(gw_step, e * 2 + 1)
                for c in range(EC):
                    last = nc.vector.scalar_tensor_tensor(gw[:, c, :], gates[:, 1, 2, :], kept[:, i, 1, c:c + 1], gw[:, c, :], ALU.mult, ALU.add)
                last.then_inc(gw_step, 1)
                if ahead:
                    normed_in(e + 1, 1 - i)
                for c in range(EC):
                    dve.wait_ge(fc2_mm, e * EC + (c + 1))
                    if c == 0:
                        dve.wait_ge(ld_weights[i], n * 48 + 48)
                    nc.vector.tensor_tensor(o_sb[:, i, c, :], fc2_ps[c % 2][:, 0:D], b2_sb[:, i, :], ALU.add).then_inc(sum_done, 1)
                    dve.wait_ge(sum_done, e * EC + (c + 3))
                    if c == 0:
                        dve.wait_ge(gw_step, e * 2 + 2)
                    nc.vector.tensor_tensor(o_sb[:, i, c, :], o_sb[:, i, c, :], gw[:, c, :], ALU.mult).then_inc(o_done, 1)

            normed_in(0, 0)
            over_experts(dve, emit)

        @block.gpsimd
        def _(pool):
            nc.gpsimd.memset(bits[:, :], 1).then_inc(bits_set, 1)
            nc.gpsimd.iota(powers[:, :], [[1, BITS]], base=0, channel_multiplier=0).then_inc(bits_set, 1)
            for s in range(G + 3):
                if s < G:
                    g = s
                    t0, t1 = g * GT, (g + 1) * GT
                    if g % 2 == 0:
                        pool.wait_ge(ld_x[g // 2], 16)
                    nc.gpsimd.tensor_tensor(xs[:, t0:t1, :], xs[:, t0:t1, :], bo_gated[:, g // GB, :].unsqueeze(1).to_broadcast([P, GT, D]),
                                            ALU.add).then_inc(xb_done, 1)
                if s >= 3:
                    g = s - 3
                    t0, t1 = g * GT, (g + 1) * GT
                    pool.wait_ge(h2_done, g + 1)
                    nc.gpsimd.tensor_tensor(base[:, t0:t1, :], h2[:, t0:t1, :], gates[:, g // GB, 2, :].unsqueeze(1).to_broadcast([P, GT, D]),
                                            ALU.mult).then_inc(gbh_done, 1)
                    pool.wait_ge(gbh_done, g + 1)
                    nc.gpsimd.tensor_tensor(base[:, t0:t1, :], base[:, t0:t1, :], xs[:, t0:t1, :], ALU.add).then_inc(base_done, 1)

            def gather(e, i):
                nc.gpsimd.tensor_copy(idx_cur[:, i, :], idx_all[:, at(e), :].rearrange("p o c -> p (o c)")).then_inc(idx_copied, 1)
                pool.wait_ge(idx_copied, e + 1)
                pool.sem_inc(passed_pool, 1)
                for c in range(EC):
                    nc.gpsimd.indirect_dma_start(y_sb[:, i, c, :], None, normed,
                                                 bass.IndirectOffsetOnAxis(ap=idx_cur[:, i, c:c + 1], axis=0)).then_inc(gathered[i], 16)

            def emit(e, n, i, ahead, gathers):
                for c in range(EC):
                    pool.wait_ge(o_done, e * EC + (c + 1))
                    pool.sem_inc(passed_pool, 1)
                    nc.gpsimd.indirect_dma_start(out, bass.IndirectOffsetOnAxis(ap=idx_cur[:, i, c:c + 1], axis=0),
                                                 o_sb[:, i, c, :], None, compute_op=ALU.add).then_inc(scattered, 16)
                pool.wait_ge(scattered, e * (16 * EC) + 16 * EC)
                pool.sem_inc(passed_pool, 1)
                if gathers:
                    gather(e + 2, i)

            pool.wait_ge(idx_moved, 16 * (P // LOW))
            pool.wait_ge(st_normed, 16 * G)
            pool.wait_ge(st_scores, 32)
            pool.wait_ge(st_out, 16 * G)
            gather(0, 0)
            gather(1, 1)
            over_experts(pool, emit)


def kernel(L0_attn_x, L0_attn_Wq, L0_attn_Wk, L0_attn_Wv, L0_attn_Wo, L0_attn_bo, L0_attn_w, L0_attn_v,
           L0_ffn_gate_w, L0_ffn_ln_w, L0_ffn_ln_b, L0_ffn_fc1s, L0_ffn_b1s, L0_ffn_fc2s, L0_ffn_b2s, L0_c, L0_wmod):
    import concourse.bacc as bacc
    import numpy as np
    from concourse.bass_utils import run_bass_kernel_spmd

    def a(v):
        return np.asarray(v)

    p = np.arange(P)
    consts = np.zeros((P, C_W), np.float32)
    consts[:, C_ID:C_ID + P] = np.eye(P)
    consts[:, C_DIAG:C_DIAG + P] = np.where(p[:, None] > P - 1 - p[None, :], MASKED, 0.0)
    consts[:, C_FULL:C_FULL + P] = MASKED
    consts[:, C_SAME:C_SAME + P] = p[:, None] % E == p[None, :] % E
    consts[:, C_BELOW:C_BELOW + P] = (p[:, None] % E == p[None, :] % E) & (p[:, None] // E < p[None, :] // E)
    consts[:, C_IOTA:C_IOTA + P] = p[None, :] + 1
    col = np.arange(NT * E)
    consts[:, C_TILE:C_TILE + NT * E] = (2 * (col // E % (NT // 2)) + col // (NT * E // 2))[None, :]
    consts[:, C_ROW:C_ROW + NT * E] = p[:, None]
    arrays = {
        "x": a(L0_attn_x).reshape(TOK, D),
        "c_t": a(L0_c).T,
        "wmod": a(L0_wmod),
        "wq": a(L0_attn_Wq), "wk": a(L0_attn_Wk), "wv": a(L0_attn_Wv), "wo": a(L0_attn_Wo),
        "bo": a(L0_attn_bo).reshape(1, D),
        "dist_w": a(L0_attn_w).reshape(H, 1), "dist_v": a(L0_attn_v).reshape(H, 1),
        "gate_t": a(L0_ffn_gate_w).T,
        "ln_w": a(L0_ffn_ln_w).reshape(KC, P).T, "ln_b": a(L0_ffn_ln_b).reshape(KC, P).T,
        "fc1_t": a(L0_ffn_fc1s).transpose(0, 2, 1),
        "b1": a(L0_ffn_b1s).reshape(E, FC, P).transpose(2, 0, 1).reshape(P, E * FC),
        "fc2_t": a(L0_ffn_fc2s).transpose(0, 2, 1),
        "b2": a(L0_ffn_b2s),
        "consts": consts,
    }
    nc = bacc.Bacc("TRN2", target_bir_lowering=False, num_devices=1)
    arrays = {f"in_{k}": np.ascontiguousarray(v) for k, v in arrays.items()}
    args = [nc.dram_tensor(k, v.shape, mybir.dt.from_np(v.dtype), kind="ExternalInput").ap() for k, v in arrays.items()]
    result = nc.dram_tensor("result", (TOK, D), F32, kind="ExternalOutput").ap()
    adaln_block(nc, *args, result)
    r = run_bass_kernel_spmd(nc, [arrays], core_ids=[0])
    return r.results[0]["result"].reshape(B, N, D)
```

```python
from contextlib import ExitStack

import concourse.bass as bass
from concourse import mybir

F32 = mybir.dt.float32
BF16 = mybir.dt.bfloat16
I32 = mybir.dt.int32
U32 = mybir.dt.uint32
ALU = mybir.AluOpType
ACT = mybir.ActivationFunctionType
AX = mybir.AxisListType

P = 128
B, N, D = 2, 2048, 256
H = 16
HD = D // H
TOK = B * N
NT = TOK // P
BT = N // P
KC = D // P
E = 8
F = 4 * D
FC = F // P
CAP = TOK // E
EC = CAP // P
EPS = 1e-5
NW = D + E
LN_GROUP = 4
NG = NT // LN_GROUP
GW = LN_GROUP * P
RW = N + P
MASKED = -1e30
VW = 32

C_ID, C_FULL, C_SAME, C_BELOW, C_TILE = (P * i for i in range(5))
C_ROW = C_TILE + NT * E
C_W = C_ROW + 1


def adaln_block(nc, x, c_t, wmod, wq, wk, wv, wo, bo, dist_w, dist_v, gate_t, ln_w, ln_b,
                fc1_t, b1, fc2_t, b2, consts, out):
    ctx = ExitStack()
    with ctx:
        def sb(name, shape, dt=F32):
            return ctx.enter_context(nc.sbuf_tensor(name, shape, dt))

        def ps(name, shape, dt=F32):
            return ctx.enter_context(nc.psum_tensor(name, shape, dt))

        def dram(name, shape, dt):
            return nc.dram_tensor(name, shape, dt, kind="Internal").ap()

        q_split = dram("q_split", (3, D, TOK), BF16)
        k_split = dram("k_split", (3, D, TOK), BF16)
        factor_rows = dram("factor_rows", (H, RW), F32)
        normed = dram("normed", (TOK, NW), F32)

        region_x = sb("region_x", [P, NT * D])
        region_a = sb("region_a", [P, 8192])
        region_v = sb("region_v", [P, NT * D])
        region_c = sb("region_c", [P, NT * D])
        region_s = sb("region_s", [P, 4096])
        region_t = sb("region_t", [P, 4096])
        region_o = sb("region_o", [P, 4096])
        region_p = sb("region_p", [P, 2048])
        xs = region_x[:, :].rearrange("p (t d) -> p t d", d=D)
        vals = region_v[:, :].rearrange("p (t d) -> p t d", d=D)
        context = region_c[:, :].rearrange("p (t d) -> p t d", d=D)

        ident = sb("ident", [P, P])
        bconst = sb("bconst", [P, C_W], BF16)
        ident_b = bconst[:, C_ID:C_ID + P]
        mask_full = bconst[:, C_FULL:C_FULL + P]
        same_expert = bconst[:, C_SAME:C_SAME + P]
        rows_before = bconst[:, C_BELOW:C_BELOW + P]
        tile_of = bconst[:, C_TILE:C_TILE + NT * E]
        row_of = bconst[:, C_ROW:C_ROW + 1]
        wo_gated = sb("wo_gated", [P, B, KC, D])
        bo_gated = sb("bo_gated", [P, B, D])
        gates = sb("gates", [P, B, 3, D])
        modt = sb("modt", [P, 4, B])
        gate_sb = sb("gate_sb", [P, KC, E])
        lnw_sb = sb("lnw_sb", [P, KC])
        lnb_sb = sb("lnb_sb", [P, KC])
        b1_sb = sb("b1_sb", [P, E, FC])
        moments = sb("moments", [P, NT, 2])
        rstd = sb("rstd", [P, NT])

        stacks = region_s[:, :].bitcast(BF16).rearrange("p (b w t) -> p b w t", b=B, w=2)
        factors = region_t[:, :].rearrange("p (b t) -> p b t", b=B)
        vblock = sb("vblock", [P, B, BT, VW])
        loaded = [ctx.enter_context(nc.semaphore("loaded0")), ctx.enter_context(nc.semaphore("loaded1"))]

        def load_head(sp, h, b):
            t0 = b * N
            for first, s, copies in ((0, 0, 3), (3, 1, 3), (6, 2, 2)):
                src = q_split[s, bass.ds(h * HD, HD), t0:t0 + N]
                src = bass.AP(tensor=src.tensor, offset=src.offset, ap=[[0, copies], *src.ap])
                sp.dma_start(stacks[first * HD:(first + copies) * HD, b, 0, :], src).then_inc(loaded[b], 16)
            for first, count in ((0, 3), (3, 3), (6, 2)):
                src = k_split[0:count, bass.ds(h * HD, HD), t0:t0 + N]
                sp.dma_start(stacks[first * HD:(first + count) * HD, b, 1, :], src).then_inc(loaded[b], 16)
            src = factor_rows[bass.ds(h, 1), 0:N]
            sp.dma_start(factors[:, b, :], bass.AP(tensor=src.tensor, offset=src.offset, ap=[[1, P], [1, N]])).then_inc(loaded[b], 16)

        with ExitStack() as st, nc.Block() as block:
            sem = lambda name: st.enter_context(nc.semaphore(name))
            ld_x = [sem(f"ld_x{i}") for i in range(4)]
            vblock_set = sem("vblock_set")
            ld_c, ld_mod, ld_rows, ld_ident, ld_bo = sem("ld_c"), sem("ld_mod"), sem("ld_rows"), sem("ld_ident"), sem("ld_bo")
            ld_rest, ld_w, ld_dist = sem("ld_rest"), sem("ld_w"), sem("ld_dist")
            silu_exp, silu_done, modt_mm, modt_done = sem("silu_exp"), sem("silu_done"), sem("modt_mm"), sem("modt_done")
            bc_mm, gates_done = sem("bc_mm"), sem("gates_done")
            dist_iota, dist_exp, dist_done = sem("dist_iota"), sem("dist_exp"), sem("dist_done")
            dve_step, var_done, sqrt_done, xn_done = sem("dve_step"), sem("var_done"), sem("sqrt_done"), sem("xn_done")
            xt_mm, ht0_done, ht1_done = sem("xt_mm"), sem("ht0_done"), sem("ht1_done")
            proj_mm, part1, rest1, part2, part3 = sem("proj_mm"), sem("part1"), sem("rest1"), sem("part2"), sem("part3")
            val_mm, val_done, consts_done = sem("val_mm"), sem("val_done"), sem("consts_done")
            st_split, st_dist = [sem(f"st_split{i}") for i in range(4)], sem("st_dist")

            PB, SPLITS = 3, 4
            psum_xt = st.enter_context(nc.psum_tensor("psum_xt", [P, KC, GW], F32))
            psum_proj = st.enter_context(nc.psum_tensor("psum_proj", [P, PB, GW], F32))
            psum_rows = st.enter_context(nc.psum_tensor("psum_rows", [P, 2, D], F32))
            psum_val = st.enter_context(nc.psum_tensor("psum_val", [P, 2, 2, D], F32))
            ht = region_a[:, :].rearrange("p (k t) -> p k t", k=KC)
            w_sb = region_s[:, 2048:2048 + 3 * KC * D].rearrange("p (w k m) -> p w k m", w=3, k=KC)
            wmod_sb = region_c[:, 0:KC * 6 * D].rearrange("p (k m) -> p k m", k=KC)
            xn = region_c[:, 3072:3072 + 8 * D].rearrange("p (t d) -> p t d", d=D)
            rest = region_c[:, 5120:5120 + SPLITS * GW].rearrange("p (i t) -> p i t", i=SPLITS)
            PW = 3 * GW // 2
            parts = [r[:, at:at + PW].bitcast(BF16).rearrange("p (s t) -> p s t", s=3)
                     for r, at in ((region_o, 768), (region_o, 768 + PW), (region_t, N), (region_t, N + PW))]
            const_f = region_o[:, 2304:2304 + C_W]
            DQ = RW // 4
            dist = region_o[:, 0:DQ]
            silu_bc = region_p[:, 0:KC * B * P].rearrange("p (k b m) -> p k b m", k=KC, b=B)
            wo_sb = region_p[:, 512:1024].rearrange("p (k m) -> p k m", k=KC)
            attn_gate = region_p[:, 1024:1536].rearrange("p (b d) -> p b d", b=B)
            cs = st.enter_context(nc.sbuf_tensor("cs", [P, 4, KC, B], F32))
            dw_sb = st.enter_context(nc.sbuf_tensor("dw_sb", [P, 4], F32))
            bo_sb = st.enter_context(nc.sbuf_tensor("bo_sb", [P, D], F32))
            stats = st.enter_context(nc.sbuf_tensor("stats", [P, NT, 6], F32))
            gtmp = region_p[:, 1536:2048].rearrange("p (i d) -> p i d", i=2)
            XQ = NT // 4
            N_REST = 6

            @block.sync
            def _(sp):
                def load_x(i):
                    sp.dma_start(xs[:, i * XQ:(i + 1) * XQ, :],
                                 x[i * XQ * P:(i + 1) * XQ * P, :].rearrange("(t p) d -> p t d", p=P)).then_inc(ld_x[i], 16)

                load_x(0)
                for i, w in enumerate((wq, wk, wv)):
                    sp.dma_start(w_sb[:, i, :, :], w.rearrange("(k p) m -> p k m", p=P)).then_inc(ld_w, 16)
                for i in range(1, 4):
                    load_x(i)
                for u in range(4 * NG):
                    g, which, m = u // 4, (u // 2) % 2, u % 2
                    if u == 4 * (NG // B):
                        sp.wait_ge(dist_done, 1)
                        for c in range(4):
                            sp.dma_start(factor_rows[:, c * DQ:(c + 1) * DQ], dist[32 * c:32 * c + H, :]).then_inc(st_dist, 16)
                    if u == 4 * (NG // B) + 2 * SPLITS:
                        for i in range(SPLITS):
                            sp.wait_ge(st_split[i], 16 * 4 * (NG // B) // SPLITS)
                        sp.wait_ge(st_dist, 64)
                        load_head(sp, 0, 0)
                    sp.wait_ge(part3, u + 1)
                    dst = (q_split, k_split)[which]
                    sp.dma_start(dst[:, m * P:(m + 1) * P, g * GW:(g + 1) * GW].rearrange("s p t -> p s t"),
                                 parts[u % SPLITS]).then_inc(st_split[u % SPLITS], 16)
                for i in range(SPLITS):
                    sp.wait_ge(st_split[i], 16 * 4 * NG // SPLITS)

            @block.gpsimd
            def _(pool):
                pool.dma_start(ident[:, :], consts[:, C_ID:C_ID + P]).then_inc(ld_ident, 16)
                for c in range(4):
                    if c:
                        pool.wait_ge(dist_iota, c)
                    nc.gpsimd.iota(dist[32 * c:32 * c + 32, :], [[-1, DQ]], base=N - 1 - c * DQ, channel_multiplier=0,
                                   allow_small_or_imprecise_dtypes=True).then_inc(dist_iota, 1)
                pool.dma_start(const_f, consts).then_inc(ld_rest, 16)
                pool.dma_start(wo_sb, wo.rearrange("(k p) m -> p k m", p=P)).then_inc(ld_rest, 16)
                pool.dma_start(gate_sb[:, :, :], gate_t.rearrange("(k p) e -> p k e", p=P)).then_inc(ld_rest, 16)
                pool.dma_start(lnw_sb[:, :], ln_w).then_inc(ld_rest, 16)
                pool.dma_start(lnb_sb[:, :], ln_b).then_inc(ld_rest, 16)
                pool.dma_start(b1_sb[:, :, :], b1.rearrange("p (e f) -> p e f", e=E)).then_inc(ld_rest, 16)
                pool.wait_ge(ld_rest, 16 * N_REST)
                pool.wait_ge(dist_iota, 4)
                nc.gpsimd.tensor_copy(bconst[:, :], const_f).then_inc(consts_done, 1)
                nc.gpsimd.memset(vblock[:, :, :, :], 0.0).then_inc(vblock_set, 1)
                pool.wait_ge(vblock_set, 1)
                nc.gpsimd.memset(vblock[:, :, :, HD:HD + 1], 1.0)
                for u in range(4 * NG):
                    pool.wait_ge(part2, u + 1)
                    nc.gpsimd.tensor_tensor(parts[u % SPLITS][:, 2, :], rest[:, u % SPLITS, :], parts[u % SPLITS][:, 1, :],
                                            ALU.subtract).then_inc(part3, 1)

            def evacuate(act, split, second, g):
                for i in range(4):
                    u = 4 * g + i
                    split(u)
                    if u >= 1:
                        second(u - 1)
                if g == NG - 1:
                    second(4 * NG - 1)
                for i in range(2):
                    act.wait_ge(val_mm, 2 * g + i + 1)
                    nc.scalar.copy(vals[:, 4 * g + 2 * i:4 * g + 2 * i + 2, :], psum_val[:, i, :, :]).then_inc(val_done, 1)

            @block.scalar
            def _(act):
                act.dma_start(cs[:, 0, :, :], c_t.rearrange("(k p) b -> p k b", p=P)).then_inc(ld_c, 16)
                wmod_v = wmod.rearrange("(k p) m -> p k m", p=P)
                act.dma_start(wmod_sb[:, :, 0:2 * D], wmod_v[:, :, 0:2 * D]).then_inc(ld_mod, 16)
                for i, v in enumerate((dist_w, dist_v)):
                    act.dma_start(dw_sb[:, i:i + 1], bass.AP(tensor=v.tensor, offset=v.offset, ap=[[0, P // H], *v.ap])).then_inc(ld_dist, 16)
                act.dma_start(wmod_sb[:, :, 2 * D:], wmod_v[:, :, 2 * D:]).then_inc(ld_rows, 16)
                act.dma_start(bo_sb[:, :], bass.AP(tensor=bo.tensor, offset=bo.offset, ap=[[0, P], [1, D]])).then_inc(ld_bo, 16)
                act.wait_ge(ld_c, 16)
                nc.scalar.activation(cs[:, 1, :, :], cs[:, 0, :, :], ACT.Exp, scale=-1.0).then_inc(silu_exp, 1)
                def deviation(i):
                    act.wait_ge(var_done, i + 1)
                    nc.scalar.activation(rstd[:, i * XQ:(i + 1) * XQ], rstd[:, i * XQ:(i + 1) * XQ],
                                         ACT.Sqrt).then_inc(sqrt_done, 1)

                deviation(0)

                def distance_exps():
                    act.wait_ge(ld_dist, 32)
                    nc.scalar.activation(dw_sb[:, 2:3], dw_sb[:, 1:2], ACT.Exp).then_inc(dist_exp, 1)
                    act.wait_ge(dist_iota, 5)
                    nc.scalar.activation(dist, dist, ACT.Exp, bias=dw_sb[:, 1:2], scale=dw_sb[:, 3:4]).then_inc(dist_exp, 1)


                def split(u):
                    act.wait_ge(proj_mm, u + 1)
                    if u >= SPLITS:
                        act.wait_ge(st_split[u % SPLITS], 16 * (u // SPLITS))
                    src = psum_proj[:, u % PB, :]
                    if (u // 2) % 2 == 0:
                        src = src.rearrange("p (a b) -> p a b", b=P)[:, :, ::-1]
                    dst = parts[u % SPLITS][:, 0, :]
                    if (u // 2) % 2 == 0:
                        dst = dst.rearrange("p (a b) -> p a b", b=P)
                    nc.scalar.copy(dst, src).then_inc(part1, 1)

                def second(u):
                    act.wait_ge(rest1, u + 1)
                    nc.scalar.copy(parts[u % SPLITS][:, 1, :], rest[:, u % SPLITS, :]).then_inc(part2, 1)

                for g in range(NG):
                    act.wait_ge(xt_mm, 2 * g + 1)
                    act.wait_ge(modt_done, 1)
                    nc.scalar.activation(ht[:, 0, g * GW:(g + 1) * GW], psum_xt[:, 0, :], ACT.Identity,
                                         bias=modt[:, 0, g // (NG // B):g // (NG // B) + 1],
                                         scale=modt[:, 2, g // (NG // B):g // (NG // B) + 1]).then_inc(ht0_done, 1)
                    if g == 0:
                        deviation(1)
                        distance_exps()
                    if g >= 1:
                        evacuate(act, split, second, g - 1)
                    if g in (1, 3):
                        deviation((g + 3) // 2)
                evacuate(act, split, second, NG - 1)

            @block.vector
            def _(dve):
                steps = [0]

                def step(ins):
                    steps[0] += 1
                    ins.then_inc(dve_step, 1)
                    dve.wait_ge(dve_step, steps[0])

                def silu():
                    dve.wait_ge(silu_exp, 1)
                    step(nc.vector.tensor_scalar_add(cs[:, 2, :, :], cs[:, 1, :, :], 1.0))
                    step(nc.vector.reciprocal(cs[:, 3, :, :], cs[:, 2, :, :]))
                    step(nc.vector.tensor_tensor(cs[:, 1, :, :], cs[:, 0, :, :], cs[:, 3, :, :], ALU.mult))
                    dve.sem_inc(silu_done, 1)
                    nc.vector.tensor_copy(silu_bc, cs[:, 1, :, :].unsqueeze(3).to_broadcast([P, KC, B, P])).then_inc(silu_done, 1)

                def distances():
                    dve.wait_ge(ld_dist, 32)
                    step(nc.vector.tensor_scalar(dw_sb[:, 3:4], dw_sb[:, 0:1], -1.0, None, ALU.mult))
                    dve.wait_ge(dist_iota, 4)
                    nc.vector.tensor_scalar(dist, dist, 0.0, None, ALU.max).then_inc(dist_iota, 1)

                def norm_group(i):
                    dve.wait_ge(ld_x[i], 16)
                    for t in range(i * XQ, (i + 1) * XQ):
                        last = nc.vector.bn_stats(stats[:, t, :], xs[:, t, :])
                    step(last)
                    for t in range(i * XQ, (i + 1) * XQ):
                        last = nc.vector.bn_aggr(moments[:, t, :], stats[:, t, :])
                    step(last)
                    nc.vector.tensor_scalar_add(rstd[:, i * XQ:(i + 1) * XQ], moments[:, i * XQ:(i + 1) * XQ, 1],
                                                EPS).then_inc(var_done, 1)

                def normed_tiles(g):
                    i = g * LN_GROUP // XQ
                    if g * LN_GROUP % XQ == 0:
                        dve.wait_ge(sqrt_done, i + 1)
                        step(nc.vector.reciprocal(rstd[:, i * XQ:(i + 1) * XQ], rstd[:, i * XQ:(i + 1) * XQ]))
                    if g >= 2:
                        dve.wait_ge(xt_mm, 2 * g - 2)
                    for t in range(g * LN_GROUP, (g + 1) * LN_GROUP):
                        last = nc.vector.tensor_scalar(xn[:, t % 8, :], xs[:, t, :], moments[:, t, 0:1], rstd[:, t:t + 1],
                                                       ALU.subtract, ALU.mult)
                    last.then_inc(xn_done, 1)

                def transposed(g):
                    dve.wait_ge(xt_mm, 2 * g + 2)
                    if g == 0:
                        dve.wait_ge(modt_done, 1)
                    nc.vector.tensor_scalar(ht[:, 1, g * GW:(g + 1) * GW], psum_xt[:, 1, :],
                                            modt[:, 3, g // (NG // B):g // (NG // B) + 1],
                                            modt[:, 1, g // (NG // B):g // (NG // B) + 1], ALU.mult, ALU.add).then_inc(ht1_done, 1)

                def remainder(u):
                    dve.wait_ge(part1, u + 1)
                    if u >= SPLITS:
                        dve.wait_ge(part3, u - SPLITS + 1)
                    a, b_, c_ = rest[:, u % SPLITS, :], psum_proj[:, u % PB, :], parts[u % SPLITS][:, 0, :]
                    if (u // 2) % 2 == 0:
                        a, b_, c_ = (v.rearrange("p (a b) -> p a b", b=P) for v in (a, b_, c_))
                        b_ = b_[:, :, ::-1]
                    nc.vector.tensor_tensor(a, b_, c_, ALU.subtract).then_inc(rest1, 1)

                def factors():
                    dve.wait_ge(dist_exp, 2)
                    step(nc.vector.tensor_scalar(dw_sb[:, 2:3], dw_sb[:, 2:3], 1.0, 1.0 / HD ** 0.5, ALU.add, ALU.mult))
                    step(nc.vector.tensor_scalar_add(dist, dist, 1.0))
                    step(nc.vector.reciprocal(dist, dist))
                    step(nc.vector.tensor_scalar(dist, dist, dw_sb[:, 2:3], None, ALU.mult))
                    nc.vector.memset(dist[96:P, N - 3 * DQ:DQ], 0.0).then_inc(dist_done, 1)

                def gate_rows(n):
                    b, i = n // 2, n % 2
                    dve.wait_ge(bc_mm, n + 1)
                    raw = psum_rows[:, i, :]
                    nc.vector.tensor_scalar(gtmp[:, 0, :], raw, 0.0, 2.0, ALU.is_ge, ALU.mult)
                    step(nc.vector.tensor_scalar(gtmp[:, 1, :], raw, -1.0, 0.25, ALU.mult, ALU.max))
                    step(nc.vector.tensor_tensor(gtmp[:, 1, :], gtmp[:, 1, :], raw, ALU.max))
                    if i == 0:
                        nc.vector.tensor_copy(gates[:, b, 0, :], psum_rows[:, 1, :]).then_inc(gates_done, 1)
                    else:
                        nc.vector.tensor_scalar_add(gates[:, b, 1, :], psum_rows[:, 0, :], 1.0).then_inc(gates_done, 1)
                    dst = gates[:, b, 2, :] if i else attn_gate[:, b, :]
                    step(nc.vector.scalar_tensor_tensor(dst, gtmp[:, 0, :], -1.0, gtmp[:, 1, :], ALU.add, ALU.mult))
                    if i == 0:
                        dve.wait_ge(ld_rest, 16 * N_REST)
                        dve.wait_ge(ld_bo, 16)
                        for k in range(KC):
                            nc.vector.tensor_tensor(wo_gated[:, b, k, :], wo_sb[:, k, :], attn_gate[:, b, :], ALU.mult)
                        nc.vector.tensor_tensor(bo_gated[:, b, :], bo_sb[:, :], attn_gate[:, b, :], ALU.mult)

                norm_group(0)
                silu()
                normed_tiles(0)
                dve.wait_ge(modt_mm, 1)
                step(nc.vector.tensor_copy(modt[:, :, :], psum_val[:, 0, 0, 0:8].rearrange("p (m b) -> p m b", b=B)))
                nc.vector.tensor_scalar_add(modt[:, 2:4, :], modt[:, 2:4, :], 1.0).then_inc(modt_done, 1)
                normed_tiles(1)
                for g in range(NG):
                    transposed(g)
                    if g == 0:
                        norm_group(1)
                        distances()
                    if g + 2 < NG:
                        normed_tiles(g + 2)
                    if g >= 1:
                        for u in range(4 * g - 4, 4 * g):
                            remainder(u)
                    if g in (1, 3):
                        norm_group((g + 3) // 2)
                    if g == 1:
                        factors()
                    if 2 <= g < 2 + 2 * B:
                        gate_rows(g - 2)
                for u in range(4 * NG - 4, 4 * NG):
                    remainder(u)

            @block.tensor
            def _(pe):
                pe.wait_ge(ld_mod, 16)
                pe.wait_ge(silu_done, 1)
                for m in range(4):
                    for k in range(KC):
                        last = nc.tensor.matmul(psum_val[:, 0, 0, 2 * m:2 * m + 2], wmod_sb[:, k, m * P:(m + 1) * P],
                                                cs[:, 1, k, :], start=(k == 0), stop=(k == KC - 1))
                last.then_inc(modt_mm, 1)
                pe.wait_ge(ld_ident, 16)

                def mod_rows(n):
                    b, i = n // 2, n % 2
                    if n:
                        pe.wait_ge(gates_done, n)
                    else:
                        pe.wait_ge(ld_rows, 16)
                        pe.wait_ge(silu_done, 2)
                    for k in range(KC):
                        last = nc.tensor.matmul(psum_rows[:, :, :].rearrange("p i d -> p (i d)"), silu_bc[:, k, b, :],
                                                wmod_sb[:, k, 2 * D + i * GW:2 * D + (i + 1) * GW], start=(k == 0), stop=(k == KC - 1))
                    last.then_inc(bc_mm, 1)

                def transpose_group(g):
                    pe.wait_ge(xn_done, g + 1)
                    if g >= 1:
                        pe.wait_ge(ht0_done, g)
                        pe.wait_ge(ht1_done, g)
                    for k in range(KC):
                        for i in range(LN_GROUP):
                            last = nc.tensor.transpose(psum_xt[:, k, i * P:(i + 1) * P],
                                                       xn[:, (g * LN_GROUP + i) % 8, k * P:(k + 1) * P], ident[:, :])
                        last.then_inc(xt_mm, 1)

                transpose_group(0)
                pe.wait_ge(ld_w, 48)
                for g in range(NG):
                    if g + 1 < NG:
                        transpose_group(g + 1)
                    pe.wait_ge(ht0_done, g + 1)
                    pe.wait_ge(ht1_done, g + 1)
                    for i in range(4):
                        u = 4 * g + i
                        if u >= PB:
                            pe.wait_ge(rest1, u - PB + 1)
                        for k in range(KC):
                            last = nc.tensor.matmul(psum_proj[:, u % PB, :], w_sb[:, i // 2, k, (i % 2) * P:(i % 2 + 1) * P],
                                                    ht[:, k, g * GW:(g + 1) * GW], start=(k == 0), stop=(k == KC - 1))
                        last.then_inc(proj_mm, 1)
                    for i in range(2):
                        if g >= 1:
                            pe.wait_ge(val_done, 2 * g + i - 1)
                        for j in range(2):
                            t = 4 * g + 2 * i + j
                            for k in range(KC):
                                last = nc.tensor.matmul(psum_val[:, i, j, :], ht[:, k, t * P:(t + 1) * P],
                                                        w_sb[:, 2, k, :], start=(k == 0), stop=(k == KC - 1))
                        last.then_inc(val_mm, 1)
                    if 1 <= g < 1 + 2 * B:
                        mod_rows(g - 1)

        attention(nc, locals())
        mixture(nc, locals())


def attention(nc, o):
    region_a, region_o, region_p = (o[k] for k in ("region_a", "region_o", "region_p"))
    vals, context, ident, ident_b = o["vals"], o["context"], o["ident"], o["ident_b"]
    mask_full = o["mask_full"]

    NP = BT // 2
    SB, SW = 4, 512
    stacks, factors, vblock, loaded, load_head = (o[k] for k in ("stacks", "factors", "vblock", "loaded", "load_head"))
    packing = ((o["region_x"], (16, 15, 14, 13, 6)), (region_a, (12, 11, 10, 9, 8, 7, 5, 2)), (region_o[:, N:], (4, 3, 1)))
    rows = {}
    for region, counts in packing:
        starts = [sum(counts[:m]) * P for m in range(len(counts))]
        rows.update({nb: region[:, at:at + nb * P] for nb, at in zip(counts, starts)})
    LEAD = 16
    sums = region_o[:, 0:N]
    weights = region_p[:, :].rearrange("p (i t) -> p i t", i=4)

    CUT = [0, 0, 0, 0, 0, 0, 0, 4, 4, 4, 4, 4, 4, 8, 8, 8, 8]

    SMALL = 4

    def cut(nb):
        return CUT[nb]

    def small(n):
        return block_range(n)[1] <= SMALL

    def pieces(lo, hi):
        count = -(-(hi - lo) // (SW // P))
        return [(lo + (hi - lo) * m // count, lo + (hi - lo) * (m + 1) // count) for m in range(count)]

    order = [m for i in range(NP // 2) for m in (NP - 1 - i, i)]
    pairs = [(b, i) for b in range(B) for i in order]
    tiles = [(b, i, w) for b, i in pairs for w in range(2)]
    slots = []
    for n, (b, i, w) in enumerate(tiles):
        nb = 2 * i + w + 1
        on_dve = [(n, False, lo, hi) for lo, hi in pieces(cut(nb), nb)]
        on_act = [(n, True, lo, hi) for lo, hi in pieces(0, cut(nb))]
        while on_dve or on_act:
            slots += on_dve[:1] + on_act[:1]
            on_dve, on_act = on_dve[1:], on_act[1:]
    NS = len(slots)
    NY = sum(not s[1] for s in slots)
    NX = sum(s[1] for s in slots)
    NTL = len(tiles)
    NPR = len(pairs)
    blocks = [(g, k) for g, (b, i) in enumerate(pairs) for k in range(i + 1)]
    NB = len(blocks)
    BACK_LAG = 3
    PV_LAG = 2
    NC = 4 * B
    LOADS = 7 * 16
    assert NS % SB == 0 and NB % 4 == 0
    on_dve = [[s for s in range(NS) if slots[s][0] == n and not slots[s][1]] for n in range(NTL)]
    on_act = [[s for s in range(NS) if slots[s][0] == n and slots[s][1]] for n in range(NTL)]
    x_to = [sum(slots[r][1] for r in range(s + 1)) for s in range(NS)]
    y_to = [s + 1 - x_to[s] for s in range(NS)]
    first_of = [min(s for s in range(NS) if tiles[slots[s][0]][0] == b) for b in range(B)]
    last_of = [max(s for s in range(NS) if tiles[slots[s][0]][0] == b) for b in range(B)]
    blocks_to = [sum(1 for gg, _ in blocks if gg <= g) for g in range(NPR)]
    x_tiles_to = [sum(1 for m in range(n + 1) if on_act[m]) for n in range(NTL)]
    NXT = x_tiles_to[-1]

    with ExitStack() as st, nc.Block() as block:
        sem = lambda name: st.enter_context(nc.semaphore(name))
        score_done, relu_done = sem("score_done"), sem("relu_done")
        scaled_y, scaled_x = sem("scaled_y"), sem("scaled_x")
        shifted, shifted_x, negated = sem("shifted"), sem("shifted_x"), sem("negated")
        masked, shifted_small = sem("masked"), sem("shifted_small")
        turned, exp_done, pv_done, pv_saved = sem("turned"), sem("exp_done"), sem("pv_done"), sem("pv_saved")
        back_done, summed, recip_done, cleared = sem("back_done"), sem("summed"), sem("recip_done"), sem("cleared")
        values_done = [sem("values_done0"), sem("values_done1")]
        passed, passed_pool, passed_sp = sem("passed"), sem("passed_pool"), sem("passed_sp")
        score_ps = st.enter_context(nc.psum_tensor("score_ps", [P, SB, SW], F32))
        turn_ps = st.enter_context(nc.psum_tensor("turn_ps", [P, 2, 4 * P], F32))
        pv_ps = st.enter_context(nc.psum_tensor("pv_ps", [P, 2, 2 * P], F32))
        back_ps = st.enter_context(nc.psum_tensor("back_ps", [P, 4, P], F32))
        maxima = st.enter_context(nc.sbuf_tensor("maxima", [P, 5, NTL], F32))
        csum = st.enter_context(nc.sbuf_tensor("csum", [P, B, BT, HD + 1], F32))
        crec = st.enter_context(nc.sbuf_tensor("crec", [P, B, BT], F32))

        FREE_SCALED, FREE_RELU, FREE_PV, FREE_BLOCKS, FREE_PAIRS, FREE_BACK = NY, NX, 4 + NB, 2 + NB, 2 + NPR, 1 + NC

        def block_range(n):
            nb = 2 * tiles[n][1] + tiles[n][2] + 1
            return cut(nb), nb

        width = [hi - lo for _, _, lo, hi in slots]
        due = [NB * sum(width[:s]) / sum(width) - LEAD for s in range(NS)]
        timed = [(j + 0.1, "turn", j) for j in range(NB)] + [(due[s] - 0.2, "score", s) for s in range(NS)]
        timed += [(j + PV_LAG + (1 if blocks[j][1] == 0 else 0) + 0.3 + 0.01 * (blocks[j][1] == 1), "pv", j) for j in range(NB)]
        timed += [(blocks_to[2 * c + 1] + BACK_LAG + 0.4, "back", c) for c in range(NC)]
        timed += [(BACK_LAG + 0.5, "values", 1), (BACK_LAG + 0.5 - NB // B, "values", 0)]
        timed = sorted(timed)
        START = BACK_LAG + 1
        lead_in = [(what, n, 0) for t, what, n in timed if t < START]
        program = [(what, n, later) for t, what, n, later in sorted([(t, what, n, 0) for t, what, n in timed if t >= START] +
                                                                    [(t + NB, what, n, 1) for t, what, n in timed if t < START])]
        scores_ahead = sum(what == "score" for what, _, _ in lead_in)

        def tile_steps(m):
            steps = []
            mine = [("slot", s, m // NTL) for s in on_dve[m % NTL]]
            other = [("slot", s, (m - 1) // NTL) for s in on_act[(m - 1) % NTL]] if m >= 1 else []
            while mine or other:
                steps += mine[:1] + other[:1]
                mine, other = mine[1:], other[1:]
            return steps + ([("shift", (m - 2) % NTL, (m - 2) // NTL)] if m >= 2 else [])

        ahead = slots[scores_ahead][0]
        lead_in_tiles = [step for m in range(ahead) for step in tile_steps(m)]
        tile_program = []
        returned = 0
        for m in range(ahead, ahead + NTL):
            tile_program += tile_steps(m)
            while returned < NC:
                upto = program[:program.index(("back", returned, 0))]
                before = [later * NTL + slots[s][0] for what, s, later in upto if what == "score"]
                if m < max(before) + 1 and m < ahead + NTL - 1:
                    break
                tile_program.append(("back", returned, 0))
                returned += 1
                if returned % (NC // B) == 0:
                    tile_program.append(("divide", returned * B // NC - 1, 0))

        def place_of(j, a, w):
            g, k = blocks[j]
            b, i = pairs[g]
            if i < 2 or 2 * k + a <= 2 * i:
                return (2 * a + w) * P
            return 2 * P if w else None

        def row_free(g):
            return FREE_BLOCKS + (blocks_to[g - NP] if g >= NP else blocks_to[g - NP] - NB)

        small_to = [sum(small(m) for m in range(n + 1)) for n in range(NTL)]
        NSM = small_to[-1]

        def top(n):
            place = len(on_dve[n]) + len(on_act[n]) - 1
            return maxima[:, place, n:n + 1]

        def wait_scaled(eng, n, h):
            if on_act[n]:
                eng.wait_ge(scaled_x, h * NX + x_to[on_act[n][-1]])
            else:
                eng.wait_ge(scaled_y, h * NY + (FREE_SCALED + y_to[on_dve[n][-1]]))

        def over_heads(eng, emit, first, body):
            for what, j, _ in first:
                emit(what, j, 0)
            with eng.Fori(0, H - 1) as h:
                for what, j, later in body:
                    emit(what, j, h + later)
            for what, j, later in body:
                if not later:
                    emit(what, j, H - 1)

        @block.sync
        def _(sp):
            load_head(sp, 0, 1)
            with sp.Fori(0, H - 1) as h:
                for b in range(B):
                    sp.wait_ge(scaled_y, h * NY + (FREE_SCALED + y_to[last_of[b]]))
                    sp.sem_inc(passed_sp, 1)
                    sp.wait_ge(scaled_x, h * NX + x_to[last_of[b]])
                    sp.sem_inc(passed_sp, 1)
                    load_head(sp, h + 1, b)

        @block.tensor
        def _(pe):
            pe.sem_inc(pv_done, FREE_PV)

            def emit(what, j, h):
                if what == "score":
                    n, on_act, lo, hi = slots[j]
                    b, i, w = tiles[n]
                    if j == first_of[b]:
                        pe.wait_ge(loaded[b], h * LOADS + LOADS)
                    before = (j - SB) % NS
                    if slots[before][1]:
                        pe.wait_ge(relu_done, h * NX + (FREE_RELU + x_to[before] - (0 if j >= SB else NX)))
                    else:
                        pe.wait_ge(scaled_y, h * NY + (FREE_SCALED + y_to[before] - (0 if j >= SB else NY)))
                    q0 = (2 * i + w) * P
                    nc.tensor.matmul(score_ps[:, j % SB, 0:(hi - lo) * P], stacks[:, b, 0, q0:q0 + P],
                                     stacks[:, b, 1, lo * P:hi * P], start=True, stop=True).then_inc(score_done, 1)
                elif what == "turn":
                    g, k = blocks[j]
                    b, i = pairs[g]
                    if k == 0:
                        pe.wait_ge(masked, h * NTL + (2 * g + 2))
                        if x_tiles_to[2 * g + 1] > (x_tiles_to[2 * g - 1] if g else 0):
                            pe.wait_ge(shifted_x, h * NXT + x_tiles_to[2 * g + 1])
                    pe.wait_ge(exp_done, h * NB + (FREE_BLOCKS + j - 1))
                    for a in range(2):
                        for w in range(2):
                            kb = 2 * k + a
                            if kb <= 2 * i + w:
                                dst = turn_ps[:, j % 2, place_of(j, a, w):place_of(j, a, w) + P]
                                last = nc.tensor.transpose(dst, rows[2 * i + w + 1][:, kb * P:(kb + 1) * P], ident[:, :])
                            elif place_of(j, a, w) is not None:
                                last = nc.tensor.matmul(turn_ps[:, j % 2, a * 2 * P:a * 2 * P + P], ident_b, mask_full, start=True, stop=True)
                    last.then_inc(turned, 1)
                elif what == "pv":
                    g, k = blocks[j]
                    b, i = pairs[g]
                    if k == 0:
                        pe.wait_ge(pv_saved, h * NPR + (FREE_PAIRS + g))
                        if i == NP - 1:
                            pe.wait_ge(values_done[b], h + 1)
                    pe.wait_ge(exp_done, h * NB + (FREE_BLOCKS + j + 1))
                    for a in range(2):
                        kb = 2 * k + a
                        c = 32 * (kb % 4)
                        w0 = 0 if place_of(j, a, 0) is not None else 1
                        last = nc.tensor.matmul(pv_ps[c:c + VW, g % 2, w0 * P:2 * P], vblock[:, b, kb, :],
                                                weights[:, j % 4, a * 2 * P:(a * 2 + 2 - w0) * P],
                                                start=(kb < 4), stop=(kb + 4 > 2 * i + 1))
                    last.then_inc(pv_done, 1)
                elif what == "back":
                    b, c = j // 4, j % 4
                    pe.wait_ge(pv_saved, h * NPR + (FREE_PAIRS + 2 * j + 2))
                    pe.wait_ge(summed, h * NC + (FREE_BACK + j))
                    for q in range(4):
                        qt = 4 * c + q
                        last = nc.tensor.transpose(back_ps[:, q, :], sums[:, qt * P:(qt + 1) * P], ident[:, :])
                    last.then_inc(back_done, 1)

            over_heads(pe, emit, lead_in, program)

        @block.scalar
        def _(act):
            act.sem_inc(exp_done, FREE_BLOCKS)
            act.sem_inc(pv_saved, FREE_PAIRS)
            act.sem_inc(relu_done, FREE_RELU)
            act.wait_ge(cleared, 1)

            def emit(what, j, h):
                if what == "values":
                    act.wait_ge(pv_done, h * NB + (FREE_PV - NB + NB // B * (j + 1)))
                    nc.scalar.copy(vblock[:, j, :, 0:HD], vals[:, j * BT:(j + 1) * BT, bass.ds(h * HD, HD)]).then_inc(values_done[j], 1)
                elif what == "score" and slots[j][1]:
                    n, _, lo, hi = slots[j]
                    b, i, w = tiles[n]
                    g = n // 2
                    act.wait_ge(score_done, h * NS + (j + 1))
                    act.wait_ge(exp_done, h * NB + row_free(g))
                    nc.scalar.activation(rows[2 * i + w + 1][:, lo * P:hi * P], score_ps[:, j % SB, 0:(hi - lo) * P],
                                         ACT.Relu).then_inc(relu_done, 1)
                elif what == "turn":
                    act.wait_ge(turned, h * NB + (j + 1))
                    act.wait_ge(pv_done, h * NB + (FREE_PV + j - 3))
                    used = 4 * P if place_of(j, 1, 0) is not None else 3 * P
                    nc.scalar.activation(weights[:, j % 4, 0:used], turn_ps[:, j % 2, 0:used], ACT.Exp).then_inc(exp_done, 1)
                elif what == "pv":
                    g, k = blocks[j]
                    b, i = pairs[g]
                    if k == i:
                        act.wait_ge(pv_done, h * NB + (FREE_PV + j + 1))
                        act.wait_ge(summed, h * NC + (FREE_BACK + g // 2 + 1 - NC // B))
                        used = P if i else P // 2
                        nc.scalar.copy(sums[0:used, 2 * (g % NP) * P:(2 * (g % NP) + 2) * P].rearrange("p (w t) -> p w t", w=2),
                                       pv_ps[0:used, g % 2, :].rearrange("p (w t) -> p w t", w=2)[:, :, ::-1]).then_inc(pv_saved, 1)

            over_heads(act, emit, lead_in, program)

        @block.vector
        def _(dve):
            dve.sem_inc(scaled_y, FREE_SCALED)
            dve.sem_inc(summed, FREE_BACK)
            alone = order.index(0)
            nc.vector.memset(sums[P // 2:P, 2 * alone * P:2 * (alone + 1) * P], 0.0).then_inc(cleared, 1)

            def scale(s, h):
                n, act_s, lo, hi = slots[s]
                b, i, w = tiles[n]
                g = n // 2
                if s == first_of[b]:
                    dve.wait_ge(loaded[b], h * LOADS + LOADS)
                row = rows[2 * i + w + 1][:, lo * P:hi * P]
                u0 = N - P - (2 * i + w) * P + lo * P
                earlier = on_dve[n] + on_act[n]
                place = earlier.index(s)
                start = maxima[:, place - 1, n:n + 1] if place else 0.0
                if place > len(on_dve[n]):
                    dve.wait_ge(scaled_x, h * NX + x_to[s] - 1)
                elif place:
                    dve.wait_ge(scaled_y, h * NY + (FREE_SCALED + y_to[earlier[place - 1]]))
                if act_s:
                    dve.wait_ge(relu_done, h * NX + (FREE_RELU + x_to[s]))
                    src = row
                else:
                    dve.wait_ge(exp_done, h * NB + row_free(g))
                    dve.wait_ge(score_done, h * NS + (s + 1))
                    src = score_ps[:, s % SB, 0:(hi - lo) * P]
                dve.sem_inc(passed, 1)
                nc.vector.tensor_tensor_reduce(out=row, in0=src, in1=factors[:, b, u0:u0 + (hi - lo) * P], scale=1.0,
                                               scalar=start, op0=ALU.mult, op1=ALU.max,
                                               accum_out=maxima[:, place, n:n + 1]).then_inc(scaled_x if act_s else scaled_y, 1)

            def shift(n, h):
                b, i, w = tiles[n]
                lo, hi = block_range(n)
                wait_scaled(dve, n, h)
                row = rows[hi][:, lo * P:hi * P]
                nc.vector.tensor_scalar(row, row, 0.0, top(n), ALU.max, ALU.subtract).then_inc(shifted, 1)

            def emit(what, j, h):
                if what == "slot":
                    scale(j, h)
                elif what == "shift":
                    if not small(j):
                        shift(j, h)
                elif what == "back":
                    b, c = j // 4, j % 4
                    dve.wait_ge(back_done, h * NC + (j + 1))
                    nc.vector.tensor_reduce(csum[:, b, 4 * c:4 * c + 4, :],
                                            back_ps[:, :, :].rearrange("p q (j r) -> p q r j", r=VW)[:, :, 0:HD + 1, :],
                                            AX.X, ALU.add).then_inc(summed, 1)
                else:
                    b = j
                    dve.wait_ge(summed, h * NC + (FREE_BACK + 4 * b + 4))
                    nc.vector.reciprocal(crec[:, b, :], csum[:, b, :, HD]).then_inc(recip_done, 1)
                    dve.wait_ge(recip_done, h * B + (b + 1))
                    ordered = [v.rearrange("p (m r w) d -> p r m w d", r=2, w=2)
                               for v in (csum[:, b, :, 0:HD], crec[:, b, :].unsqueeze(2).to_broadcast([P, BT, HD]))]
                    for r in range(2):
                        t0 = b * BT + (1 - r) * BT // 2
                        dst = context[:, t0:t0 + BT // 2, bass.ds(h * HD, HD)].rearrange("p (m w) d -> p m w d", w=2)
                        parts = [v[:, r] if r else v[:, r, ::-1] for v in ordered]
                        nc.vector.tensor_tensor(dst, *parts, ALU.mult)

            over_heads(dve, emit, lead_in_tiles, tile_program)

        @block.gpsimd
        def _(pool):
            def emit(what, n, h):
                if what != "shift":
                    return
                lo, hi = block_range(n)
                if lo:
                    shift_x(n, lo, hi, h)
                if small(n):
                    wait_scaled(pool, n, h)
                    pool.sem_inc(passed_pool, 1)
                    row = rows[hi][:, lo * P:hi * P]
                    nc.gpsimd.tensor_scalar(row, row, 0.0, top(n), ALU.max, ALU.subtract).then_inc(shifted_small, 1)
                    pool.wait_ge(shifted_small, h * NSM + small_to[n])
                else:
                    pool.wait_ge(shifted, h * (NTL - NSM) + (n + 1 - small_to[n]))
                pool.sem_inc(passed_pool, 1)
                block = rows[hi][:, (hi - 1) * P:hi * P]
                nc.gpsimd.affine_select(out=block, in_=block, pattern=[[-1, P]], compare_op=ALU.is_ge, fill=MASKED,
                                        base=P - 1, channel_multiplier=-1).then_inc(masked, 1)

            def shift_x(n, lo, hi, h):
                wait_scaled(pool, n, h)
                pool.sem_inc(passed_pool, 1)
                nc.gpsimd.tensor_scalar(maxima[:, 4, n:n + 1], top(n), -1.0, 0.0, ALU.mult, ALU.add).then_inc(negated, 1)
                pool.wait_ge(negated, h * NXT + x_tiles_to[n])
                pool.sem_inc(passed_pool, 1)
                row = rows[hi][:, 0:lo * P]
                nc.gpsimd.tensor_scalar(row, row, maxima[:, 4, n:n + 1], 1.0, ALU.add, ALU.mult).then_inc(shifted_x, 1)

            over_heads(pool, emit, lead_in_tiles, tile_program)


def mixture(nc, o):
    g_ = lambda *names: [o[k] for k in names]
    x, out, normed, fc1_t, fc2_t, b2 = g_("x", "out", "normed", "fc1_t", "fc2_t", "b2")
    xs, context, ident, gates, gate_sb = g_("xs", "context", "ident", "gates", "gate_sb")
    wo_gated, bo_gated, lnw_sb, lnb_sb, b1_sb = g_("wo_gated", "bo_gated", "lnw_sb", "lnb_sb", "b1_sb")
    same_expert, rows_before, tile_of, row_of = g_("same_expert", "rows_before", "tile_of", "row_of")
    region_a, region_v, region_s, region_t, region_o, region_p, region_x = g_(
        "region_a", "region_v", "region_s", "region_t", "region_o", "region_p", "region_x")

    GT = 4
    G = NT // GT
    GB = G // B
    COLS = NT * E
    LOW = 32
    HIGH = CAP // LOW
    DIGITS = 15
    TRIES = 3

    with ExitStack() as st, nc.Block() as block:
        sem = lambda name: st.enter_context(nc.semaphore(name))
        ld_x = [sem(f"ld_x2_{i}") for i in range(4)]
        xb_done, ctx_turned, ctxt_done, proj_done = sem("xb_done"), sem("ctx_turned"), sem("ctxt_done"), sem("proj_done")
        x2_done, rstd1_done, z_done, h2_done, rstd2_done = sem("x2_done"), sem("rstd1_done"), sem("z_done"), sem("h2_done"), sem("rstd2_done")
        h2_turned, h2t_done, gate_mm, gate_saved, gate_back, logits_done = (
            sem("h2_turned"), sem("h2t_done"), sem("gate_mm"), sem("gate_saved"), sem("gate_back"), sem("logits_done"))
        gbh_done, base_done, normed_done = sem("gbh_done"), sem("base_done"), sem("normed_done")
        st_out, st_normed, st_scores = sem("st_out"), sem("st_normed"), sem("st_scores")
        dve_step, cleared = sem("dve_step2"), sem("cleared2")
        centred, exped, scores_done, scores_turned = sem("centred"), sem("exped"), sem("scores_done"), sem("scores_turned")
        counted, totalled, places_done, places_turned = sem("counted"), sem("totalled"), sem("places_done"), sem("places_turned")
        onehot_done, tokens_mm, tokens_done, idx_moved = sem("onehot_done"), sem("tokens_mm"), sem("tokens_done"), sem("idx_moved")
        ld_weights, gathered = [sem("ld_weights0"), sem("ld_weights1")], [sem("gathered0"), sem("gathered1")]
        idx_copied, y_turned, yt_done = sem("idx_copied"), sem("y_turned"), sem("yt_done")
        fc1_mm, gelu_done, fc2_mm, o_done, scattered = sem("fc1_mm"), sem("gelu_done"), sem("fc2_mm"), sem("o_done"), sem("scattered")
        sum_done, kept_done, gw_step, bits_set = sem("sum_done"), sem("kept_done"), sem("gw_step"), sem("bits_set")
        var_done, sqrt_done = [sem("var1_done"), sem("var2_done")], [sem("sqrt1_done"), sem("sqrt2_done")]
        passed_pool = sem("passed_pool2")
        high_done, row_copied = sem("high_done"), sem("row_copied")

        bank = [st.enter_context(nc.psum_tensor(f"bank{i}", [P, 512], F32)) for i in range(8)]
        ctx_ps, h2_ps, gate_ps, small_ps = bank[0:2], bank[2:4], bank[6], bank[7]
        proj_ps = [bank[4 + i][:, :].rearrange("p (t d) -> p t d", d=D) for i in range(2)]
        y_ps, fc1_ps, fc2_ps = bank[0:2], bank[2:4], bank[4:6]

        ctxt = region_s[:, 0:2048].rearrange("p (i k t) -> p i k t", i=2, k=KC)
        h2t = region_s[:, 2048:4096].rearrange("p (i k t) -> p i k t", i=2, k=KC)
        h2 = region_a[:, :].rearrange("p (t d) -> p t d", d=D)
        base = region_v[:, :].rearrange("p (t d) -> p t d", d=D)
        nrm = context
        stats = region_t[:, 0:NT * 6].rearrange("p (t s) -> p t s", s=6)
        mom = region_t[:, 192:192 + 2 * NT * 2].rearrange("p (l t s) -> p l t s", l=2, s=2)
        rst = region_t[:, 320:320 + 2 * NT].rearrange("p (l t) -> p l t", l=2)
        nmr = region_t[:, 384:384 + 2 * NT].rearrange("p (l t) -> p l t", l=2)
        gate_t_sb = region_t[:, 512:512 + 2 * P].rearrange("p (i t) -> p i t", i=2)
        scores = region_t[:, 1024:1024 + COLS].rearrange("p (h t e) -> p h t e", h=2, e=E)
        row_stat = region_t[:, 1280:1280 + 2 * NT].rearrange("p (i t) -> p i t", i=2)

        def tokens(i):
            return region_p[:, i * 256:(i + 1) * 256]
        scores_t, above, equal, chosen, run, zeros, trash = (tokens(i) for i in range(7))
        found = st.enter_context(nc.sbuf_tensor("found", [P, 2 + 2 * TRIES], I32))
        threshold, digit_found = found[:, 0:1], found[:, 1:2]
        candidates, next_ones = found[:, 2:2 + TRIES], found[:, 2 + TRIES:2 + 2 * TRIES]
        bits = st.enter_context(nc.sbuf_tensor("bits", [P, DIGITS, TRIES], I32))
        count_b = st.enter_context(nc.sbuf_tensor("count_b", [P, 2 * TRIES + 4], BF16))
        count_f = st.enter_context(nc.sbuf_tensor("count_f", [P, 4], F32))
        high = region_t[:, 1536:1536 + COLS // 2].bitcast(BF16)
        low = region_t[:, 1664:1664 + COLS // 2].bitcast(BF16)
        place_i = region_p[:, 0:3 * COLS].bitcast(I32).rearrange("p (i c) -> p i c", i=3)
        high_hot = region_t[:, 2048:4096].bitcast(BF16).rearrange("p (r c) -> p r c", r=HIGH)
        low_hot = region_o[:, :].bitcast(BF16).rearrange("p (r c) -> p r c", r=LOW)
        token_of = region_s[:, :].bitcast(BF16).rearrange("p (s r c) -> p s r c", r=HIGH, s=2)
        row_f = st.enter_context(nc.sbuf_tensor("row_f", [P, 1], F32))
        idx_low = st.enter_context(nc.sbuf_tensor("idx_low", [LOW, E, HIGH], U32))
        idx_f = region_t[0:LOW, 1792:1792 + E * HIGH].rearrange("p (e r) -> p e r", e=E)
        powers = st.enter_context(nc.sbuf_tensor("powers", [P, DIGITS, TRIES], I32))
        idx_all = st.enter_context(nc.sbuf_tensor("idx_all", [P, E, EC], U32))
        idx_cur = st.enter_context(nc.sbuf_tensor("idx_cur", [P, 2, EC], U32))
        sides = st.enter_context(nc.sbuf_tensor("sides", [P, B, E, EC], F32))
        kept = st.enter_context(nc.sbuf_tensor("kept", [P, 2, B, EC], F32))
        w1_sb = [region_x[:, i * 4096:i * 4096 + 2048].rearrange("p (k f) -> p k f", k=KC) for i in range(2)]
        w2_sb = [region_x[:, i * 4096 + 2048:(i + 1) * 4096].rearrange("p (f d) -> p f d", d=D) for i in range(2)]
        hidden = region_a[:, 0:4096].rearrange("p (f t) -> p f t", f=FC)
        yt = region_a[:, 4096:6144].rearrange("p (i k t) -> p i k t", i=2, k=KC)
        o_sb = region_a[:, 6144:8192].rearrange("p (i c d) -> p i c d", i=2, c=EC)
        y_sb = region_v[:, 0:2 * EC * NW].rearrange("p (i c w) -> p i c w", i=2, c=EC)
        b2_sb = region_v[:, 4096:4096 + 2 * D].rearrange("p (i d) -> p i d", i=2)
        gw = region_v[:, 5120:5120 + EC * D].rearrange("p (c d) -> p c d", c=EC)

        ABOVE, EQUAL, CHOSEN = (2 * TRIES + m for m in range(3))

        def tries(i):
            return slice(i % 2 * TRIES, (i % 2 + 1) * TRIES)

        def over_experts(eng, emit):
            with eng.Fori(0, E // 2 - 1) as n:
                emit(2 * n, n, 0, True, True)
                emit(2 * n + 1, n, 1, True, True)
            emit(E - 2, E // 2 - 1, 0, True, False)
            emit(E - 1, E // 2 - 1, 1, False, False)

        def at(e, base=0):
            return bass.ds(e + base, 1) if not isinstance(e, int) else slice(e + base, e + base + 1)

        @block.sync
        def _(sp):
            XQ = NT // 4
            for i in range(4):
                sp.dma_start(xs[:, i * XQ:(i + 1) * XQ, :],
                             x[i * XQ * P:(i + 1) * XQ * P, :].rearrange("(t p) d -> p t d", p=P)).then_inc(ld_x[i], 16)
            for g in range(G):
                t0, t1 = g * GT, (g + 1) * GT
                sp.wait_ge(base_done, g + 1)
                sp.dma_start(out[t0 * P:t1 * P, :].rearrange("(t p) d -> p t d", p=P), base[:, t0:t1, :]).then_inc(st_out, 16)
                sp.wait_ge(normed_done, g + 1)
                sp.dma_start(normed[t0 * P:t1 * P, 0:D].rearrange("(t p) d -> p t d", p=P), nrm[:, t0:t1, :]).then_inc(st_normed, 16)

            def load(e, i):
                src = fc1_t[at(e), :, :]
                sp.dma_start(w1_sb[i], src.rearrange("o (k p) f -> p (o k) f", p=P)).then_inc(ld_weights[i], 16)
                src = fc2_t[at(e), :, :]
                sp.dma_start(w2_sb[i], src.rearrange("o (f p) d -> p (o f) d", p=P)).then_inc(ld_weights[i], 16)
                src = b2[at(e), :]
                sp.dma_start(b2_sb[:, i, :], bass.AP(tensor=src.tensor, offset=src.offset, ap=[[0, P], [1, D]])).then_inc(ld_weights[i], 16)

            sp.wait_ge(st_out, 16 * G)
            for i in range(2):
                load(i, i)
            sp.wait_ge(scores_done, 1)
            for half in range(2):
                sp.dma_start(normed[:, D:NW].rearrange("(t h p) e -> h p t e", h=2, p=P)[half], scores[:, half, :, :]).then_inc(st_scores, 16)
            sp.wait_ge(tokens_done, 1)
            for j in range(P // LOW):
                sp.dma_start(idx_all[j * LOW:(j + 1) * LOW, :, :], idx_low[:, :, j * EC:(j + 1) * EC]).then_inc(idx_moved, 16)
            with sp.Fori(0, E // 2 - 1) as i:
                for j in range(2):
                    sp.wait_ge(sum_done, i * (2 * EC) + (2 + (j + 1) * EC))
                    load(2 * i + (2 + j), j)
            sp.wait_ge(scattered, 16 * EC * E)

        @block.tensor
        def _(pe):
            for s in range(G + 5):
                if s < G:
                    g = s
                    for k in range(KC):
                        if g:
                            pe.wait_ge(ctxt_done, KC * (g - 1) + k + 1)
                        for i in range(GT):
                            last = nc.tensor.transpose(ctx_ps[k][:, i * P:(i + 1) * P],
                                                       context[:, g * GT + i, k * P:(k + 1) * P], ident[:, :])
                        last.then_inc(ctx_turned, 1)
                if 0 <= s - 1 < G:
                    g = s - 1
                    pe.wait_ge(ctxt_done, KC * (g + 1))
                    if g:
                        pe.wait_ge(x2_done, g)
                    for i in range(GT):
                        for k in range(KC):
                            last = nc.tensor.matmul(proj_ps[i // 2][:, i % 2, :], ctxt[:, g % 2, k, i * P:(i + 1) * P],
                                                    wo_gated[:, g // GB, k, :], start=(k == 0), stop=(k == KC - 1))
                    last.then_inc(proj_done, 1)
                if 0 <= s - 3 < G:
                    g = s - 3
                    pe.wait_ge(h2_done, g + 1)
                    for k in range(KC):
                        if g:
                            pe.wait_ge(h2t_done, KC * (g - 1) + k + 1)
                        for i in range(GT):
                            last = nc.tensor.transpose(h2_ps[k][:, i * P:(i + 1) * P], h2[:, g * GT + i, k * P:(k + 1) * P], ident[:, :])
                        last.then_inc(h2_turned, 1)
                if 0 <= s - 4 < G:
                    g = s - 4
                    pe.wait_ge(h2t_done, KC * (g + 1))
                    if g:
                        pe.wait_ge(gate_saved, g)
                    else:
                        pe.wait_ge(cleared, 1)
                    for k in range(KC):
                        for i in range(GT):
                            last = nc.tensor.matmul(gate_ps[32 * i:32 * i + E, 0:P], gate_sb[:, k, :],
                                                    h2t[:, g % 2, k, i * P:(i + 1) * P], start=(k == 0), stop=(k == KC - 1))
                    last.then_inc(gate_mm, 1)
                if 0 <= s - 5:
                    g = s - 5
                    pe.wait_ge(gate_saved, g + 1)
                    if g:
                        pe.wait_ge(logits_done, g)
                    nc.tensor.transpose(small_ps[:, 0:P], gate_t_sb[:, g % 2, :], ident[:, :]).then_inc(gate_back, 1)
            pe.wait_ge(scores_done, 1)
            for half in range(2):
                last = nc.tensor.transpose(small_ps[:, half * P:(half + 1) * P],
                                           scores[:, half, :, :].rearrange("p t e -> p (t e)"), ident[:, :])
            last.then_inc(scores_turned, 1)
            for i in range(DIGITS + 1):
                pe.wait_ge(counted, i + 1)
                cols = tries(i) if i < DIGITS else slice(ABOVE, ABOVE + 1)
                nc.tensor.matmul(gate_ps[:, cols], same_expert, count_b[:, cols], start=True, stop=True).then_inc(totalled, 1)
            for i in range(2):
                pe.wait_ge(counted, DIGITS + 2 + i)
                col = (EQUAL, CHOSEN)[i]
                nc.tensor.matmul(gate_ps[:, col:col + 1], rows_before, count_b[:, col:col + 1], start=True, stop=True).then_inc(totalled, 1)
            pe.wait_ge(places_done, 1)
            for half in range(2):
                last = nc.tensor.transpose(small_ps[:, half * P:(half + 1) * P], chosen[:, half * P:(half + 1) * P], ident[:, :])
            last.then_inc(places_turned, 1)
            pe.wait_ge(onehot_done, 3)
            for e in range(E):
                for t in range(NT):
                    c = t * E + e
                    last = nc.tensor.matmul(bank[5][0:LOW, e * 2 * HIGH:(e + 1) * 2 * HIGH], low_hot[:, :, c],
                                            token_of[:, :, :, c], start=(t == 0), stop=(t == NT - 1))
                last.then_inc(tokens_mm, 1)

            def turn(n, i):
                pe.wait_ge(gathered[i], n * (16 * EC) + 16 * EC)
                for k in range(KC):
                    for c in range(EC):
                        last = nc.tensor.transpose(y_ps[k][:, c * P:(c + 1) * P], y_sb[:, i, c, k * P:(k + 1) * P], ident[:, :])
                    last.then_inc(y_turned, 1)

            def emit(e, n, i, ahead, gathers):
                pe.wait_ge(ld_weights[i], n * 48 + 48)
                pe.wait_ge(yt_done, e * KC + KC)
                for f in range(FC):
                    pe.wait_ge(gelu_done, e * FC + (f + 1))
                    for k in range(KC):
                        last = nc.tensor.matmul(fc1_ps[f % 2][:, :], w1_sb[i][:, k, f * P:(f + 1) * P], yt[:, i, k, :],
                                                start=(k == 0), stop=(k == KC - 1))
                    last.then_inc(fc1_mm, 1)
                if ahead:
                    turn(n + i, 1 - i)
                for c in range(EC):
                    pe.wait_ge(sum_done, e * EC + (c + 1))
                    for f in range(FC):
                        if c == 0 and f >= FC - 2:
                            pe.wait_ge(gelu_done, e * FC + (f + 3))
                        last = nc.tensor.matmul(fc2_ps[c % 2][:, 0:D], hidden[:, f, c * P:(c + 1) * P], w2_sb[i][:, f, :],
                                                start=(f == 0), stop=(f == FC - 1))
                    last.then_inc(fc2_mm, 1)

            turn(0, 0)
            over_experts(pe, emit)

        @block.scalar
        def _(act):
            act.sem_inc(gelu_done, 2)

            def deviation(lvl, g):
                act.wait_ge(var_done[lvl], g + 1)
                nc.scalar.activation(rst[:, lvl, g * GT:(g + 1) * GT], rst[:, lvl, g * GT:(g + 1) * GT], ACT.Sqrt).then_inc(sqrt_done[lvl], 1)

            for s in range(G + 5):
                if s < G:
                    g = s
                    for k in range(KC):
                        act.wait_ge(ctx_turned, KC * g + k + 1)
                        if g >= 2:
                            act.wait_ge(proj_done, g - 1)
                        nc.scalar.copy(ctxt[:, g % 2, k, :], ctx_ps[k][:, :]).then_inc(ctxt_done, 1)
                if 0 <= s - 2 < G:
                    deviation(0, s - 2)
                if 0 <= s - 3 < G:
                    deviation(1, s - 3)
                    g = s - 3
                    for k in range(KC):
                        act.wait_ge(h2_turned, KC * g + k + 1)
                        if g >= 2:
                            act.wait_ge(gate_mm, g - 1)
                        nc.scalar.copy(h2t[:, g % 2, k, :], h2_ps[k][:, :]).then_inc(h2t_done, 1)
                if 0 <= s - 2 < G:
                    g = s - 2
                    act.wait_ge(rstd1_done, g + 1)
                    for t in range(g * GT, (g + 1) * GT):
                        last = nc.scalar.activation(h2[:, t, :], xs[:, t, :], ACT.Identity, bias=nmr[:, 0, t:t + 1], scale=rst[:, 0, t:t + 1])
                    last.then_inc(z_done, 1)
                if 0 <= s - 4 < G:
                    g = s - 4
                    act.wait_ge(gate_mm, g + 1)
                    if g >= 2:
                        act.wait_ge(gate_back, g - 1)
                    nc.scalar.copy(gate_t_sb[:, g % 2, :], gate_ps[:, 0:P]).then_inc(gate_saved, 1)
                if 0 <= s - 3 < G:
                    g = s - 3
                    act.wait_ge(rstd2_done, g + 1)
                    for t in range(g * GT, (g + 1) * GT):
                        last = nc.scalar.activation(nrm[:, t, :], h2[:, t, :], ACT.Identity, bias=nmr[:, 1, t:t + 1], scale=rst[:, 1, t:t + 1])
                    last.then_inc(normed_done, 1)
            act.wait_ge(centred, 1)
            nc.scalar.activation(scores[:, :, :, :], scores[:, :, :, :], ACT.Exp).then_inc(exped, 1)
            nc.scalar.copy(row_f[:, :], row_of).then_inc(row_copied, 1)
            act.wait_ge(row_copied, 1)
            act.wait_ge(high_done, 1)
            nc.scalar.activation(token_of[:, 1, :, :], high_hot, ACT.Identity, scale=row_f[:, :]).then_inc(onehot_done, 1)

            def emit(e, n, i, ahead, gathers):
                for f in range(FC):
                    act.wait_ge(fc1_mm, e * FC + (f + 1))
                    nc.scalar.activation(hidden[:, f, :], fc1_ps[f % 2][:, :], ACT.Gelu_apprx_tanh,
                                         bias=b1_sb[:, at(e), f].rearrange("p o -> p o")).then_inc(gelu_done, 1)

            over_experts(act, emit)

        @block.vector
        def _(dve):
            dve.sem_inc(sum_done, 2)
            steps = [0]

            def step(ins):
                steps[0] += 1
                ins.then_inc(dve_step, 1)
                dve.wait_ge(dve_step, steps[0])

            nc.vector.memset(gate_ps[:, :], 0.0).then_inc(cleared, 1)
            dve.wait_ge(bits_set, 2)
            nc.vector.tensor_tensor(bits[:, :, :], bits[:, :, :], powers[:, :, :], ALU.logical_shift_left)

            def norm(lvl, g, src):
                t0, t1 = g * GT, (g + 1) * GT
                for t in range(t0, t1):
                    last = nc.vector.bn_stats(stats[:, t, :], src[:, t, :])
                step(last)
                for t in range(t0, t1):
                    last = nc.vector.bn_aggr(mom[:, lvl, t, :], stats[:, t, :])
                step(last)
                nc.vector.tensor_scalar_add(rst[:, lvl, t0:t1], mom[:, lvl, t0:t1, 1], EPS).then_inc(var_done[lvl], 1)

            def rest_of_norm(lvl, g, done):
                t0, t1 = g * GT, (g + 1) * GT
                dve.wait_ge(sqrt_done[lvl], g + 1)
                step(nc.vector.reciprocal(rst[:, lvl, t0:t1], rst[:, lvl, t0:t1]))
                nc.vector.scalar_tensor_tensor(nmr[:, lvl, t0:t1], mom[:, lvl, t0:t1, 0], -1.0, rst[:, lvl, t0:t1], ALU.mult, ALU.mult).then_inc(done, 1)

            for s in range(G + 5):
                if 0 <= s - 2 < G:
                    rest_of_norm(0, s - 2, rstd1_done)
                if 0 <= s - 3 < G:
                    rest_of_norm(1, s - 3, rstd2_done)
                if 0 <= s - 1 < G:
                    g = s - 1
                    t0, t1 = g * GT, (g + 1) * GT
                    dve.wait_ge(proj_done, g + 1)
                    dve.wait_ge(xb_done, g + 1)
                    nc.vector.tensor_tensor(xs[:, t0:t0 + 2, :], xs[:, t0:t0 + 2, :], proj_ps[0], ALU.add)
                    nc.vector.tensor_tensor(xs[:, t0 + 2:t1, :], xs[:, t0 + 2:t1, :], proj_ps[1], ALU.add).then_inc(x2_done, 1)
                    dve.wait_ge(x2_done, g + 1)
                    norm(0, g, xs)
                if 0 <= s - 2 < G:
                    g = s - 2
                    b, t0, t1 = g // GB, g * GT, (g + 1) * GT
                    dve.wait_ge(z_done, g + 1)
                    step(nc.vector.tensor_tensor(h2[:, t0:t1, :], h2[:, t0:t1, :], gates[:, b, 1, :].unsqueeze(1).to_broadcast([P, GT, D]), ALU.mult))
                    nc.vector.tensor_tensor(h2[:, t0:t1, :], h2[:, t0:t1, :], gates[:, b, 0, :].unsqueeze(1).to_broadcast([P, GT, D]), ALU.add).then_inc(h2_done, 1)
                    dve.wait_ge(h2_done, g + 1)
                    norm(1, g, h2)
                if 0 <= s - 5:
                    g = s - 5
                    dve.wait_ge(gate_back, g + 1)
                    nc.vector.tensor_copy(scores[:, :, 2 * g:2 * g + 2, :].rearrange("p h t e -> p t h e"),
                                          small_ps[:, 0:P].rearrange("p (t h r) -> p t h r", t=2, h=2)[:, :, :, 0:E]).then_inc(logits_done, 1)
            dve.wait_ge(logits_done, G)
            every = scores[:, :, :, :].rearrange("p h t e -> p (h t) e")
            step(nc.vector.tensor_reduce(row_stat[:, 0, :], every, AX.X, ALU.max))
            nc.vector.tensor_tensor(every, every, row_stat[:, 0, :].unsqueeze(2).to_broadcast([P, NT, E]), ALU.subtract).then_inc(centred, 1)
            nc.vector.memset(threshold, 0)
            nc.vector.memset(zeros, 0.0)
            dve.wait_ge(exped, 1)
            step(nc.vector.tensor_reduce(row_stat[:, 0, :], every, AX.X, ALU.add))
            step(nc.vector.reciprocal(row_stat[:, 1, :], row_stat[:, 0, :]))
            nc.vector.tensor_tensor(every, every, row_stat[:, 1, :].unsqueeze(2).to_broadcast([P, NT, E]), ALU.mult).then_inc(scores_done, 1)
            step(nc.vector.tensor_copy(candidates, bits[:, DIGITS - 1, :]))
            dve.wait_ge(scores_turned, 1)
            step(nc.vector.tensor_copy(scores_t, small_ps[:, 0:2 * P]))
            for i in range(DIGITS):
                digit = DIGITS - 1 - i
                for c in range(TRIES):
                    at_c = tries(i).start + c
                    last = nc.vector.tensor_scalar((above, equal, run)[c], scores_t, candidates[:, c:c + 1].bitcast(F32), None, ALU.is_ge, ALU.add,
                                                   accum_out=count_b[:, at_c:at_c + 1])
                last.then_inc(counted, 1)
                if i:
                    step(nc.vector.tensor_tensor(threshold, threshold, digit_found, ALU.bitwise_or))
                if digit:
                    nc.vector.tensor_tensor(next_ones, bits[:, digit - 1, :], threshold.to_broadcast([P, TRIES]), ALU.bitwise_or)
                dve.wait_ge(totalled, i + 1)
                step(nc.vector.tensor_scalar(count_f[:, 0:TRIES], gate_ps[:, tries(i)], float(CAP), None, ALU.is_ge, ALU.add,
                                             accum_out=count_f[:, TRIES:TRIES + 1]))
                step(nc.vector.tensor_scalar(digit_found, count_f[:, TRIES:TRIES + 1], float(1 << 2 * digit), None, ALU.mult))
                if digit:
                    step(nc.vector.tensor_tensor(candidates, next_ones, digit_found.to_broadcast([P, TRIES]), ALU.bitwise_or))
            step(nc.vector.tensor_tensor(threshold, threshold, digit_found, ALU.bitwise_or))
            threshold_f = threshold.bitcast(F32)
            nc.vector.tensor_scalar(above, scores_t, threshold_f, None, ALU.is_gt, ALU.add, accum_out=count_b[:, ABOVE:ABOVE + 1]).then_inc(counted, 1)
            nc.vector.tensor_scalar(equal, scores_t, threshold_f, None, ALU.is_equal, ALU.add, accum_out=count_b[:, EQUAL:EQUAL + 1]).then_inc(counted, 1)
            dve.wait_ge(counted, DIGITS + 2)
            step(nc.vector.tensor_tensor_scan(run, equal, zeros, 0.0, ALU.add, ALU.add))
            dve.wait_ge(totalled, DIGITS + 2)
            step(nc.vector.tensor_scalar(count_f[:, 0:1], gate_ps[:, ABOVE:ABOVE + 1], -1.0, float(CAP), ALU.mult, ALU.add))
            step(nc.vector.tensor_tensor(count_f[:, 0:1], count_f[:, 0:1], gate_ps[:, EQUAL:EQUAL + 1], ALU.subtract))
            step(nc.vector.scalar_tensor_tensor(equal, run, count_f[:, 0:1], equal, ALU.is_le, ALU.mult))
            step(nc.vector.tensor_tensor(above, above, equal, ALU.add))
            nc.vector.tensor_scalar(trash, above, 1.0, None, ALU.mult, ALU.add, accum_out=count_b[:, CHOSEN:CHOSEN + 1]).then_inc(counted, 1)
            step(nc.vector.tensor_tensor_scan(run, above, zeros, 0.0, ALU.add, ALU.add))
            dve.wait_ge(totalled, DIGITS + 3)
            step(nc.vector.tensor_copy(count_f[:, 1:2], gate_ps[:, CHOSEN:CHOSEN + 1]))
            nc.vector.scalar_tensor_tensor(chosen, run, count_f[:, 1:2], above, ALU.add, ALU.mult).then_inc(places_done, 1)
            dve.wait_ge(places_turned, 1)
            step(nc.vector.tensor_scalar(place_i[:, 0, :], small_ps[:, 0:2 * P], float(LOW - 1), None, ALU.add))
            nc.vector.tensor_scalar(place_i[:, 1, :], place_i[:, 0, :], LOW.bit_length() - 1, None, ALU.arith_shift_right)
            step(nc.vector.tensor_scalar(place_i[:, 2, :], place_i[:, 0, :], LOW - 1, None, ALU.bitwise_and))
            nc.vector.tensor_copy(high, place_i[:, 1, :])
            step(nc.vector.tensor_scalar_add(low, place_i[:, 2, :], 1.0))
            for r in range(HIGH):
                last = nc.vector.tensor_scalar(high_hot[:, r, :], high, float(r + 1), None, ALU.is_equal)
            last.then_inc(high_done, 1)
            dve.wait_ge(high_done, 1)
            nc.vector.tensor_tensor(token_of[:, 0, :, :], high_hot, tile_of.unsqueeze(1).to_broadcast([P, HIGH, COLS]),
                                    ALU.mult).then_inc(onehot_done, 1)
            for r in range(LOW):
                last = nc.vector.tensor_scalar(low_hot[:, r, :], low, float(r + 1), None, ALU.is_equal)
            last.then_inc(onehot_done, 1)
            dve.wait_ge(tokens_mm, E)
            found_ps = bank[5][0:LOW, 0:E * 2 * HIGH].rearrange("p (e s r) -> p e s r", e=E, s=2)
            step(nc.vector.tensor_scalar(idx_f, found_ps[:, :, 0, :], float(P), None, ALU.mult))
            nc.vector.tensor_tensor(idx_low[:, :, :], idx_f, found_ps[:, :, 1, :], ALU.add).then_inc(tokens_done, 1)
            dve.wait_ge(idx_moved, 16 * (P // LOW))
            nc.vector.tensor_scalar(sides[:, 0, :, :], idx_all[:, :, :], float(N), None, ALU.is_lt)
            step(nc.vector.tensor_scalar(sides[:, 1, :, :], idx_all[:, :, :], float(N), None, ALU.is_ge))

            def normed_in(e, i):
                for k in range(KC):
                    dve.wait_ge(y_turned, e * KC + (k + 1))
                    nc.vector.tensor_scalar(yt[:, i, k, :], y_ps[k][:, :], lnw_sb[:, k:k + 1], lnb_sb[:, k:k + 1],
                                            ALU.mult, ALU.add).then_inc(yt_done, 1)

            def emit(e, n, i, ahead, gathers):
                dve.wait_ge(gathered[i], n * (16 * EC) + 16 * EC)
                for b in range(B):
                    last = nc.vector.tensor_tensor(kept[:, i, b, :], y_sb[:, i, :, at(e, D)].rearrange("p c o -> p (c o)"),
                                                   sides[:, b, at(e), :].rearrange("p o c -> p (o c)"), ALU.mult)
                last.then_inc(kept_done, 1)
                dve.wait_ge(kept_done, e + 1)
                for c in range(EC):
                    last = nc.vector.tensor_scalar(gw[:, c, :], gates[:, 0, 2, :], kept[:, i, 0, c:c + 1], None, ALU.mult)
                last.then_inc(gw_step, 1)
                dve.wait_ge(gw_step, e * 2 + 1)
                for c in range(EC):
                    last = nc.vector.scalar_tensor_tensor(gw[:, c, :], gates[:, 1, 2, :], kept[:, i, 1, c:c + 1], gw[:, c, :], ALU.mult, ALU.add)
                last.then_inc(gw_step, 1)
                if ahead:
                    normed_in(e + 1, 1 - i)
                for c in range(EC):
                    dve.wait_ge(fc2_mm, e * EC + (c + 1))
                    if c == 0:
                        dve.wait_ge(ld_weights[i], n * 48 + 48)
                    nc.vector.tensor_tensor(o_sb[:, i, c, :], fc2_ps[c % 2][:, 0:D], b2_sb[:, i, :], ALU.add).then_inc(sum_done, 1)
                    dve.wait_ge(sum_done, e * EC + (c + 3))
                    if c == 0:
                        dve.wait_ge(gw_step, e * 2 + 2)
                    nc.vector.tensor_tensor(o_sb[:, i, c, :], o_sb[:, i, c, :], gw[:, c, :], ALU.mult).then_inc(o_done, 1)

            normed_in(0, 0)
            over_experts(dve, emit)

        @block.gpsimd
        def _(pool):
            nc.gpsimd.iota(bits[:, :, :], [[0, DIGITS], [1, TRIES]], base=1, channel_multiplier=0).then_inc(bits_set, 1)
            nc.gpsimd.iota(powers[:, :, :], [[2, DIGITS], [0, TRIES]], base=0, channel_multiplier=0).then_inc(bits_set, 1)
            for s in range(G + 3):
                if s < G:
                    g = s
                    t0, t1 = g * GT, (g + 1) * GT
                    if g % 2 == 0:
                        pool.wait_ge(ld_x[g // 2], 16)
                    nc.gpsimd.tensor_tensor(xs[:, t0:t1, :], xs[:, t0:t1, :], bo_gated[:, g // GB, :].unsqueeze(1).to_broadcast([P, GT, D]),
                                            ALU.add).then_inc(xb_done, 1)
                if s >= 3:
                    g = s - 3
                    t0, t1 = g * GT, (g + 1) * GT
                    pool.wait_ge(h2_done, g + 1)
                    nc.gpsimd.tensor_tensor(base[:, t0:t1, :], h2[:, t0:t1, :], gates[:, g // GB, 2, :].unsqueeze(1).to_broadcast([P, GT, D]),
                                            ALU.mult).then_inc(gbh_done, 1)
                    pool.wait_ge(gbh_done, g + 1)
                    nc.gpsimd.tensor_tensor(base[:, t0:t1, :], base[:, t0:t1, :], xs[:, t0:t1, :], ALU.add).then_inc(base_done, 1)

            def gather(e, i):
                nc.gpsimd.tensor_copy(idx_cur[:, i, :], idx_all[:, at(e), :].rearrange("p o c -> p (o c)")).then_inc(idx_copied, 1)
                pool.wait_ge(idx_copied, e + 1)
                pool.sem_inc(passed_pool, 1)
                for c in range(EC):
                    nc.gpsimd.indirect_dma_start(y_sb[:, i, c, :], None, normed,
                                                 bass.IndirectOffsetOnAxis(ap=idx_cur[:, i, c:c + 1], axis=0)).then_inc(gathered[i], 16)

            def emit(e, n, i, ahead, gathers):
                for c in range(EC):
                    pool.wait_ge(o_done, e * EC + (c + 1))
                    pool.sem_inc(passed_pool, 1)
                    nc.gpsimd.indirect_dma_start(out, bass.IndirectOffsetOnAxis(ap=idx_cur[:, i, c:c + 1], axis=0),
                                                 o_sb[:, i, c, :], None, compute_op=ALU.add).then_inc(scattered, 16)
                pool.wait_ge(scattered, e * (16 * EC) + 16 * EC)
                pool.sem_inc(passed_pool, 1)
                if gathers:
                    gather(e + 2, i)

            pool.wait_ge(idx_moved, 16 * (P // LOW))
            pool.wait_ge(st_normed, 16 * G)
            pool.wait_ge(st_scores, 32)
            pool.wait_ge(st_out, 16 * G)
            gather(0, 0)
            gather(1, 1)
            over_experts(pool, emit)


def kernel(L0_attn_x, L0_attn_Wq, L0_attn_Wk, L0_attn_Wv, L0_attn_Wo, L0_attn_bo, L0_attn_w, L0_attn_v,
           L0_ffn_gate_w, L0_ffn_ln_w, L0_ffn_ln_b, L0_ffn_fc1s, L0_ffn_b1s, L0_ffn_fc2s, L0_ffn_b2s, L0_c, L0_wmod):
    import concourse.bacc as bacc
    import numpy as np
    from concourse.bass_utils import run_bass_kernel_spmd

    def a(v):
        return np.asarray(v)

    p = np.arange(P)
    consts = np.zeros((P, C_W), np.float32)
    consts[:, C_ID:C_ID + P] = np.eye(P)
    consts[:, C_FULL:C_FULL + P] = MASKED
    consts[:, C_SAME:C_SAME + P] = p[:, None] % E == p[None, :] % E
    consts[:, C_BELOW:C_BELOW + P] = (p[:, None] % E == p[None, :] % E) & (p[:, None] // E < p[None, :] // E)
    col = np.arange(NT * E)
    consts[:, C_TILE:C_TILE + NT * E] = (2 * (col // E % (NT // 2)) + col // (NT * E // 2))[None, :]
    consts[:, C_ROW:C_ROW + 1] = p[:, None]
    arrays = {
        "x": a(L0_attn_x).reshape(TOK, D),
        "c_t": a(L0_c).T,
        "wmod": a(L0_wmod),
        "wq": a(L0_attn_Wq), "wk": a(L0_attn_Wk), "wv": a(L0_attn_Wv), "wo": a(L0_attn_Wo),
        "bo": a(L0_attn_bo).reshape(1, D),
        "dist_w": a(L0_attn_w).reshape(H, 1), "dist_v": a(L0_attn_v).reshape(H, 1),
        "gate_t": a(L0_ffn_gate_w).T,
        "ln_w": a(L0_ffn_ln_w).reshape(KC, P).T, "ln_b": a(L0_ffn_ln_b).reshape(KC, P).T,
        "fc1_t": a(L0_ffn_fc1s).transpose(0, 2, 1),
        "b1": a(L0_ffn_b1s).reshape(E, FC, P).transpose(2, 0, 1).reshape(P, E * FC),
        "fc2_t": a(L0_ffn_fc2s).transpose(0, 2, 1),
        "b2": a(L0_ffn_b2s),
        "consts": consts,
    }
    nc = bacc.Bacc("TRN2", target_bir_lowering=False, num_devices=1)
    arrays = {f"in_{k}": np.ascontiguousarray(v) for k, v in arrays.items()}
    args = [nc.dram_tensor(k, v.shape, mybir.dt.from_np(v.dtype), kind="ExternalInput").ap() for k, v in arrays.items()]
    result = nc.dram_tensor("result", (TOK, D), F32, kind="ExternalOutput").ap()
    adaln_block(nc, *args, result)
    r = run_bass_kernel_spmd(nc, [arrays], core_ids=[0])
    return r.results[0]["result"].reshape(B, N, D)
```
